# Optimizing a Trainium2 kernel written in Bass

```python
import numpy as np
import jax
import jax.numpy as jnp

def _softmax(x, axis=-1):
    return jax.nn.softmax(x, axis=axis)

def _gelu(x):
    return jax.nn.gelu(x, approximate=True)

def _silu(x):
    return jax.nn.silu(x)

def _sigmoid(x):
    return jax.nn.sigmoid(x)

def _layernorm(x, axis=-1, eps=1e-05):
    m = jnp.mean(x, axis=axis, keepdims=True)
    v = jnp.var(x, axis=axis, keepdims=True)
    return (x - m) / jnp.sqrt(v + eps)

def _scatter_add(tgt, idx, src, axis=0):
    return tgt.at[idx].add(src)

def _segment_sum(src, seg, n):
    return jax.ops.segment_sum(src, seg, n)
kernel_name = 'mk_adaln_d2_jaxref_r8_a4f2d6'

def setup_inputs(seed: int=0):
    np.random.seed(seed)
    _w = jnp.asarray

    def _L0_attn_setup():
        import jax, jax.numpy as jnp
        import numpy as np
        D_MODEL = 128
        HEADS = 16
        SCALE = float(np.sqrt(D_MODEL / HEADS))
        key = jax.random.key(seed)
        ks = jax.random.split(key, 5)
        B, S, D = (4, 256, D_MODEL)
        q = jax.random.normal(ks[0], (B, S, D), dtype=jnp.float32)
        init = 0.02
        wq = jax.random.normal(ks[1], (D, D), dtype=jnp.float32) * init
        wk = jax.random.normal(ks[2], (D, D), dtype=jnp.float32) * init
        wv = jax.random.normal(ks[3], (D, D), dtype=jnp.float32) * init
        wo = jax.random.normal(ks[4], (D, D), dtype=jnp.float32) * init
        return {'q': q, 'wq': wq, 'wk': wk, 'wv': wv, 'wo': wo}
    _L0_attn_in = _L0_attn_setup()

    def _L0_ffn_setup():
        import jax, jax.numpy as jnp
        import numpy as np
        from jax import lax
        LOKAL_GRUP = 7
        TOP_K = 2
        EPS = 1e-08
        CACHE_BONUS = 0.1

        def _route(tokens, uzman_embeddings, onbellek_durumu):
            sim = tokens @ uzman_embeddings.T
            _, local_idx = lax.top_k(sim, LOKAL_GRUP)
            t_norm = tokens / (jnp.linalg.norm(tokens, axis=-1, keepdims=True) + EPS)
            e_norm = uzman_embeddings / (jnp.linalg.norm(uzman_embeddings, axis=-1, keepdims=True) + EPS)
            local_embs = e_norm[local_idx]
            scores = jnp.einsum('nld,nd->nl', local_embs, t_norm)
            scores = scores + CACHE_BONUS * onbellek_durumu[local_idx]
            top_scores, top_local = lax.top_k(scores, TOP_K)
            global_idx = jnp.take_along_axis(local_idx, top_local, axis=1)
            weights = jax.nn.softmax(top_scores, axis=-1)
            return (global_idx, lax.stop_gradient(weights))
        key = jax.random.key(seed)
        ks = jax.random.split(key, 6)
        B, S, D, E, H = (2, 256, 128, 8, 512)
        return {'x': jax.random.normal(ks[0], (B, S, D), jnp.float32), 'uzman_embeddings': jax.random.normal(ks[1], (E, D), jnp.float32) * 0.01, 'W1': jax.random.normal(ks[2], (E, D, H), jnp.float32) * 0.02, 'b1': jax.random.normal(ks[3], (E, H), jnp.float32) * 0.02, 'W2': jax.random.normal(ks[4], (E, H, D), jnp.float32) * 0.02, 'b2': jax.random.normal(ks[5], (E, D), jnp.float32) * 0.02, 'onbellek_durumu': jnp.ones((E,), jnp.float32)}
    _L0_ffn_in = _L0_ffn_setup()
    _L0_c = _w((lambda *s: np.random.randn(*s).astype(np.float32) * 0.05)(8, 128))
    _L0_wmod = _w((lambda *s: np.random.randn(*s).astype(np.float32) * 0.05)(128, 6 * 128) * 128 ** (-0.5))

    def _L1_attn_setup():
        import jax, jax.numpy as jnp
        import numpy as np
        DIM = 128
        key = jax.random.key(seed)
        kx, kw = jax.random.split(key)
        x = jax.random.normal(kx, (4, 256, DIM), dtype=jnp.float32)
        W_qkv = jax.random.normal(kw, (3 * DIM, DIM), dtype=jnp.float32) * DIM ** (-0.5)
        return {'x': x, 'W_qkv': W_qkv}
    _L1_attn_in = _L1_attn_setup()

    def _L1_ffn_setup():
        import jax, jax.numpy as jnp
        import numpy as np
        E, D, H = (8, 128, 512)
        B, S = (4, 512)
        TEMPERATURE = 1.0
        key = jax.random.key(seed)
        ks = jax.random.split(key, 7)
        sc = 0.02
        return {'x': jax.random.normal(ks[0], (B, S, D), dtype=jnp.float32), 'W1': jax.random.normal(ks[1], (E, D, H), dtype=jnp.float32) * sc, 'b1': jax.random.normal(ks[2], (E, H), dtype=jnp.float32) * sc, 'W2': jax.random.normal(ks[3], (E, H, D), dtype=jnp.float32) * sc, 'b2': jax.random.normal(ks[4], (E, D), dtype=jnp.float32) * sc, 'Wr': jax.random.normal(ks[5], (D, E), dtype=jnp.float32) * sc, 'br': jax.random.normal(ks[6], (E,), dtype=jnp.float32) * sc}
    _L1_ffn_in = _L1_ffn_setup()
    _L1_c = _w((lambda *s: np.random.randn(*s).astype(np.float32) * 0.05)(8, 128))
    _L1_wmod = _w((lambda *s: np.random.randn(*s).astype(np.float32) * 0.05)(128, 6 * 128) * 128 ** (-0.5))
    _d = {'L0_attn_q': _L0_attn_in['q'], 'L0_attn_wq': _L0_attn_in['wq'], 'L0_attn_wk': _L0_attn_in['wk'], 'L0_attn_wv': _L0_attn_in['wv'], 'L0_attn_wo': _L0_attn_in['wo'], 'L0_ffn_uzman_embeddings': _L0_ffn_in['uzman_embeddings'], 'L0_ffn_W1': _L0_ffn_in['W1'], 'L0_ffn_b1': _L0_ffn_in['b1'], 'L0_ffn_W2': _L0_ffn_in['W2'], 'L0_ffn_b2': _L0_ffn_in['b2'], 'L0_ffn_onbellek_durumu': _L0_ffn_in['onbellek_durumu'], 'L0_c': _L0_c, 'L0_wmod': _L0_wmod, 'L1_attn_W_qkv': _L1_attn_in['W_qkv'], 'L1_ffn_W1': _L1_ffn_in['W1'], 'L1_ffn_b1': _L1_ffn_in['b1'], 'L1_ffn_W2': _L1_ffn_in['W2'], 'L1_ffn_b2': _L1_ffn_in['b2'], 'L1_ffn_Wr': _L1_ffn_in['Wr'], 'L1_ffn_br': _L1_ffn_in['br'], 'L1_c': _L1_c, 'L1_wmod': _L1_wmod}
    _x0 = _d['L0_attn_q']
    _d['L0_attn_q'] = jax.random.normal(jax.random.fold_in(jax.random.key(seed), 1), (8, 512, 128), dtype=_x0.dtype)
    del _x0
    return _d

def reference(L0_attn_q, L0_attn_wq, L0_attn_wk, L0_attn_wv, L0_attn_wo, L0_ffn_uzman_embeddings, L0_ffn_W1, L0_ffn_b1, L0_ffn_W2, L0_ffn_b2, L0_ffn_onbellek_durumu, L0_c, L0_wmod, L1_attn_W_qkv, L1_ffn_W1, L1_ffn_b1, L1_ffn_W2, L1_ffn_b2, L1_ffn_Wr, L1_ffn_br, L1_c, L1_wmod):

    def _L0_attn_ref(q, wq, wk, wv, wo):
        import jax, jax.numpy as jnp
        import numpy as np
        D_MODEL = 128
        HEADS = 16
        SCALE = float(np.sqrt(D_MODEL / HEADS))
        B, S, D = q.shape
        Q = jnp.einsum('bsd,ed->bse', q, wq)
        K = jnp.einsum('bsd,ed->bse', q, wk)
        V = jnp.einsum('bsd,ed->bse', q, wv)
        scores = jnp.einsum('bqe,bke->bqk', Q, K) / SCALE
        attn = jax.nn.softmax(scores, axis=-1)
        out = jnp.einsum('bqk,bke->bqe', attn, V)
        out = jnp.transpose(out, (0, 2, 1)).reshape(B, S, D)
        return jnp.einsum('bsd,ed->bse', out, wo)

    def _L0_ffn_ref(x, uzman_embeddings, W1, b1, W2, b2, onbellek_durumu):
        import jax, jax.numpy as jnp
        import numpy as np
        from jax import lax
        LOKAL_GRUP = 7
        TOP_K = 2
        EPS = 1e-08
        CACHE_BONUS = 0.1

        def _route(tokens, uzman_embeddings, onbellek_durumu):
            sim = tokens @ uzman_embeddings.T
            _, local_idx = lax.top_k(sim, LOKAL_GRUP)
            t_norm = tokens / (jnp.linalg.norm(tokens, axis=-1, keepdims=True) + EPS)
            e_norm = uzman_embeddings / (jnp.linalg.norm(uzman_embeddings, axis=-1, keepdims=True) + EPS)
            local_embs = e_norm[local_idx]
            scores = jnp.einsum('nld,nd->nl', local_embs, t_norm)
            scores = scores + CACHE_BONUS * onbellek_durumu[local_idx]
            top_scores, top_local = lax.top_k(scores, TOP_K)
            global_idx = jnp.take_along_axis(local_idx, top_local, axis=1)
            weights = jax.nn.softmax(top_scores, axis=-1)
            return (global_idx, lax.stop_gradient(weights))
        B, S, D = x.shape
        tokens = x.reshape(-1, D)
        global_idx, weights = _route(tokens, uzman_embeddings, onbellek_durumu)
        h = jnp.einsum('nd,edh->enh', tokens, W1) + b1[:, None, :]
        h = jax.nn.gelu(h, approximate=False)
        out_all = jnp.einsum('enh,ehd->end', h, W2) + b2[:, None, :]
        N = tokens.shape[0]
        out_sel = out_all[global_idx, jnp.arange(N)[:, None]]
        out = jnp.sum(weights[..., None] * out_sel, axis=1)
        return out.reshape(B, S, D)

    def _L1_attn_ref(x, W_qkv):
        import jax, jax.numpy as jnp
        import numpy as np
        DIM = 128
        qkv = jnp.einsum('bnd,ed->bne', x, W_qkv)
        B, N, _ = qkv.shape
        qkv = qkv.reshape(B, N, 3, DIM).transpose(2, 0, 1, 3)
        q, k, v = (qkv[0], qkv[1], qkv[2])
        scale = DIM ** (-0.5)
        attn = jnp.einsum('bnd,bmd->bnm', q * scale, k)
        attn = jax.nn.softmax(attn, axis=-1)
        out = jnp.einsum('bnm,bmd->bnd', attn, v)
        return out

    def _L1_ffn_ref(x, W1, b1, W2, b2, Wr, br):
        import jax, jax.numpy as jnp
        import numpy as np
        E, D, H = (8, 128, 512)
        B, S = (4, 512)
        TEMPERATURE = 1.0
        routing_logits = (x @ Wr + br) / TEMPERATURE
        routing_probs = jax.nn.softmax(routing_logits, axis=-1)
        indices = jnp.argmax(routing_probs, axis=-1)
        out = jnp.zeros_like(x)
        num_experts = W1.shape[0]
        for i in range(num_experts):
            mask = (indices == i).astype(x.dtype)[..., None]
            xi = x * mask
            h = jax.nn.relu(xi @ W1[i] + b1[i])
            out = out + (h @ W2[i] + b2[i])
        return out
    x = L0_attn_q
    mod = (_silu(L0_c) @ L0_wmod).reshape(L0_c.shape[0], 6, 1, -1)
    sa, ca, ga, sb, cb, gb = (mod[:, 0], mod[:, 1], mod[:, 2], mod[:, 3], mod[:, 4], mod[:, 5])
    ga = (2 * (ga >= 0) - 1) * jnp.maximum(jnp.abs(ga), 0.25)
    gb = (2 * (gb >= 0) - 1) * jnp.maximum(jnp.abs(gb), 0.25)
    h = _layernorm(x, axis=-1) * (1 + ca) + sa
    x = x + ga * _L0_attn_ref(h, L0_attn_wq, L0_attn_wk, L0_attn_wv, L0_attn_wo)
    h = _layernorm(x, axis=-1) * (1 + cb) + sb
    x = x + gb * _L0_ffn_ref(h, L0_ffn_uzman_embeddings, L0_ffn_W1, L0_ffn_b1, L0_ffn_W2, L0_ffn_b2, L0_ffn_onbellek_durumu)
    mod = (_silu(L1_c) @ L1_wmod).reshape(L1_c.shape[0], 6, 1, -1)
    sa, ca, ga, sb, cb, gb = (mod[:, 0], mod[:, 1], mod[:, 2], mod[:, 3], mod[:, 4], mod[:, 5])
    ga = (2 * (ga >= 0) - 1) * jnp.maximum(jnp.abs(ga), 0.25)
    gb = (2 * (gb >= 0) - 1) * jnp.maximum(jnp.abs(gb), 0.25)
    h = _layernorm(x, axis=-1) * (1 + ca) + sa
    x = x + ga * _L1_attn_ref(h, L1_attn_W_qkv)
    h = _layernorm(x, axis=-1) * (1 + cb) + sb
    x = x + gb * _L1_ffn_ref(h, L1_ffn_W1, L1_ffn_b1, L1_ffn_W2, L1_ffn_b2, L1_ffn_Wr, L1_ffn_br)
    return x

_drawn_inputs = setup_inputs


def setup_inputs(seed=0):
    import zlib

    import numpy as np

    out = dict(_drawn_inputs(seed))
    spreads = {'L0_ffn_onbellek_durumu': (1.0, 0.6)}
    factors = {'L0_attn_wq': 8.0,
     'L0_attn_wk': 8.0,
     'L0_attn_wv': 8.0,
     'L0_attn_wo': 8.0,
     'L0_ffn_uzman_embeddings': 6.397,
     'L0_ffn_W1': 5.97,
     'L0_ffn_b1': 8.0,
     'L0_ffn_W2': 5.9,
     'L0_ffn_b2': 8.0,
     'L0_c': 5.555,
     'L0_wmod': 5.404,
     'L1_ffn_W1': 3.796,
     'L1_ffn_b1': 8.0,
     'L1_ffn_W2': 3.089,
     'L1_ffn_b2': 3.906,
     'L1_ffn_Wr': 3.449,
     'L1_ffn_br': 8.0}
    for name, (base, spread) in spreads.items():
        noise = np.random.default_rng([zlib.crc32(name.encode()), seed]).standard_normal(out[name].shape)
        drawn = base * np.exp(spread * noise) if base else spread * noise
        out[name] = jnp.asarray(drawn.astype(out[name].dtype))
    for name, factor in factors.items():
        out[name] = (out[name] * factor).astype(out[name].dtype)
    return out
```

```python
from contextlib import ExitStack

import concourse.bass as bass
from concourse import mybir

P = 128
F32 = mybir.dt.float32
BF16 = mybir.dt.bfloat16
I32 = mybir.dt.int32
ALU = mybir.AluOpType
ACT = mybir.ActivationFunctionType
AX = mybir.AxisListType

NB = 8
S = 512
D = 128
J = S // P
E = 8
HID = 512
HC = HID // P
GB = NB // 2
GT = GB * J
TOPK = [2, 1]
NR = [2 * E, E]
TILES = [k * GT + E for k in TOPK]
BIAS = 4
LN_EPS = 1e-5
NORM_EPS = 1e-8
CACHE_BONUS = 0.1
BIG = 3.0e38
LN_STEPS = 4 + 4 + 2 + 9
MAGIC = 0x5F3759DF


def adaln_kernel(nc, L0_attn_q, L0_attn_wq, L0_attn_wk, L0_attn_wv, L0_attn_wo,
                 L0_ffn_uzman_embeddings, L0_ffn_W1, L0_ffn_b1, L0_ffn_W2, L0_ffn_b2,
                 L0_ffn_onbellek_durumu, L0_c, L0_wmod, L1_attn_W_qkv, L1_ffn_W1, L1_ffn_b1,
                 L1_ffn_W2, L1_ffn_b2, L1_ffn_Wr, L1_ffn_br, L1_c, L1_wmod, out):
    W1_D, W2_D = [L0_ffn_W1, L1_ffn_W1], [L0_ffn_W2, L1_ffn_W2]
    B1_D, B2_D = [L0_ffn_b1, L1_ffn_b1], [L0_ffn_b2, L1_ffn_b2]
    C_D, WMOD_D = [L0_c, L1_c], [L0_wmod, L1_wmod]
    SCALE = [(D / 16) ** -0.5, D ** -0.5]

    xs_d = [nc.dram_tensor(f"xs_scratch{g}", (TILES[0] * P, D), F32, kind="Internal").ap() for g in (0, 1)]
    ys_d = [[nc.dram_tensor(f"ys_scratch{L}{g}", (TILES[L] * P, D), F32, kind="Internal").ap() for g in (0, 1)]
            for L in (0, 1)]
    mod_d = [nc.dram_tensor(f"mod_scratch{L}", (NB, 4 * D), F32, kind="Internal").ap() for L in (0, 1)]
    b2_d = nc.dram_tensor("b2_scratch", (1, E * D), F32, kind="Internal").ap()

    ctx = ExitStack()
    with ctx:
        def sb(name, shape, dt=F32):
            return ctx.enter_context(nc.sbuf_tensor(name, shape, dt))

        def sem(name):
            return ctx.enter_context(nc.semaphore(name))

        def sem2(name):
            return [sem(f"{name}_{L}") for L in (0, 1)]

        ps_a = ctx.enter_context(nc.psum_tensor("ps_a", [P, 512], F32))
        ps_b = ctx.enter_context(nc.psum_tensor("ps_b", [P, 512], F32))
        ps_s = ctx.enter_context(nc.psum_tensor("ps_s", [P, 2, 512], F32))
        ps_p = ctx.enter_context(nc.psum_tensor("ps_p", [P, 2, 512], F32))
        ps_o = ctx.enter_context(nc.psum_tensor("ps_o", [P, 2, 512], F32))

        X = sb("X", [P, NB * J, D])
        W1 = sb("W1", [P, E, HID])
        W2 = [sb(f"W2_{L}", [P, E, HC, D]) for L in (0, 1)]
        B1 = sb("B1", [P, E, HID])
        B2 = [sb(f"B2_{L}", [P, E, D]) for L in (0, 1)]
        MB = sb("MB", [P, NB, 3, D])
        GBB = [sb(f"GBB_{L}", [P, NB, D]) for L in (0, 1)]
        H = sb("H", [P, NB * J, D])
        Hc = sb("Hc", [P, 2, J, D])
        xn = sb("xn", [P, 2, J, D])
        hT = sb("hT", [P, 2, S])
        gT = sb("gT", [P, 2, S])
        V = sb("V", [P, 2, J, D])
        prob = sb("prob", [P, 2, S])
        probT = sb("probT", [P, 2, J, P])
        hT2 = sb("hT2", [P, S])
        sq = sb("sq", [P, 2, J, D])
        xt = sb("xt", [P, 4, D])
        xT = sb("xT", [P, 2, P])
        hu = sb("hu", [P, 2, HID])
        hTm = sb("hTm", [P, 2, HC, P])
        yt = sb("yt", [P, 4, D])
        yg = sb("yg", [P, 4, 2, D])
        On = yg[:, :, 0, :]
        acc = sb("acc", [P, 2, D])
        A = [sb(f"A_{L}", [P, D]) for L in (0, 1)]
        WvT = [sb(f"WvT_{L}", [P, D]) for L in (0, 1)]
        woT = sb("woT", [P, D])
        woG = sb("woG", [P, 2, D])
        RW = [sb(f"RW_{L}", [P, NR[L]]) for L in (0, 1)]
        caT = [sb(f"caT_{L}", [P, NB]) for L in (0, 1)]
        saT = [sb(f"saT_{L}", [P, NB]) for L in (0, 1)]
        ident = sb("ident", [P, P])
        upper = sb("upper", [P, P], BF16)
        ones = sb("ones", [P, P], BF16)
        rev8 = sb("rev8", [P, E])
        up8 = sb("up8", [P, E])
        thr16 = sb("thr16", [P, GT])
        iotaT = sb("iotaT", [P, TILES[0]])
        NC = [k * GT for k in TOPK]
        keep = [sb(f"keep_{L}", [P, E * NC[L]]) for L in (0, 1)]
        onesf = sb("onesf", [P, E])
        bonus = sb("bonus", [P, E])
        brB = sb("brB", [P, E])
        st1, st2 = sb("st1", [P, J, 6]), sb("st2", [P, J, 6])
        mv1, mv2 = sb("mv1", [P, J, 2]), sb("mv2", [P, J, 2])
        nt1, nt2 = sb("nt1", [P, 3, J]), sb("nt2", [P, 3, J])
        rs1, rs2 = sb("rs1", [P, 2, J]), sb("rs2", [P, 2, J])
        nb1, nb2 = sb("nb1", [P, 2, J]), sb("nb2", [P, 2, J])
        negm = sb("negm", [P, 8])
        rowsum = sb("rowsum", [P, 8])
        rinv = sb("rinv", [P, 8])
        sims = sb("sims", [P, GT * 2, NR[0]])
        sumsq = sb("sumsq", [P, GT * 2])
        score = sb("score", [P, GT, E])
        rtmp = sb("rtmp", [P, GT, E])
        cmpt = sb("cmpt", [P, TILES[0], E])
        M = sb("M", [P, E * NC[0]])
        Mb = sb("Mb", [P, E * NC[0]], BF16)
        cum = sb("cum", [P, E * NC[0]])
        tot = sb("tot", [P, E * NC[0]])
        row = sb("row", [P, 8, GT])
        exs = sb("exs", [P, 3, E])
        slotf = sb("slotf", [P, 2 * GT])
        slot = sb("slot", [P, 2, 2 * GT], I32)
        weight = sb("weight", [P, 2, NB * J])
        eidf = sb("eidf", [P, TILES[0]])
        eid = sb("eid", [P, 2 * TILES[0]], I32)
        cur = sb("cur", [P, 4, 2], I32)
        crow = sb("crow", [NB, 4, D])
        scT = sb("scT", [P, NB])
        wsm = [hu[:, 0, 0:D], hu[:, 0, D:2 * D], hu[:, 0, 2 * D:3 * D], hu[:, 0, 3 * D:4 * D]]
        csrow = sb("csrow", [NB, 2, D])
        erow = sb("erow", [E, 2, D])
        nte = sb("nte", [E, 8])
        wmod = [MB[:, 0:2, :, :].rearrange("p a b d -> p (a b d)"),
                prob[:, :, :].rearrange("p a s -> p (a s)")[:, 0:6 * D]]
        b1row, b1T = yt[0:E * HC, 0, :], sb("b1T", [P, E * HC])
        rrow = sb("rrow", [1, 2 * D])

        in_small = sem2("in_small")
        in_x0, in_x = sem("in_x0"), sem("in_x")
        in_moe = sem2("in_moe")
        in_late = sem("in_late")
        consts = sem("consts")
        passed = sem("passed")
        s_act, s_pe, s_dve = sem("setup_act"), sem("setup_pe"), sem("setup_dve")
        rows_ready = sem("rows_ready")
        mod_out, mod_in = sem2("mod_out"), sem2("mod_in")
        b2_out, b2_in = sem("b2_out"), sem("b2_in")
        xs_zero = sem("xs_zero")
        chain = sem("dve_chain")
        pool_chain = sem("pool_chain")
        ln1_ready = sem2("ln1_ready")
        xn_ready = sem2("xn_ready")
        xn_chain = sem2("xn_chain")
        h_tr = sem2("h_tr")
        hT_ready = sem2("hT_ready")
        g_mm = sem2("g_mm")
        gT_ready = sem2("gT_ready")
        v_mm = sem2("v_mm")
        v_ready = sem2("v_ready")
        s_mm = sem2("s_mm")
        negm_ready = sem2("negm_ready")
        exp_done = sem2("exp_done")
        rinv_ready = sem2("rinv_ready")
        pt_mm = sem2("pt_mm")
        pt_ready = sem2("pt_ready")
        pv_mm = sem2("pv_mm")
        o_done = sem2("o_done")
        wog_ready = sem("wog_ready")
        y_mm = sem("y_mm")
        y_add = sem("y_add")
        hc_ready = sem2("hc_ready")
        hkeep = [[sem(f"hkeep_{L}_{u}") for u in (0, 1)] for L in (0, 1)]
        p_tr = sem2("p_tr")
        hT2_ready = sem2("hT2_ready")
        r_mm = sem2("r_mm")
        r_ready = sem2("r_ready")
        sq_ready = sem("sq_ready")
        sq_used = sem("sq_used")
        ln1_chain, ln2_chain = sem2("ln1_chain"), sem2("ln2_chain")
        hc_chain = sem2("hc_chain")
        m_ready, rank_mm, rank_read, route_done = sem("m_ready"), sem("rank_mm"), sem("rank_read"), sem("route_done")
        gap_ready, gap_exp = sem("gap_ready"), sem("gap_exp")
        scat = [[sem(f"scat_{L}_{g}") for g in (0, 1)] for L in (0, 1)]
        ld = [[sem(f"ld_{L}_{r}") for r in range(4)] for L in (0, 1)]
        st = [[sem(f"st_{L}_{r}") for r in range(4)] for L in (0, 1)]
        xt_mm = sem2("xt_mm")
        xT_ready = sem2("xT_ready")
        up_mm = sem2("up_mm")
        hu_ready = sem2("hu_ready")
        ht_mm = sem2("ht_mm")
        hTm_ready = sem2("hTm_ready")
        dn_mm = sem2("dn_mm")
        y_ready = sem2("y_ready")
        gat = [[sem(f"gat_{L}_{r}") for r in range(4)] for L in (0, 1)]
        cur_ready = sem2("cur_ready")
        comb_chain = sem2("comb_chain")
        comb_done = sem2("comb_done")
        stored = sem("stored")

        paced = {
            "pe": h_tr + g_mm + v_mm + s_mm + pt_mm + pv_mm + [y_mm] + p_tr + r_mm + xt_mm + up_mm + ht_mm + dn_mm,
            "act": hT_ready + gT_ready + [v_ready[0]] + exp_done + pt_ready + [o_done[0]] + hT2_ready + xT_ready + hTm_ready,
            "dve": ln1_ready + [v_ready[1]] + negm_ready + rinv_ready + [o_done[1], y_add, sq_used] + hc_ready + r_ready
                   + hu_ready + y_ready + comb_done,
            "pool": xn_ready + [wog_ready, sq_ready],
        }

        def upto(n):
            return min(n, NB) if isinstance(n, int) else n

        def wait_apart(eng, s, value):
            eng.wait_ge(s, value)
            if not isinstance(value, int):
                eng.sem_inc(passed, 1)

        def bias(eng, name):
            for s in paced[name]:
                eng.sem_inc(s, BIAS)

        block = ctx.enter_context(nc.Block())

        @block.sync
        def _(sp):
            for L in (0, 1):
                for u in (0, 1):
                    sp.sem_inc(hkeep[L][u], 16)
                for r in range(4):
                    sp.sem_inc(st[L][r], 16)

            def load_batch(b, s):
                sp.dma_start(X[:, b * J:(b + 1) * J, :], L0_attn_q[b].rearrange("(p j) d -> p j d", j=J)).then_inc(s, 16)

            def load_mods(L):
                sp.dma_start(MB[:, :, :, :].rearrange("p b m d -> p b (m d)"),
                             mod_d[L][:, 0:3 * D].partition_broadcast(P)).then_inc(mod_in[L], 16)
                if L == 0:
                    sp.dma_start(GBB[0][:, :, :], mod_d[0][:, 3 * D:4 * D].partition_broadcast(P)).then_inc(mod_in[0], 16)

            sp.dma_start(crow[:, 0, :], C_D[0]).then_inc(in_small[0], 16)
            load_batch(0, in_x0)
            sp.dma_start(wmod[0], WMOD_D[0]).then_inc(in_small[0], 16)
            for w, src in zip(wsm, (L0_attn_wq, L0_attn_wk, L0_attn_wv, L0_attn_wo)):
                sp.dma_start(w, src).then_inc(in_small[0], 16)
            sp.dma_start(erow[:, 0, :], L0_ffn_uzman_embeddings).then_inc(in_small[0], 16)
            sp.dma_start(bonus[:, :], L0_ffn_onbellek_durumu.partition_broadcast(P)).then_inc(in_small[0], 16)
            for b in range(1, NB):
                load_batch(b, in_x)
            sp.wait_ge(rows_ready, 1)
            sp.dma_start(mod_d[0], crow[:, :, :].rearrange("b m d -> b (m d)")).then_inc(mod_out[0], 16)
            sp.wait_ge(mod_out[0], 16)
            load_mods(0)
            sp.wait_ge(mod_out[0], 16)
            sp.dma_start(crow[:, 0, :], C_D[1]).then_inc(in_small[1], 16)
            sp.dma_start(wmod[1], WMOD_D[1]).then_inc(in_small[1], 16)
            for n in range(3):
                sp.dma_start(wsm[n], L1_attn_W_qkv[n * D:(n + 1) * D, :]).then_inc(in_small[1], 16)
            sp.dma_start(RW[1][:, :], L1_ffn_Wr).then_inc(in_small[1], 16)
            sp.dma_start(brB[:, :], L1_ffn_br.partition_broadcast(P)).then_inc(in_small[1], 16)
            sp.dma_start(b1row, L1_ffn_b1.rearrange("e (c p) -> (e c) p", p=P)).then_inc(in_small[1], 16)
            sp.dma_start(B2[1][0:1, :, :].rearrange("a e d -> a (e d)"), L1_ffn_b2.rearrange("(a e) d -> a (e d)", a=1)).then_inc(in_small[1], 16)
            for L in (0, 1):
                if L == 0:
                    sp.dma_start(W1[:, :, :], W1_D[0].rearrange("e d h -> d e h")).then_inc(in_moe[0], 16)
                sp.dma_start(W2[L][:, :, :, :], W2_D[L].rearrange("e (c p) d -> p e c d", p=P)).then_inc(in_moe[L], 16)
                if L == 0:
                    sp.dma_start(B1[:, :, :].rearrange("p e h -> p (e h)"),
                                 B1_D[0].rearrange("e h -> (e h)").partition_broadcast(P)).then_inc(in_moe[0], 16)
                    sp.dma_start(B2[0][:, :, :].rearrange("p e d -> p (e d)"),
                                 B2_D[0].rearrange("e d -> (e d)").partition_broadcast(P)).then_inc(in_moe[0], 16)
            sp.wait_ge(rows_ready, 2)
            sp.dma_start(mod_d[1], crow[:, :, :].rearrange("b m d -> b (m d)")).then_inc(mod_out[1], 16)
            sp.wait_ge(mod_out[1], 16)
            sp.dma_start(GBB[1][:, :, :], mod_d[1][:, 3 * D:4 * D].partition_broadcast(P)).then_inc(mod_in[1], 16)
            sp.wait_ge(consts, 3)
            for g in (0, 1):
                sp.dma_start(xs_d[g].rearrange("(a p r) d -> p a (r d)", p=P, r=J),
                             H[:, 0:J, :].rearrange("p j d -> p (j d)").unsqueeze(1).to_broadcast([P, TILES[0] // J, J * D]))\
                  .then_inc(xs_zero, 16)

            def load(L, g, t, r):
                sp.wait_ge(xt_mm[L], BIAS + t + (g * TILES[L] - 3))
                sp.dma_start(xt[:, r, :], xs_d[g][bass.ds(t * P, P), :]).then_inc(ld[L][r], 16)

            def store(L, g, t, r):
                sp.wait_ge(y_ready[L], BIAS + t + (g * TILES[L] + 1))
                sp.dma_start(ys_d[L][g][bass.ds(t * P, P), :], yt[:, r, :]).then_inc(st[L][r], 16)

            def keep(L, q, u, at):
                sp.wait_ge(hc_ready[L], BIAS + q + 1)
                sp.dma_start(H[:, at, :], Hc[:, u, :, :]).then_inc(hkeep[L][u], 16)

            sp.wait_ge(xs_zero, 32)
            for L in (0, 1):
                if L == 1:
                    sp.wait_ge(hu_ready[0], BIAS + 2 * TILES[0])
                    sp.dma_start(B1[:, :, :].rearrange("p e h -> p (e h)"),
                                 B1_D[1].rearrange("e h -> (e h)").partition_broadcast(P)).then_inc(in_late, 16)
                    sp.dma_start(W1[:, :, :], W1_D[1].rearrange("e d h -> d e h")).then_inc(in_late, 16)
                keep(L, 0, 0, slice(0, J))
                with sp.Fori(0, 3, 1) as i:
                    keep(L, 2 * i + 1, 1, bass.ds(i * 2 * J + J, J))
                    keep(L, 2 * i + 2, 0, bass.ds(i * 2 * J + 2 * J, J))
                if L == 1:
                    sp.wait_ge(rows_ready, 3)
                    sp.dma_start(b2_d, B2[1][0:1, :, :].rearrange("p e d -> p (e d)")).then_inc(b2_out, 16)
                    sp.wait_ge(b2_out, 16)
                    sp.dma_start(B2[1][:, :, :].rearrange("p e d -> p (e d)"),
                                 b2_d.rearrange("a n -> (a n)").partition_broadcast(P)).then_inc(b2_in, 16)
                NTG = TILES[L]
                sp.wait_ge(scat[L][0], 16 * TOPK[L] * GT)
                for r in range(4):
                    load(L, 0, r, r)
                keep(L, 7, 1, slice(7 * J, 8 * J))
                if L == 0:
                    sp.wait_ge(wog_ready, BIAS + NB)
                    load_mods(1)
                for g in (0, 1):
                    with sp.Fori(0, NTG // 4 - 1, 1) as q:
                        for r in range(4):
                            load(L, g, q * 4 + (4 + r), r)
                            store(L, g, q * 4 + r, r)
                    if g == 0:
                        sp.wait_ge(scat[L][1], 16 * TOPK[L] * GT)
                    for r in range(4):
                        if g == 0:
                            load(L, 1, r, r)
                        store(L, g, NTG - 4 + r, r)
            for b in range(NB):
                sp.wait_ge(comb_done[1], BIAS + (b + 1) * J)
                sp.dma_start(out[b].rearrange("(p j) d -> p j d", j=J), X[:, b * J:(b + 1) * J, :]).then_inc(stored, 16)
            sp.wait_ge(stored, 16 * NB)


        N_SMALL = [8, 9]
        in_moe_all = [4, 1]

        @block.tensor
        def _(pe):
            bias(pe, "pe")
            mm, tr = nc.tensor.matmul, nc.tensor.transpose

            def setup(L):
                d = 16 * L
                pe.wait_ge(in_small[L], 16 * N_SMALL[L])
                pe.wait_ge(consts, 3)
                base = [0, 5][L]
                if L == 1:
                    pe.wait_ge(s_dve, base)
                mm(ps_p[:, 0, 0:D], wsm[0], wsm[1], start=True, stop=True)
                tr(ps_p[:, 1, 0:D], wsm[2], ident[:, :])
                if L == 0:
                    tr(ps_p[:, 1, D:2 * D], wsm[3], ident[:, :])
                    pe.wait_ge(s_dve, 1)
                    tr(ps_p[:, 1, 2 * D:2 * D + E], erow[:, 0, :], ident[0:E, 0:E])
                    tr(ps_p[:, 1, 2 * D + E:2 * D + 2 * E], erow[:, 1, :], ident[0:E, 0:E]).then_inc(s_pe, 1)
                else:
                    tr(ps_p[:, 1, D:D + E * HC], b1row, ident[0:E * HC, 0:E * HC]).then_inc(s_pe, 1)
                pe.wait_ge(s_dve, base + 2 - L)
                tr(ps_a[:, 0:NB], crow[:, 2, :], ident[0:NB, 0:NB]).then_inc(s_pe, 1)
                pe.wait_ge(s_dve, base + 3 - L)
                mm(ps_s[0:NB, 0, 0:3 * D], scT[:, :], wmod[L][:, 0:3 * D], start=True, stop=True)
                mm(ps_s[0:NB, 1, 0:3 * D], scT[:, :], wmod[L][:, 3 * D:6 * D], start=True, stop=True).then_inc(s_pe, 1)
                pe.wait_ge(s_dve, base + 4 - L)
                tr(ps_a[:, 0:NB], csrow[:, 0, :], ident[0:NB, 0:NB])
                tr(ps_a[:, NB:2 * NB], csrow[:, 1, :], ident[0:NB, 0:NB]).then_inc(s_pe, 1)

            def constant_rows():
                pe.wait_ge(in_moe[1], 16)
                for e in range(E):
                    for c in range(HC):
                        last = mm(ps_o[0:1, e // 4, (e % 4) * D:(e % 4 + 1) * D], b1T[:, e * HC + c:e * HC + c + 1],
                                  W2[1][:, e, c, :], start=(c == 0), stop=(c == HC - 1))
                last.then_inc(s_pe, 1)

            def head(L, b, u):
                pe.wait_ge(xn_ready[L], BIAS + b + 1)
                pe.wait_ge(hT2_ready[L], BIAS + b - 2)
                for j in range(J):
                    last = tr(ps_a[:, j * P:(j + 1) * P], xn[:, u, j, :], ident[:, :])
                last.then_inc(h_tr[L], 1)
                pe.wait_ge(hT_ready[L], BIAS + b + 1)
                pe.wait_ge(r_ready[L], BIAS + b - 2)
                if L == 0:
                    pe.wait_ge(y_add, BIAS + b - 1)
                mm(ps_b[:, :], A[L][:, :], hT[:, u, :], start=True, stop=True).then_inc(g_mm[L], 1)
                for j in range(J):
                    last = mm(ps_a[:, j * P:(j + 1) * P], hT[:, u, j * P:(j + 1) * P], WvT[L][:, :], start=True, stop=True)
                last.then_inc(v_mm[L], 1)

            def scores(L, n, b, u, j):
                if j == 0:
                    pe.wait_ge(gT_ready[L], BIAS + b + 1)
                pe.wait_ge(exp_done[L], BIAS + n - 1)
                mm(ps_s[:, j % 2, :], gT[:, u, j * P:(j + 1) * P], hT[:, u, :], start=True, stop=True).then_inc(s_mm[L], 1)

            def prob_tr(L, n, j):
                pe.wait_ge(exp_done[L], BIAS + n + 1)
                pe.wait_ge(pt_ready[L], BIAS + n - 1)
                for c in range(J):
                    last = tr(ps_p[:, j % 2, c * P:(c + 1) * P], prob[:, j % 2, c * P:(c + 1) * P], ident[:, :])
                last.then_inc(pt_mm[L], 1)

            def prob_v(L, n, u, j):
                pe.wait_ge(pt_ready[L], BIAS + n + 1)
                pe.wait_ge(o_done[L], BIAS + n - 1)
                for c in range(J):
                    last = mm(ps_o[:, j % 2, 0:D], probT[:, j % 2, c, :], V[:, u, c, :], start=(c == 0), stop=(c == J - 1))
                last.then_inc(pv_mm[L], 1)

            def out_proj(b, u):
                pe.wait_ge(o_done[0], BIAS + 4 * b + 4)
                pe.wait_ge(wog_ready, BIAS + b + 1)
                pe.wait_ge(r_ready[0], BIAS + b)
                pe.wait_ge(gT_ready[0], BIAS + upto(b + 2))
                for j in range(J):
                    last = mm(ps_b[:, j * P:(j + 1) * P], On[:, j, :], woG[:, u, :], start=True, stop=True)
                last.then_inc(y_mm, 1)

            def post_tr(L, q, u, last_v):
                pe.wait_ge(hc_ready[L], BIAS + q + 1)
                pe.wait_ge(v_ready[L], BIAS + last_v)
                for j in range(J):
                    last = tr(ps_a[:, j * P:(j + 1) * P], Hc[:, u, j, :], ident[:, :])
                last.then_inc(p_tr[L], 1)

            def router(L, q):
                pe.wait_ge(hT2_ready[L], BIAS + q + 1)
                pe.wait_ge(gT_ready[L], BIAS + upto(q + 3))
                if L == 0:
                    pe.wait_ge(y_add, BIAS + q + 1)
                w = NR[L]
                for j in range(J):
                    last = mm(ps_b[:, j * w:(j + 1) * w], hT2[:, j * P:(j + 1) * P], RW[L][:, :], start=True, stop=True)
                last.then_inc(r_mm[L], 1)

            def ranks(L, g):
                c = TOPK[L] * GT
                pe.wait_ge(m_ready, 2 * L + g + 1)
                pe.wait_ge(gT_ready[L], BIAS + (NB - 1 if g == 0 else NB))
                mm(ps_b[:, 0:E * c], upper[:, :], Mb[:, 0:E * c], start=True, stop=True)
                last = mm(ps_b[:, E * c:2 * E * c], ones[:, :], Mb[:, 0:E * c], start=True, stop=True)
                last.then_inc(rank_mm, 1)

            def body(L, b, u, prev2, prev, nxt, rank=0):
                for j in range(J):
                    n = 4 * b + j
                    if j < 3:
                        scores(L, n + 1, b, u, j + 1)
                    elif nxt:
                        scores(L, n + 1, b + 1, 1 - u, 0)
                    prob_tr(L, n, j)
                    if j == 1 and prev and L == 0:
                        out_proj(b - 1, 1 - u)
                    if j > 0:
                        prob_v(L, n - 1, u, j - 1)
                    elif prev:
                        prob_v(L, n - 1, 1 - u, 3)
                    if j == 0 and rank:
                        pe.wait_ge(rank_read, rank)
                    if j == 0 and prev2:
                        router(L, b - 2)
                    if j == 2 and nxt:
                        head(L, b + 1, 1 - u)
                    if j == 3 and prev:
                        post_tr(L, b - 1, 1 - u, b + 2 if nxt else NB)

            def x_tr(L, t, r):
                pe.wait_ge(ld[L][r], 16 * (t // 4 + 1) if isinstance(t, int) else t[1])
                m = t if isinstance(t, int) else t[0]
                pe.wait_ge(xT_ready[L], BIAS + m)
                tr(ps_a[:, 0:P], xt[:, r, :], ident[:, :]).then_inc(xt_mm[L], 1)

            def up(L, t, r):
                e = pe.value_load(eid[0:1, bass.ds(t, 1)], min_val=0, max_val=E - 1)
                pe.wait_ge(xT_ready[L], BIAS + t + 1)
                pe.wait_ge(hu_ready[L], BIAS + t - 1)
                mm(ps_s[:, r % 2, :], xT[:, r % 2, :], W1[:, bass.ds(e, 1), :].rearrange("p a h -> p (a h)"),
                   start=True, stop=True).then_inc(up_mm[L], 1)
                return e

            def h_tr_mm(L, t, r):
                pe.wait_ge(hu_ready[L], BIAS + t + 1)
                pe.wait_ge(hTm_ready[L], BIAS + t - 1)
                for c in range(HC):
                    last = tr(ps_p[:, r % 2, c * P:(c + 1) * P], hu[:, r % 2, c * P:(c + 1) * P], ident[:, :])
                last.then_inc(ht_mm[L], 1)

            def down(L, t, r, e):
                pe.wait_ge(hTm_ready[L], BIAS + t + 1)
                pe.wait_ge(y_ready[L], BIAS + t - 1)
                for c in range(HC):
                    last = mm(ps_o[:, r % 2, 0:D], hTm[:, r % 2, c, :],
                              W2[L][:, bass.ds(e, 1), c, :].rearrange("p a d -> p (a d)"), start=(c == 0), stop=(c == HC - 1))
                last.then_inc(dn_mm[L], 1)

            def quad(L, q, first=False, last=False):
                for r in range(4):
                    t = 4 * q + r
                    if not (last and r >= 2):
                        x_tr(L, (t + 2, 16 * (q + 1 + (r + 2) // 4)), (r + 2) % 4)
                    if not (last and r == 3):
                        up(L, t + 1, (r + 1) % 4)
                    h_tr_mm(L, t, r)
                    if not (first and r == 0):
                        e = pe.value_load(eid[0:1, bass.ds(t - 1, 1)], min_val=0, max_val=E - 1)
                        down(L, t - 1, (r + 3) % 4, e)

            for L in (0, 1):
                setup(L)
            pe.wait_ge(s_dve, 10)
            for L in (0, 1):
                NQ, CQ = 2 * TILES[L] // 4, TILES[L] // 4 + 1
                if L == 1:
                    pe.wait_ge(y_ready[0], BIAS + 2 * TILES[0])
                    constant_rows()
                head(L, 0, 0)
                scores(L, 0, 0, 0, 0)
                if L == 1:
                    pe.wait_ge(rows_ready, 3)
                body(L, 0, 0, False, False, True)
                body(L, 1, 1, False, True, True)
                with pe.Fori(1, 3, 1) as i:
                    body(L, 2 * i, 0, True, True, True)
                    body(L, 2 * i + 1, 1, True, True, True)
                ranks(L, 0)
                body(L, 6, 0, True, True, True, rank=2 * L + 1)
                body(L, 7, 1, True, True, False)
                prob_v(L, 4 * 7 + 3, 1, 3)
                router(L, 6)
                pe.wait_ge(in_moe[L], 16 * in_moe_all[L])
                if L == 1:
                    pe.wait_ge(in_late, 32)
                pe.wait_ge(hT2_ready[L], BIAS + NB - 1)
                pe.wait_ge(exp_done[L], BIAS + NB * J)
                pe.wait_ge(route_done, 2 * L + 1)
                x_tr(L, 0, 0)
                x_tr(L, 1, 1)
                up(L, 0, 0)
                if L == 0:
                    out_proj(7, 1)
                pe.wait_ge(pt_ready[L], BIAS + NB * J)
                pe.wait_ge(o_done[L], BIAS + NB * J)
                quad(L, 0, first=True)
                pe.wait_ge(xT_ready[L], BIAS + 6)
                post_tr(L, 7, 1, NB)
                pe.wait_ge(hT2_ready[L], BIAS + NB)
                quad(L, 1)
                router(L, 7)
                quad(L, 2)
                ranks(L, 1)
                with pe.Fori(3, 5, 1) as q:
                    quad(L, q)
                pe.wait_ge(route_done, 2 * L + 2)
                with pe.Fori(5, NQ - 1, 1) as q:
                    quad(L, q)
                quad(L, NQ - 1, last=True)
                down(L, 4 * NQ - 1, 3, pe.value_load(eid[0:1, 4 * NQ - 1:4 * NQ], min_val=0, max_val=E - 1))

        @block.gpsimd
        def _(pool):
            bias(pool, "pool")
            g = nc.gpsimd
            steps = [0]

            def link(ins):
                steps[0] += 1
                ins.then_inc(pool_chain, 1)
                pool.wait_ge(pool_chain, steps[0])

            g.memset(H[:, 0:J, :], 0.0).then_inc(consts, 1)
            link(g.memset(ident[:, :], 0.0))
            link(g.affine_select(out=ident[:, :], in_=ident[:, :], compare_op=ALU.not_equal, fill=1.0, base=0,
                                 pattern=[[-1, P]], channel_multiplier=1))
            link(g.memset(ones[:, :], 1.0))
            link(g.affine_select(out=upper[:, :], in_=ones[:, :], compare_op=ALU.is_gt, fill=0.0, base=0,
                                 pattern=[[1, P]], channel_multiplier=-1))
            kw = dict(channel_multiplier=0, allow_small_or_imprecise_dtypes=True)
            link(g.iota(rev8[:, :], pattern=[[-1, E]], base=E, **kw))
            link(g.iota(up8[:, :], pattern=[[1, E]], base=1, **kw))
            link(g.iota(thr16[:, :], pattern=[[P, GT]], base=0, **kw))
            link(g.iota(iotaT[:, :], pattern=[[1, TILES[0]]], base=0, **kw))
            link(g.memset(onesf[:, :], 1.0))
            for L in (0, 1):
                link(g.memset(keep[L][:, :], 1.0))
                last = g.memset(keep[L][:, :].rearrange("p (e c) -> p e c", e=E)[:, :, 0:1], 0.0)
                last.then_inc(consts, 1)

            def normalise(L, b, u):
                pool.wait_ge(ln1_ready[L], BIAS + b + 1)
                pool.wait_ge(h_tr[L], BIAS + b - 1)
                def wide(stat):
                    return stat[:, u, :].unsqueeze(2).to_broadcast([P, J, D])

                g.tensor_tensor(xn[:, u, :, :], X[:, bass.ds(b * J, J), :], wide(rs1), ALU.mult).then_inc(xn_chain[L], 1)
                pool.wait_ge(xn_chain[L], b + 1)
                g.tensor_tensor(xn[:, u, :, :], xn[:, u, :, :], wide(nb1), ALU.add).then_inc(xn_ready[L], 1)

            def scale_wo(b, u):
                pool.wait_ge(y_mm, BIAS + b - 1)
                g.tensor_tensor(woG[:, u, :], woT[:, :], MB[:, bass.ds(b, 1), 0, :].rearrange("p a d -> p (a d)"),
                                ALU.mult).then_inc(wog_ready, 1)

            def squares(q, u):
                pool.wait_ge(hc_ready[0], BIAS + q + 1)
                pool.wait_ge(sq_used, BIAS + q - 1)
                g.tensor_tensor(sq[:, u, :, :], Hc[:, u, :, :], Hc[:, u, :, :], ALU.mult).then_inc(sq_ready, 1)

            def body(L, b, u, prev, nxt):
                if nxt:
                    normalise(L, b + 1, 1 - u)
                if L == 0:
                    scale_wo(b, u)
                    if prev:
                        squares(b - 1, 1 - u)

            def scatter(L, grp):
                pool.wait_ge(route_done, 2 * L + grp + 1)
                for u in (0, 1):
                    pool.wait_ge(hkeep[L][u], 16 + 16 * (GB // 2) * (grp + 1))
                if L == 0 and grp == 0:
                    pool.wait_ge(xs_zero, 32)
                for c in range(TOPK[L] * GT):
                    g.indirect_dma_start(out=xs_d[grp], out_offset=bass.IndirectOffsetOnAxis(ap=slot[:, grp, c:c + 1], axis=0),
                                         in_=H[:, grp * GT + c % GT, :], in_offset=None).then_inc(scat[L][grp], 16)

            def gather(L, grp, i, r, count):
                pool.wait_ge(comb_done[L], BIAS + count - 3)
                for k in range(TOPK[L]):
                    last = g.tensor_copy(cur[:, r, k:k + 1], slot[:, grp, bass.ds(i + k * GT, 1)])
                    last.then_inc(cur_ready[L], 1)
                wait_apart(pool, cur_ready[L], TOPK[L] * (count + 1))
                for k in range(TOPK[L]):
                    g.indirect_dma_start(out=yg[:, r, k, :], out_offset=None, in_=ys_d[L][grp],
                                         in_offset=bass.IndirectOffsetOnAxis(ap=cur[:, r, k:k + 1], axis=0)).then_inc(gat[L][r], 16)

            def stored_rows(L, grp):
                for r in range(4):
                    pool.wait_ge(st[L][r], 16 + 16 * (TILES[L] // 4) * (grp + 1))

            def gathers(L, grp):
                stored_rows(L, grp)
                with pool.Fori(0, GT // 4, 1) as q:
                    for r in range(4):
                        gather(L, grp, q * 4 + r, r, q * 4 + (r + grp * GT))

            pool.wait_ge(in_x0, 16)
            normalise(0, 0, 0)
            pool.wait_ge(mod_in[0], 32)
            pool.wait_ge(s_dve, 5)
            for L in (0, 1):
                if L == 1:
                    stored_rows(0, 1)
                    for r in range(4):
                        gather(0, 1, r, r, GT + r)
                    normalise(1, 0, 0)
                body(L, 0, 0, False, True)
                if L == 1:
                    for r in range(4):
                        gather(0, 1, 4 + r, r, GT + 4 + r)
                body(L, 1, 1, True, True)
                with pool.Fori(1, 3, 1) as i:
                    for k in (0, 1):
                        body(L, 2 * i + k, k, True, True)
                        if L == 1:
                            for r in (2 * k, 2 * k + 1):
                                gather(0, 1, i * 4 + (4 + r), r, i * 4 + (GT + 4 + r))
                body(L, 6, 0, True, True)
                if L == 0:
                    scale_wo(7, 1)
                scatter(L, 0)
                if L == 0:
                    squares(6, 0)
                    squares(7, 1)
                scatter(L, 1)
                gathers(L, 0)
                if L == 1:
                    gathers(1, 1)

        @block.scalar
        def _(act):
            bias(act, "act")
            fn = nc.scalar.activation

            def evac(out_, in_):
                return fn(out_, in_, ACT.Copy)

            def setup(L):
                act.wait_ge(in_small[L], 16 * N_SMALL[L])
                fn(crow[:, 1, :], crow[:, 0, :], ACT.Exp, scale=-1.0).then_inc(s_act, 1)

            def head(L, b, u):
                act.wait_ge(h_tr[L], BIAS + b + 1)
                src = ps_a[:, :].rearrange("p (j t) -> p j t", j=J)
                dst = hT[:, u, :].rearrange("p (t j) -> p j t", j=J) if L == 0 else hT[:, u, :].rearrange("p (j t) -> p j t", j=J)
                fn(dst, src, ACT.Identity, bias=saT[L][:, bass.ds(b, 1)], scale=caT[L][:, bass.ds(b, 1)]).then_inc(hT_ready[L], 1)
                act.wait_ge(g_mm[L], BIAS + b + 1)
                evac(gT[:, u, :], ps_b[:, :]).then_inc(gT_ready[L], 1)
                if L == 0:
                    act.wait_ge(v_mm[0], BIAS + b + 1)
                    evac(V[:, u, :, :], ps_a[:, :].rearrange("p (j d) -> p j d", j=J)).then_inc(v_ready[0], 1)

            def exps(L, n, j, u):
                act.wait_ge(negm_ready[L], BIAS + n + 1)
                act.wait_ge(pt_mm[L], BIAS + n - 1)
                k = 4 * u + j
                fn(prob[:, j % 2, :], ps_s[:, j % 2, :], ACT.Exp, bias=negm[:, k:k + 1],
                   accum_out=rowsum[:, k:k + 1]).then_inc(exp_done[L], 1)

            def prob_out(L, n, j):
                act.wait_ge(pt_mm[L], BIAS + n + 1)
                act.wait_ge(pv_mm[L], BIAS + n - 1)
                evac(probT[:, j % 2, :, :], ps_p[:, j % 2, :].rearrange("p (c q) -> p c q", c=J)).then_inc(pt_ready[L], 1)

            def attn_out(n, j, u, b):
                act.wait_ge(pv_mm[0], BIAS + n + 1)
                act.wait_ge(rinv_ready[0], BIAS + n + 1)
                if j == 0:
                    act.wait_ge(y_mm, BIAS + b)
                fn(On[:, j, :], ps_o[:, j % 2, 0:D], ACT.Copy, scale=rinv[:, 4 * u + j:4 * u + j + 1]).then_inc(o_done[0], 1)

            def post(L, q):
                act.wait_ge(p_tr[L], BIAS + q + 1)
                act.wait_ge(r_mm[L], BIAS + q)
                evac(hT2[:, :], ps_a[:, :]).then_inc(hT2_ready[L], 1)

            def body(L, b, u, prev, nxt):
                for j in range(J):
                    n = 4 * b + j
                    if j < 3:
                        exps(L, n + 1, j + 1, u)
                    elif nxt:
                        exps(L, n + 1, 0, 1 - u)
                    prob_out(L, n, j)
                    if L == 0:
                        if j > 0:
                            attn_out(n - 1, j - 1, u, b)
                        elif prev:
                            attn_out(n - 1, 3, 1 - u, b - 1)
                    if j == 2 and nxt:
                        head(L, b + 1, 1 - u)
                    if j == 3 and prev:
                        post(L, b - 1)

            def x_out(L, t, r):
                act.wait_ge(xt_mm[L], BIAS + t + 1)
                act.wait_ge(up_mm[L], BIAS + t - 1)
                evac(xT[:, r % 2, :], ps_a[:, 0:P]).then_inc(xT_ready[L], 1)

            def gelu(L, t, r):
                act.wait_ge(ht_mm[L], BIAS + t + 1)
                act.wait_ge(dn_mm[L], BIAS + t - 1)
                fn(hTm[:, r % 2, :, :], ps_p[:, r % 2, :].rearrange("p (c q) -> p c q", c=HC),
                   ACT.Gelu if L == 0 else ACT.Relu).then_inc(hTm_ready[L], 1)

            def quad(L, q, last=False):
                for r in range(4):
                    t = 4 * q + r
                    if not (last and r >= 2):
                        x_out(L, t + 2, r)
                    gelu(L, t, r)

            def top2_exp(g):
                act.wait_ge(gap_ready, g + 1)
                fn(row[:, 5, :], row[:, 4, :], ACT.Exp).then_inc(gap_exp, 1)

            for L in (0, 1):
                setup(L)
            for L in (0, 1):
                act.wait_ge(s_dve, [5, 10][L])
                head(L, 0, 0)
                exps(L, 0, 0, 0)
                body(L, 0, 0, False, True)
                body(L, 1, 1, True, True)
                with act.Fori(1, 3, 1) as i:
                    body(L, 2 * i, 0, True, True)
                    body(L, 2 * i + 1, 1, True, True)
                if L == 0:
                    top2_exp(0)
                body(L, 6, 0, True, True)
                body(L, 7, 1, True, False)
                if L == 0:
                    attn_out(4 * 7 + 3, 3, 1, 7)
                x_out(L, 0, 0)
                x_out(L, 1, 1)
                quad(L, 0)
                post(L, 7)
                quad(L, 1)
                quad(L, 2)
                if L == 0:
                    top2_exp(1)
                with act.Fori(3, 2 * TILES[L] // 4 - 1, 1) as q:
                    quad(L, q)
                quad(L, 2 * TILES[L] // 4 - 1, last=True)

        @block.vector
        def _(dve):
            bias(dve, "dve")
            v = nc.vector
            steps = [0]

            def link(ins):
                steps[0] += 1
                ins.then_inc(chain, 1)
                dve.wait_ge(chain, steps[0])

            def rsqrt(x, y, t, out_, step):
                step(v.tensor_scalar(y.bitcast(I32), x.bitcast(I32), -0.5, float(MAGIC), ALU.mult, ALU.add))
                for k in range(3):
                    step(v.tensor_tensor(t, y, y, ALU.mult))
                    step(v.scalar_tensor_tensor(t, t, -0.5, x, ALU.mult, ALU.mult))
                    step(v.scalar_tensor_tensor(out_ if k == 2 else y, t, 1.5, y, ALU.add, ALU.mult))

            def setup(L):
                pe0, d0 = [0, 4][L], [0, 5][L]
                dve.wait_ge(in_small[L], 16 * N_SMALL[L])
                if L == 0:
                    link(v.tensor_tensor(erow[:, 1, :], erow[:, 0, :], erow[:, 0, :], ALU.mult))
                    link(v.tensor_reduce(nte[:, 0:1], erow[:, 1, :], AX.X, ALU.add))
                    rsqrt(nte[:, 0:1], nte[:, 1:2], nte[:, 2:3], nte[:, 3:4], link)
                    link(v.tensor_tensor(nte[:, 4:5], nte[:, 3:4], nte[:, 0:1], ALU.mult))
                    link(v.tensor_scalar(nte[:, 5:6], nte[:, 4:5], NORM_EPS, None, ALU.add))
                    link(v.reciprocal(nte[:, 6:7], nte[:, 5:6]))
                    v.tensor_scalar(erow[:, 1, :], erow[:, 0, :], nte[:, 6:7], None, ALU.mult).then_inc(s_dve, 1)
                dve.wait_ge(s_act, L + 1)
                link(v.tensor_scalar(crow[:, 1, :], crow[:, 1, :], 1.0, None, ALU.add))
                link(v.reciprocal(crow[:, 3, :], crow[:, 1, :]))
                v.tensor_tensor(crow[:, 2, :], crow[:, 0, :], crow[:, 3, :], ALU.mult).then_inc(s_dve, 1)
                dve.wait_ge(s_pe, pe0 + 1)
                v.tensor_scalar(A[L][:, :], ps_p[:, 0, 0:D], SCALE[L], None, ALU.mult)
                v.tensor_copy(WvT[L][:, :], ps_p[:, 1, 0:D])
                if L == 0:
                    v.tensor_copy(woT[:, :], ps_p[:, 1, D:2 * D])
                    v.tensor_copy(RW[0][:, :], ps_p[:, 1, 2 * D:2 * D + 2 * E])
                else:
                    v.tensor_scalar(b1T[:, :], ps_p[:, 1, D:D + E * HC], 0.0, None, ALU.max)
                dve.wait_ge(s_pe, pe0 + 2)
                v.tensor_copy(scT[:, :], ps_a[:, 0:NB]).then_inc(s_dve, 1)
                dve.wait_ge(s_pe, pe0 + 3)
                if L == 1:
                    dve.wait_ge(mod_out[0], 16)
                link(v.tensor_scalar(csrow[:, 0, :], ps_s[0:NB, 0, D:2 * D], 1.0, None, ALU.add))
                v.tensor_copy(csrow[:, 1, :], ps_s[0:NB, 0, 0:D]).then_inc(s_dve, 1)
                v.tensor_scalar(crow[:, 1, :], ps_s[0:NB, 1, D:2 * D], 1.0, None, ALU.add)
                v.tensor_copy(crow[:, 2, :], ps_s[0:NB, 1, 0:D])
                for m, src in ((0, ps_s[0:NB, 0, 2 * D:3 * D]), (3, ps_s[0:NB, 1, 2 * D:3 * D])):
                    link(v.tensor_copy(crow[:, m, :], src))
                    link(v.scalar_tensor_tensor(erow[:, 0, :], crow[:, m, :], -1.0, crow[:, m, :], ALU.mult, ALU.max))
                    link(v.tensor_scalar(erow[:, 0, :], erow[:, 0, :], 0.25, None, ALU.max))
                    link(v.tensor_scalar(erow[:, 1, :], crow[:, m, :], 0.0, 2.0, ALU.is_ge, ALU.mult))
                    last = v.scalar_tensor_tensor(crow[:, m, :], erow[:, 1, :], -1.0, erow[:, 0, :], ALU.add, ALU.mult)
                    if m == 0:
                        link(last)
                last.then_inc(rows_ready, 1)
                dve.wait_ge(s_pe, pe0 + 4)
                link(v.tensor_copy(caT[L][:, :], ps_a[:, 0:NB]))
                if L == 1:
                    dve.wait_ge(rows_ready, 2)
                v.tensor_copy(saT[L][:, :], ps_a[:, NB:2 * NB]).then_inc(s_dve, 1 if L == 0 else 2)

            def constant_rows():
                dve.wait_ge(s_pe, 9)
                dve.wait_ge(in_small[1], 16 * N_SMALL[1])
                b2, r = B2[1][0:1, :, :], ps_o[0:1, :, :].rearrange("p a (e d) -> p (a e) d", d=D)
                total, rows = rrow[:, 0:D], B2[1][0:1, :, :]
                link(v.tensor_reduce(rrow[:, 0:D], b2.rearrange("p e d -> p d e"), AX.X, ALU.add))
                link(v.tensor_reduce(rrow[:, D:2 * D], r.rearrange("p e d -> p d e"), AX.X, ALU.add))
                link(v.tensor_tensor(rrow[:, 0:D], rrow[:, 0:D], rrow[:, D:2 * D], ALU.add))
                v.tensor_tensor(rows, rrow[:, 0:D].unsqueeze(1).to_broadcast([1, E, D]), r, ALU.subtract).then_inc(rows_ready, 1)

            def tile(ap, n):
                return ap[:, bass.ds(n, 1), :].rearrange("p a d -> p (a d)")

            def ln_stats(b, sem_, st_, mv_, nt_, rstd):
                base = LN_STEPS * b
                for j in range(J):
                    v.bn_stats(st_[:, j, :], tile(X, b * J + j)).then_inc(sem_, 1)
                wait_apart(dve, sem_, base + J)
                for j in range(J):
                    v.bn_aggr(mv_[:, j, :], st_[:, j, :]).then_inc(sem_, 1)
                dve.wait_ge(sem_, base + 2 * J)
                k = [2 * J]

                def step(ins):
                    k[0] += 1
                    ins.then_inc(sem_, 1)
                    dve.wait_ge(sem_, base + k[0])

                step(v.tensor_scalar(nt_[:, 0, :], mv_[:, :, 1], LN_EPS, None, ALU.add))
                rsqrt(nt_[:, 0, :], nt_[:, 1, :], nt_[:, 2, :], rstd, step)
                assert k[0] == LN_STEPS

            def ln1(L, b, u):
                if L == 1:
                    dve.wait_ge(comb_done[0], BIAS + b * J + J)
                wait_apart(dve, xn_ready[L], BIAS + b - 1)
                ln_stats(b, ln1_chain[L], st1, mv1, nt1, rs1[:, u, :])
                v.scalar_tensor_tensor(nb1[:, u, :], mv1[:, :, 0], -1.0, rs1[:, u, :], ALU.mult, ALU.mult).then_inc(ln1_ready[L], 1)

            def post(L, q, u, half):
                wait_apart(dve, *((y_add, BIAS + q + 1) if L == 0 else (o_done[1], BIAS + 4 * q + 4)))
                ln_stats(q, ln2_chain[L], st2, mv2, nt2, rs2[:, u, :])
                dve.wait_ge(p_tr[L], BIAS + q - 1)
                if L == 0:
                    dve.wait_ge(sq_ready, BIAS + q - 1)
                dve.wait_ge(hkeep[L][u], 16 + 16 * half)
                for j in range(J):
                    v.scalar_tensor_tensor(Hc[:, u, j, :], tile(X, q * J + j), mv2[:, j, 0:1],
                                           MB[:, bass.ds(q, 1), 1, :].rearrange("p a d -> p (a d)"),
                                           ALU.subtract, ALU.mult).then_inc(hc_chain[L], 1)
                dve.wait_ge(hc_chain[L], J * q + J)
                for j in range(J):
                    last = v.scalar_tensor_tensor(Hc[:, u, j, :], Hc[:, u, j, :], rs2[:, u, j:j + 1],
                                                  MB[:, bass.ds(q, 1), 2, :].rearrange("p a d -> p (a d)"), ALU.mult, ALU.add)
                last.then_inc(hc_ready[L], 1)

            def row_max(L, n, j, u):
                dve.wait_ge(s_mm[L], BIAS + n + 1)
                v.tensor_reduce(negm[:, 4 * u + j:4 * u + j + 1], ps_s[:, j % 2, :], AX.X, ALU.max, negate=True)\
                 .then_inc(negm_ready[L], 1)

            def row_scale(L, n, j, u):
                dve.wait_ge(exp_done[L], BIAS + n + 1)
                v.reciprocal(rinv[:, 4 * u + j:4 * u + j + 1], rowsum[:, 4 * u + j:4 * u + j + 1]).then_inc(rinv_ready[L], 1)

            def attn_out(n, j, u):
                dve.wait_ge(pv_mm[1], BIAS + n + 1)
                dve.wait_ge(rinv_ready[1], BIAS + n + 1)
                v.scalar_tensor_tensor(tile(X, n), ps_o[:, j % 2, 0:D], rinv[:, 4 * u + j:4 * u + j + 1], tile(X, n),
                                       ALU.mult, ALU.add).then_inc(o_done[1], 1)

            def y_out(b):
                dve.wait_ge(y_mm, BIAS + b + 1)
                xb = X[:, bass.ds(b * J, J), :]
                v.tensor_tensor(xb, ps_b[:, :].rearrange("p (j d) -> p j d", j=J), xb, ALU.add).then_inc(y_add, 1)

            def router_out(L, q):
                dve.wait_ge(r_mm[L], BIAS + q + 1)
                v.tensor_copy(sims[:, bass.ds(q * J, J), 0:NR[L]],
                              ps_b[:, 0:J * NR[L]].rearrange("p (j e) -> p j e", j=J)).then_inc(r_ready[L], 1)

            def sum_squares(q, u):
                dve.wait_ge(sq_ready, BIAS + q + 1)
                v.tensor_reduce(sumsq[:, bass.ds(q * J, J)], sq[:, u, :, :], AX.X, ALU.add).then_inc(sq_used, 1)

            def values_out(b, u):
                dve.wait_ge(v_mm[1], BIAS + b + 1)
                v.tensor_tensor(V[:, u, :, :], ps_a[:, :].rearrange("p (j d) -> p j d", j=J),
                                MB[:, bass.ds(b, 1), 0, :].to_broadcast([P, J, D]), ALU.mult).then_inc(v_ready[1], 1)

            def combine(L, b, at, r, count, uses):
                dve.wait_ge(gat[L][r], 16 * TOPK[L] * uses)
                a, grp = acc[:, r % 2, :], None
                c0 = count * (2 * TOPK[L] - 1)
                gb = tile(GBB[L], b)
                if L == 0:
                    v.tensor_scalar(a, yg[:, r, 0, :], weight[:, 0, bass.ds(at, 1)], None, ALU.mult).then_inc(comb_chain[0], 1)
                    dve.wait_ge(comb_chain[0], c0 + 1)
                    v.scalar_tensor_tensor(a, yg[:, r, 1, :], weight[:, 1, bass.ds(at, 1)], a, ALU.mult, ALU.add).then_inc(comb_chain[0], 1)
                    dve.wait_ge(comb_chain[0], c0 + 2)
                    v.tensor_tensor(a, a, gb, ALU.mult).then_inc(comb_chain[0], 1)
                    dve.wait_ge(comb_chain[0], c0 + 3)
                else:
                    v.tensor_tensor(a, yg[:, r, 0, :], gb, ALU.mult).then_inc(comb_chain[1], 1)
                    dve.wait_ge(comb_chain[1], c0 + 1)
                v.tensor_tensor(tile(X, at), tile(X, at), a, ALU.add).then_inc(comb_done[L], 1)

            def route(L, g):
                C, T = NC[L], slice(g * GT, (g + 1) * GT)
                dve.wait_ge(r_ready[L], BIAS + GB * (g + 1))
                three = [P, GT, E]
                Mv = M[:, 0:E * C].rearrange("p (e c) -> p c e", e=E)

                def over_e(x):
                    return x.unsqueeze(2).to_broadcast(three)

                def over_t(x):
                    return x.unsqueeze(1).to_broadcast(three)

                def first_of(mask, k):
                    link(v.tensor_tensor(rtmp[:, :, :], mask, over_t(rev8[:, :]), ALU.mult))
                    link(v.tensor_reduce(row[:, 1, :], rtmp[:, :, :], AX.X, ALU.max))
                    link(v.tensor_tensor(Mv[:, k * GT:(k + 1) * GT, :], over_t(rev8[:, :]), over_e(row[:, 1, :]), ALU.is_equal))

                def best(k, to):
                    link(v.tensor_reduce(row[:, to, :], score[:, :, :], AX.X, ALU.max))
                    link(v.tensor_tensor(rtmp[:, :, :], score[:, :, :], over_e(row[:, to, :]), ALU.is_equal))
                    first_of(rtmp[:, :, :], k)

                if L == 0:
                    dve.wait_ge(sq_used, BIAS + GB * (g + 1))
                    raw, cosn, ss = sims[:, T, 0:E], sims[:, T, E:2 * E], sumsq[:, T]
                    rsqrt(ss, row[:, 0, :], row[:, 1, :], row[:, 2, :], link)
                    link(v.tensor_tensor(row[:, 3, :], ss, row[:, 2, :], ALU.mult))
                    link(v.tensor_scalar(row[:, 3, :], row[:, 3, :], NORM_EPS, None, ALU.add))
                    link(v.reciprocal(row[:, 2, :], row[:, 3, :]))
                    link(v.tensor_tensor(score[:, :, :], cosn, over_e(row[:, 2, :]), ALU.mult))
                    link(v.scalar_tensor_tensor(score[:, :, :], over_t(bonus[:, :]), CACHE_BONUS, score[:, :, :], ALU.mult, ALU.add))
                    link(v.tensor_reduce(row[:, 0, :], raw, AX.X, ALU.min))
                    link(v.tensor_tensor(rtmp[:, :, :], raw, over_e(row[:, 0, :]), ALU.is_equal))
                    link(v.tensor_tensor(rtmp[:, :, :], rtmp[:, :, :], over_t(up8[:, :]), ALU.mult))
                    link(v.tensor_reduce(row[:, 1, :], rtmp[:, :, :], AX.X, ALU.max))
                    link(v.tensor_tensor(rtmp[:, :, :], over_t(up8[:, :]), over_e(row[:, 1, :]), ALU.is_equal))
                    link(v.scalar_tensor_tensor(score[:, :, :], rtmp[:, :, :], -BIG, score[:, :, :], ALU.mult, ALU.add))
                    best(0, 2)
                    link(v.scalar_tensor_tensor(score[:, :, :], Mv[:, 0:GT, :], -BIG, score[:, :, :], ALU.mult, ALU.add))
                    best(1, 3)
                    v.tensor_tensor(row[:, 4, :], row[:, 3, :], row[:, 2, :], ALU.subtract).then_inc(gap_ready, 1)
                else:
                    link(v.tensor_tensor(score[:, :, :], sims[:, T, 0:E], over_t(brB[:, :]), ALU.add))
                    best(0, 2)
                v.tensor_copy(Mb[:, 0:E * C], M[:, 0:E * C]).then_inc(m_ready, 1)
                if L == 0:
                    dve.wait_ge(gap_exp, g + 1)
                    link(v.tensor_scalar(row[:, 6, :], row[:, 5, :], 1.0, None, ALU.add))
                    link(v.reciprocal(weight[:, 0, T], row[:, 6, :]))
                    link(v.tensor_tensor(weight[:, 1, T], weight[:, 0, T], row[:, 5, :], ALU.mult))
                dve.wait_ge(rank_mm, 2 * L + g + 1)
                N = E * C
                link(v.tensor_copy(tot[:, 0:N], ps_b[:, N:2 * N]))
                link(v.tensor_tensor_scan(cum[:, 0:N], keep[L][:, :], tot[:, 0:N], 0.0, ALU.mult, ALU.add))
                link(v.tensor_tensor(tot[:, 0:N], cum[:, 0:N], tot[:, 0:N], ALU.subtract))
                v.tensor_tensor(tot[:, 0:N], tot[:, 0:N], ps_b[:, 0:N], ALU.add).then_inc(rank_read, 1)
                dve.wait_ge(rank_read, 2 * L + g + 1)
                n_e = cum[:, 0:N].rearrange("p (e c) -> p e c", e=E)[:, :, C - 1:C]
                cnt = cmpt[:, 0:GT, :].rearrange("p t e -> p (t e)").rearrange("p (e t) -> p e t", e=E)
                link(v.tensor_tensor(cnt, n_e.to_broadcast([P, E, GT]),
                                     thr16[:, :].unsqueeze(1).to_broadcast([P, E, GT]), ALU.is_gt))
                link(v.tensor_reduce(exs[:, 0, :], cnt, AX.X, ALU.add))
                link(v.tensor_tensor_scan(exs[:, 1, :], onesf[:, :], exs[:, 0, :], 0.0, ALU.mult, ALU.add))
                link(v.tensor_tensor(exs[:, 2, :], exs[:, 1, :], exs[:, 0, :], ALU.subtract))
                link(v.tensor_scalar(exs[:, 2, :], exs[:, 2, :], float(P), None, ALU.mult))
                tv = tot[:, 0:N].rearrange("p (e c) -> p e c", e=E)
                link(v.tensor_tensor(tv, tv, exs[:, 2, :].unsqueeze(2).to_broadcast([P, E, C]), ALU.add))
                link(v.tensor_tensor(tot[:, 0:N], tot[:, 0:N], M[:, 0:N], ALU.mult))
                link(v.tensor_reduce(slotf[:, 0:C], tot[:, 0:N].rearrange("p (e c) -> p c e", e=E), AX.X, ALU.add))
                link(v.tensor_copy(slot[:, g, 0:C], slotf[:, 0:C]))
                NT = TILES[L]
                link(v.tensor_tensor(cmpt[:, 0:NT, :], exs[:, 1, :].unsqueeze(1).to_broadcast([P, NT, E]),
                                     iotaT[:, 0:NT].unsqueeze(2).to_broadcast([P, NT, E]), ALU.is_le))
                link(v.tensor_reduce(eidf[:, 0:NT], cmpt[:, 0:NT, :], AX.X, ALU.add))
                v.tensor_scalar(eid[:, g * NT:(g + 1) * NT], eidf[:, 0:NT], float(E - 1), None, ALU.min).then_inc(route_done, 1)
                dve.wait_ge(route_done, 2 * L + g + 1)

            def body(L, b, u, half, prev2, prev, nxt, combos=(), squares=True):
                for j in range(J):
                    n = 4 * b + j
                    if j < 3:
                        row_max(L, n + 1, j + 1, u)
                    elif nxt:
                        row_max(L, n + 1, 0, 1 - u)
                    row_scale(L, n, j, u)
                    if L == 1:
                        if j > 0:
                            attn_out(n - 1, j - 1, u)
                        elif prev:
                            attn_out(n - 1, 3, 1 - u)
                    if j == 0:
                        if prev2:
                            router_out(L, b - 2)
                        if nxt:
                            ln1(L, b + 1, 1 - u)
                    if j == 1 and prev:
                        if L == 0:
                            y_out(b - 1)
                        post(L, b - 1, 1 - u, half)
                    if j == 2 and nxt and L == 1:
                        values_out(b + 1, 1 - u)
                    if j == 3 and prev and L == 0 and squares:
                        sum_squares(b - 1, 1 - u)
                    for c in combos[j:j + 1]:
                        for args in c:
                            combine(0, *args)

            def hidden(L, t, r):
                e = dve.value_load(eid[0:1, bass.ds(t, 1)], min_val=0, max_val=E - 1)
                dve.wait_ge(up_mm[L], BIAS + t + 1)
                dve.wait_ge(ht_mm[L], BIAS + t - 1)
                v.tensor_tensor(hu[:, r % 2, :], ps_s[:, r % 2, :], B1[:, bass.ds(e, 1), :].rearrange("p a h -> p (a h)"),
                                ALU.add).then_inc(hu_ready[L], 1)

            def expert_out(L, t, r, stores):
                e = dve.value_load(eid[0:1, bass.ds(t, 1)], min_val=0, max_val=E - 1)
                dve.wait_ge(dn_mm[L], BIAS + t + 1)
                dve.wait_ge(st[L][r], 16 + 16 * stores)
                v.tensor_tensor(yt[:, r, :], ps_o[:, r % 2, 0:D], tile(B2[L], e), ALU.add).then_inc(y_ready[L], 1)

            def quad(L, q, first=False, last=False, tiles=None):
                for r in range(4):
                    t = 4 * q + r
                    if not (last and r == 3):
                        hidden(L, t + 1, (r + 1) % 4)
                    if not (first and r == 0):
                        expert_out(L, t - 1, (r + 3) % 4, q if r else q - 1)
                    if tiles is not None:
                        combine(L, tiles, tiles * 4 + r, r, tiles * 4 + r, tiles + 1)

            dve.wait_ge(in_x0, 16)
            ln1(0, 0, 0)
            for L in (0, 1):
                setup(L)
            dve.wait_ge(in_x, 16 * (NB - 1))
            dve.wait_ge(mod_in[0], 32)
            for L in (0, 1):
                NQ, CQ = 2 * TILES[L] // 4, TILES[L] // 4 + 1
                if L == 1:
                    ln1(1, 0, 0)
                    constant_rows()
                    dve.wait_ge(mod_in[1], 32)
                    values_out(0, 0)
                row_max(L, 0, 0, 0)

                def combos(b):
                    if L == 0:
                        return ()
                    if isinstance(b, int):
                        return [[(GB + b, GT + 4 * b + r, r, GT + 4 * b + r, GB + b + 1)] for r in range(4)]
                    i, k = b[1:]
                    return [[], []] + [[(i + (GB + 1), i * 4 + (GT + 4 + r), r, i * 4 + (GT + 4 + r), i + (GB + 2))] for r in (2 * k, 2 * k + 1)]

                body(L, 0, 0, 0, False, False, True, combos(0))
                body(L, 1, 1, 0, False, True, True, combos(1))
                with dve.Fori(1, 3, 1) as i:
                    body(L, 2 * i, 0, i - 1, True, True, True, combos((None, i, 0)))
                    body(L, 2 * i + 1, 1, i, True, True, True, combos((None, i, 1)))
                route(L, 0)
                body(L, 6, 0, 2, True, True, True)
                body(L, 7, 1, 3, True, True, False, squares=False)
                if L == 1:
                    attn_out(4 * 7 + 3, 3, 1)
                router_out(L, 6)
                dve.wait_ge(in_moe[L], 16 * in_moe_all[L])
                if L == 1:
                    dve.wait_ge(in_late, 32)
                    dve.wait_ge(b2_in, 16)
                hidden(L, 0, 0)
                if L == 0:
                    y_out(7)
                post(L, 7, 1, 3)
                quad(L, 0, first=True)
                quad(L, 1)
                router_out(L, 7)
                if L == 0:
                    sum_squares(6, 0)
                    sum_squares(7, 1)
                quad(L, 2)
                route(L, 1)
                with dve.Fori(3, CQ, 1) as q:
                    quad(L, q)
                with dve.Fori(CQ, min(CQ + 4, NQ - 1), 1) as q:
                    quad(L, q, tiles=q - CQ)
                if CQ + 4 < NQ - 1:
                    with dve.Fori(CQ + 4, NQ - 1, 1) as q:
                        quad(L, q)
                quad(L, NQ - 1, last=True)
                expert_out(L, 4 * NQ - 1, 3, NQ - 1)
            with dve.Fori(0, 4, 1) as i:
                for r in range(4):
                    combine(1, i + GB, i * 4 + (GT + r), r, i * 4 + (GT + r), i + (GB + 1))


_INS = ['L0_attn_q', 'L0_attn_wq', 'L0_attn_wk', 'L0_attn_wv', 'L0_attn_wo', 'L0_ffn_uzman_embeddings', 'L0_ffn_W1',
        'L0_ffn_b1', 'L0_ffn_W2', 'L0_ffn_b2', 'L0_ffn_onbellek_durumu', 'L0_c', 'L0_wmod', 'L1_attn_W_qkv', 'L1_ffn_W1',
        'L1_ffn_b1', 'L1_ffn_W2', 'L1_ffn_b2', 'L1_ffn_Wr', 'L1_ffn_br', 'L1_c', 'L1_wmod']
_OUTS = [((8, 512, 128), 'float32')]


def kernel(**inputs):
    import numpy as _np
    import concourse.bacc as _bacc
    from concourse import mybir as _mybir
    from concourse.bass_utils import run_bass_kernel_spmd as _run

    nc = _bacc.Bacc("TRN2", target_bir_lowering=False, num_devices=1)
    arrays, args = {}, []
    for name in _INS:
        a = _np.ascontiguousarray(inputs[name])
        arrays[f"in_{name}_dram"] = a
        args.append(nc.dram_tensor(f"in_{name}_dram", a.shape, _mybir.dt.from_np(a.dtype), kind="ExternalInput").ap())
    for i, (shape, dtype) in enumerate(_OUTS):
        dt = _mybir.dt.from_np(_np.dtype(dtype))
        args.append(nc.dram_tensor(f"out_{i}_dram", shape, dt, kind="ExternalOutput").ap())
    adaln_kernel(nc, *args)
    r = _run(nc, [arrays], core_ids=[0])
    return r.results[0]["out_0_dram"]
```

```python
from contextlib import ExitStack

import concourse.bass as bass
from concourse import mybir

P = 128
F32 = mybir.dt.float32
BF16 = mybir.dt.bfloat16
I32 = mybir.dt.int32
ALU = mybir.AluOpType
ACT = mybir.ActivationFunctionType
AX = mybir.AxisListType

NB = 8
S = 512
D = 128
J = S // P
E = 8
HID = 512
HC = HID // P
GB = NB // 2
GT = GB * J
TOPK = [2, 1]
NR = [2 * E, E]
TILES = [k * GT + E for k in TOPK]
BIAS = 4
SP, PE, Activation, DVE = (mybir.EngineType.SP, mybir.EngineType.PE, mybir.EngineType.Activation, mybir.EngineType.DVE)
LN_EPS = 1e-5
NORM_EPS = 1e-8
CACHE_BONUS = 0.1
BIG = 3.0e38
LN_STEPS = 4 + 4 + 2 + 9
MAGIC = 0x5F3759DF


def adaln_kernel(nc, L0_attn_q, L0_attn_wq, L0_attn_wk, L0_attn_wv, L0_attn_wo,
                 L0_ffn_uzman_embeddings, L0_ffn_W1, L0_ffn_b1, L0_ffn_W2, L0_ffn_b2,
                 L0_ffn_onbellek_durumu, L0_c, L0_wmod, L1_attn_W_qkv, L1_ffn_W1, L1_ffn_b1,
                 L1_ffn_W2, L1_ffn_b2, L1_ffn_Wr, L1_ffn_br, L1_c, L1_wmod, out):
    W1_D, W2_D = [L0_ffn_W1, L1_ffn_W1], [L0_ffn_W2, L1_ffn_W2]
    B1_D, B2_D = [L0_ffn_b1, L1_ffn_b1], [L0_ffn_b2, L1_ffn_b2]
    C_D, WMOD_D = [L0_c, L1_c], [L0_wmod, L1_wmod]
    SCALE = [(D / 16) ** -0.5, D ** -0.5]

    xs_d = [nc.dram_tensor(f"xs_scratch{g}", (TILES[0] * P, D), F32, kind="Internal").ap() for g in (0, 1)]
    ys_d = [[nc.dram_tensor(f"ys_scratch{L}{g}", (TILES[L] * P, D), F32, kind="Internal").ap() for g in (0, 1)]
            for L in (0, 1)]
    mod_d = [nc.dram_tensor(f"mod_scratch{L}", (NB, 4 * D), F32, kind="Internal").ap() for L in (0, 1)]
    b2_d = nc.dram_tensor("b2_scratch", (1, E * D), F32, kind="Internal").ap()

    ctx = ExitStack()
    with ctx:
        def sb(name, shape, dt=F32):
            return ctx.enter_context(nc.sbuf_tensor(name, shape, dt))

        def sem(name):
            return ctx.enter_context(nc.semaphore(name))

        def sem2(name):
            return [sem(f"{name}_{L}") for L in (0, 1)]

        ps_a = ctx.enter_context(nc.psum_tensor("ps_a", [P, 512], F32))
        ps_b = ctx.enter_context(nc.psum_tensor("ps_b", [P, 512], F32))
        ps_s = ctx.enter_context(nc.psum_tensor("ps_s", [P, 2, 512], F32))
        ps_p = ctx.enter_context(nc.psum_tensor("ps_p", [P, 2, 512], F32))
        ps_o = ctx.enter_context(nc.psum_tensor("ps_o", [P, 2, 512], F32))

        X = sb("X", [P, NB * J, D])
        W1 = sb("W1", [P, 4, HID])
        W2 = [sb(f"W2_{L}", [P, E, HC, D]) for L in (0, 1)]
        B2 = [sb(f"B2_{L}", [P, E, D]) for L in (0, 1)]
        MB = sb("MB", [P, NB, 3, D])
        GBB = [sb(f"GBB_{L}", [P, NB, D]) for L in (0, 1)]
        H = sb("H", [P, NB * J, D])
        Hc = sb("Hc", [P, 2, J, D])
        xn = sb("xn", [P, 2, J, D])
        hT = sb("hT", [P, 2, S])
        gT = sb("gT", [P, 2, S])
        V = sb("V", [P, 2, J, D])
        prob = sb("prob", [P, 2, S])
        probT = sb("probT", [P, 2, J, P])
        hT2 = sb("hT2", [P, S])
        sq = sb("sq", [P, 2, J, D])
        xt = sb("xt", [P, 4, D])
        xT = sb("xT", [P, 2, P])
        hTm = sb("hTm", [P, 2, HC, P])
        yt = sb("yt", [P, 4, D])
        yg = sb("yg", [P, 4, 2, D])
        On = yg[:, :, 0, :]
        acc = sb("acc", [P, 2, D])
        A = [sb(f"A_{L}", [P, D]) for L in (0, 1)]
        WvT = [sb(f"WvT_{L}", [P, D]) for L in (0, 1)]
        woT = sb("woT", [P, D])
        woG = sb("woG", [P, 2, D])
        RW = [sb(f"RW_{L}", [P, NR[L]]) for L in (0, 1)]
        caT = [sb(f"caT_{L}", [P, NB]) for L in (0, 1)]
        saT = [sb(f"saT_{L}", [P, NB]) for L in (0, 1)]
        ident = sb("ident", [P, P])
        upper = sb("upper", [P, P], BF16)
        ones = sb("ones", [P, P], BF16)
        rev8 = sb("rev8", [P, E])
        up8 = sb("up8", [P, E])
        thr16 = sb("thr16", [P, GT])
        iotaT = sb("iotaT", [P, TILES[0]])
        NC = [k * GT for k in TOPK]
        keep = [sb(f"keep_{L}", [P, E * NC[L]]) for L in (0, 1)]
        onesf = sb("onesf", [P, E])
        bonus = sb("bonus", [P, E])
        brB = sb("brB", [P, E])
        st1, st2 = sb("st1", [P, J, 6]), sb("st2", [P, J, 6])
        mv1, mv2 = sb("mv1", [P, J, 2]), sb("mv2", [P, J, 2])
        nt1, nt2 = sb("nt1", [P, 3, J]), sb("nt2", [P, 3, J])
        rs1, rs2 = sb("rs1", [P, 2, J]), sb("rs2", [P, 2, J])
        nb1, nb2 = sb("nb1", [P, 2, J]), sb("nb2", [P, 2, J])
        negm = sb("negm", [P, 8])
        rowsum = sb("rowsum", [P, 8])
        rinv = sb("rinv", [P, 8])
        sims = sb("sims", [P, GT * 2, NR[0]])
        sumsq = sb("sumsq", [P, GT * 2])
        score = sb("score", [P, GT, E])
        rtmp = sb("rtmp", [P, GT, E])
        cmpt = sb("cmpt", [P, TILES[0], E])
        M = sb("M", [P, E * NC[0]])
        Mb = sb("Mb", [P, E * NC[0]], BF16)
        cum = sb("cum", [P, E * NC[0]])
        tot = sb("tot", [P, E * NC[0]])
        row = sb("row", [P, 8, GT])
        exs = sb("exs", [P, 3, E])
        slotf = sb("slotf", [P, 2 * GT])
        slot = sb("slot", [P, 2, 2 * GT], I32)
        weight = sb("weight", [P, 2, NB * J])
        eidf = sb("eidf", [P, TILES[0]])
        eid = sb("eid", [P, 2 * TILES[0]], I32)
        cur = sb("cur", [P, 4, 2], I32)
        crow = sb("crow", [NB, 4, D])
        scT = sb("scT", [P, NB])
        wsm = [W1[:, 0, n * D:(n + 1) * D] for n in range(4)]
        csrow = sb("csrow", [NB, 2, D])
        erow = sb("erow", [E, 2, D])
        nte = sb("nte", [E, 8])
        wmod = [MB[:, 0:2, :, :].rearrange("p a b d -> p (a b d)"),
                prob[:, :, :].rearrange("p a s -> p (a s)")[:, 0:6 * D]]
        b1row = [yt[0:E * HC, L, :] for L in (0, 1)]
        b1T = [sb(f"b1T_{L}", [P, E * HC]) for L in (0, 1)]
        relu_b1 = sb("relu_b1", [P, E * HC])
        rrow = sb("rrow", [1, 2 * D])

        in_small = sem2("in_small")
        in_x0, in_x = sem("in_x0"), sem("in_x")
        in_moe = sem2("in_moe")
        consts = sem("consts")
        passed = sem("passed")
        s_act, s_pe, s_dve = sem("setup_act"), sem("setup_pe"), sem("setup_dve")
        rows_ready = sem("rows_ready")
        mod_out, mod_in = sem2("mod_out"), sem2("mod_in")
        b2_out, b2_in = sem("b2_out"), sem("b2_in")
        xs_zero = sem("xs_zero")
        chain = sem("dve_chain")
        pool_chain = sem("pool_chain")
        ln1_ready = sem2("ln1_ready")
        xn_ready = sem2("xn_ready")
        xn_chain = sem2("xn_chain")
        h_tr = sem2("h_tr")
        hT_ready = sem2("hT_ready")
        g_mm = sem2("g_mm")
        gT_ready = sem2("gT_ready")
        v_mm = sem2("v_mm")
        v_ready = sem2("v_ready")
        s_mm = sem2("s_mm")
        negm_ready = sem2("negm_ready")
        exp_done = sem2("exp_done")
        rinv_ready = sem2("rinv_ready")
        pt_mm = sem2("pt_mm")
        pt_ready = sem2("pt_ready")
        pv_mm = sem2("pv_mm")
        o_done = sem2("o_done")
        wog_ready = sem("wog_ready")
        y_mm = sem("y_mm")
        y_add = sem("y_add")
        hc_ready = sem2("hc_ready")
        hkeep = [[sem(f"hkeep_{L}_{u}") for u in (0, 1)] for L in (0, 1)]
        p_tr = sem2("p_tr")
        hT2_ready = sem2("hT2_ready")
        r_mm = sem2("r_mm")
        r_ready = sem2("r_ready")
        sq_ready = sem("sq_ready")
        sq_used = sem("sq_used")
        ln1_chain, ln2_chain = sem2("ln1_chain"), sem2("ln2_chain")
        hc_chain = sem2("hc_chain")
        m_ready, rank_mm, rank_read, route_done = sem("m_ready"), sem("rank_mm"), sem("rank_read"), sem("route_done")
        gap_ready, gap_exp = sem("gap_ready"), sem("gap_exp")
        scat = [[sem(f"scat_{L}_{g}") for g in (0, 1)] for L in (0, 1)]
        ld = [[sem(f"ld_{L}_{h}") for h in (0, 1)] for L in (0, 1)]
        w1_in = [[sem(f"w1_in_{L}_{r}") for r in range(4)] for L in (0, 1)]
        st = [[sem(f"st_{L}_{h}") for h in (0, 1)] for L in (0, 1)]
        xt_mm = sem2("xt_mm")
        xT_ready = sem2("xT_ready")
        up_mm = sem2("up_mm")
        hTm_ready = sem2("hTm_ready")
        dn_mm = sem2("dn_mm")
        y_ready = sem2("y_ready")
        gat = [[sem(f"gat_{L}_{r}") for r in range(4)] for L in (0, 1)]
        cur_ready = sem2("cur_ready")
        comb_chain = sem2("comb_chain")
        comb_done = sem2("comb_done")
        stored = sem("stored")

        paced = {
            "pe": h_tr + g_mm + v_mm + s_mm + pt_mm + pv_mm + [y_mm] + p_tr + r_mm + xt_mm + up_mm + dn_mm,
            "act": hT_ready + gT_ready + [v_ready[0]] + exp_done + pt_ready + [o_done[0]] + hT2_ready + xT_ready + hTm_ready,
            "dve": ln1_ready + [v_ready[1]] + negm_ready + rinv_ready + [o_done[1], y_add, sq_used] + hc_ready + r_ready
                   + y_ready + comb_done,
            "pool": xn_ready + [wog_ready, sq_ready],
        }

        def upto(n):
            return min(n, NB) if isinstance(n, int) else n

        def wait_apart(eng, s, value):
            eng.wait_ge(s, value)
            if not isinstance(value, int):
                eng.sem_inc(passed, 1)

        def experts(engine, q):
            return nc.values_load_multi_w_load_instructions(
                eid[0:1, bass.ds(q * 4, 4)], engines=[engine], min_val=0, max_val=E - 1,
                skip_runtime_bounds_check_because="it counts experts up to E - 1")[1]

        def bias(eng, name):
            for s in paced[name]:
                eng.sem_inc(s, BIAS)

        block = ctx.enter_context(nc.Block())

        @block.sync
        def _(sp):
            for L in (0, 1):
                for u in (0, 1):
                    sp.sem_inc(hkeep[L][u], 16)
                for h in (0, 1):
                    sp.sem_inc(st[L][h], 16)

            def load_batch(b, s):
                sp.dma_start(X[:, b * J:(b + 1) * J, :], L0_attn_q[b].rearrange("(p j) d -> p j d", j=J)).then_inc(s, 16)

            def load_mods(L):
                sp.dma_start(MB[:, :, :, :].rearrange("p b m d -> p b (m d)"),
                             mod_d[L][:, 0:3 * D].partition_broadcast(P)).then_inc(mod_in[L], 16)
                if L == 0:
                    sp.dma_start(GBB[0][:, :, :], mod_d[0][:, 3 * D:4 * D].partition_broadcast(P)).then_inc(mod_in[0], 16)

            sp.dma_start(crow[:, 0, :], C_D[0]).then_inc(in_small[0], 16)
            load_batch(0, in_x0)
            sp.dma_start(wmod[0], WMOD_D[0]).then_inc(in_small[0], 16)
            for w, src in zip(wsm, (L0_attn_wq, L0_attn_wk, L0_attn_wv, L0_attn_wo)):
                sp.dma_start(w, src).then_inc(in_small[0], 16)
            sp.dma_start(erow[:, 0, :], L0_ffn_uzman_embeddings).then_inc(in_small[0], 16)
            sp.dma_start(b1row[0], B1_D[0].rearrange("e (c p) -> (e c) p", p=P)).then_inc(in_small[0], 16)
            sp.dma_start(bonus[:, :], L0_ffn_onbellek_durumu.partition_broadcast(P)).then_inc(in_small[0], 16)
            for b in range(1, NB):
                load_batch(b, in_x)
            sp.wait_ge(rows_ready, 1)
            sp.dma_start(mod_d[0], crow[:, :, :].rearrange("b m d -> b (m d)")).then_inc(mod_out[0], 16)
            sp.wait_ge(mod_out[0], 16)
            load_mods(0)
            sp.wait_ge(mod_out[0], 16)
            sp.dma_start(crow[:, 0, :], C_D[1]).then_inc(in_small[1], 16)
            sp.dma_start(wmod[1], WMOD_D[1]).then_inc(in_small[1], 16)
            for n in range(3):
                sp.dma_start(wsm[n], L1_attn_W_qkv[n * D:(n + 1) * D, :]).then_inc(in_small[1], 16)
            sp.dma_start(RW[1][:, :], L1_ffn_Wr).then_inc(in_small[1], 16)
            sp.dma_start(brB[:, :], L1_ffn_br.partition_broadcast(P)).then_inc(in_small[1], 16)
            sp.dma_start(b1row[1], B1_D[1].rearrange("e (c p) -> (e c) p", p=P)).then_inc(in_small[1], 16)
            sp.dma_start(B2[1][0:1, :, :].rearrange("a e d -> a (e d)"), L1_ffn_b2.rearrange("(a e) d -> a (e d)", a=1)).then_inc(in_small[1], 16)
            for L in (0, 1):
                sp.dma_start(W2[L][:, :, :, :], W2_D[L].rearrange("e (c p) d -> p e c d", p=P)).then_inc(in_moe[L], 16)
                if L == 0:
                    sp.dma_start(B2[0][:, :, :].rearrange("p e d -> p (e d)"),
                                 B2_D[0].rearrange("e d -> (e d)").partition_broadcast(P)).then_inc(in_moe[0], 16)
            sp.wait_ge(rows_ready, 2)
            sp.dma_start(mod_d[1], crow[:, :, :].rearrange("b m d -> b (m d)")).then_inc(mod_out[1], 16)
            sp.wait_ge(mod_out[1], 16)
            sp.dma_start(GBB[1][:, :, :], mod_d[1][:, 3 * D:4 * D].partition_broadcast(P)).then_inc(mod_in[1], 16)
            sp.wait_ge(consts, 3)
            for g in (0, 1):
                sp.dma_start(xs_d[g].rearrange("(a p r) d -> p a (r d)", p=P, r=J),
                             H[:, 0:J, :].rearrange("p j d -> p (j d)").unsqueeze(1).to_broadcast([P, TILES[0] // J, J * D]))\
                  .then_inc(xs_zero, 16)

            def load(L, g, q, h, first=False):
                if not first:
                    sp.wait_ge(xt_mm[L], BIAS + q * 4 + (2 * h - 2))
                sp.dma_start(xt[:, 2 * h:2 * h + 2, :], rows(xs_d[g], q * 4 + (2 * h - g * TILES[L]))).then_inc(ld[L][h], 16)

            def weights(L, e, q, r, first=False):
                if not first:
                    sp.wait_ge(up_mm[L], BIAS + q * 4 + (r - 3))
                sp.dma_start(W1[:, r, :], W1_D[L][bass.ds(e, 1), :, :].rearrange("a d h -> d (a h)")).then_inc(w1_in[L][r], 16)

            def store(L, g, q, h):
                sp.wait_ge(y_ready[L], BIAS + q * 4 + (2 * h + 2))
                sp.dma_start(rows(ys_d[L][g], q * 4 + (2 * h - g * TILES[L])), yt[:, 2 * h:2 * h + 2, :]).then_inc(st[L][h], 16)

            def rows(scratch, t):
                return scratch[bass.ds(t * P, 2 * P), :].rearrange("(k p) d -> p k d", p=P)

            def fetch(L, g, q, g_a=0, g_b=0, stores=2, first=False):
                e = experts(SP, q)
                load(L, g, q, 0, first)
                weights(L, e[0], q, 0, first)
                weights(L, e[1], q, 1, first)
                if stores == 2:
                    store(L, g_a, q - 2, 1)
                load(L, g, q, 1, first)
                weights(L, e[2], q, 2, first)
                weights(L, e[3], q, 3, first)
                if stores:
                    store(L, g_b, q - 1, 0)

            def keep(L, q, u, at):
                sp.wait_ge(hc_ready[L], BIAS + q + 1)
                sp.dma_start(H[:, at, :], Hc[:, u, :, :]).then_inc(hkeep[L][u], 16)

            sp.wait_ge(xs_zero, 32)
            for L in (0, 1):
                keep(L, 0, 0, slice(0, J))
                with sp.Fori(0, 3, 1) as i:
                    keep(L, 2 * i + 1, 1, bass.ds(i * 2 * J + J, J))
                    keep(L, 2 * i + 2, 0, bass.ds(i * 2 * J + 2 * J, J))
                if L == 1:
                    sp.wait_ge(rows_ready, 3)
                    sp.dma_start(b2_d, B2[1][0:1, :, :].rearrange("p e d -> p (e d)")).then_inc(b2_out, 16)
                    sp.wait_ge(b2_out, 16)
                    sp.dma_start(B2[1][:, :, :].rearrange("p e d -> p (e d)"),
                                 b2_d.rearrange("a n -> (a n)").partition_broadcast(P)).then_inc(b2_in, 16)
                NG = TILES[L] // 4
                sp.wait_ge(route_done, 2 * L + 1)
                sp.wait_ge(scat[L][0], 16 * TOPK[L] * GT)
                fetch(L, 0, 0, stores=0, first=True)
                keep(L, 7, 1, slice(7 * J, 8 * J))
                if L == 0:
                    sp.wait_ge(wog_ready, BIAS + NB)
                    load_mods(1)
                fetch(L, 0, 1, stores=1)
                with sp.Fori(2, NG, 1) as q:
                    fetch(L, 0, q)
                sp.wait_ge(route_done, 2 * L + 2)
                sp.wait_ge(scat[L][1], 16 * TOPK[L] * GT)
                fetch(L, 1, NG)
                fetch(L, 1, NG + 1, 0, 1)
                with sp.Fori(NG + 2, 2 * NG, 1) as q:
                    fetch(L, 1, q, 1, 1)
                store(L, 1, 2 * NG - 2, 1)
                store(L, 1, 2 * NG - 1, 0)
                store(L, 1, 2 * NG - 1, 1)
            for b in range(NB):
                sp.wait_ge(comb_done[1], BIAS + (b + 1) * J)
                sp.dma_start(out[b].rearrange("(p j) d -> p j d", j=J), X[:, b * J:(b + 1) * J, :]).then_inc(stored, 16)
            sp.wait_ge(stored, 16 * NB)


        N_SMALL = [9, 9]
        in_moe_all = [2, 1]

        @block.tensor
        def _(pe):
            bias(pe, "pe")
            mm, tr = nc.tensor.matmul, nc.tensor.transpose

            def setup(L):
                d = 16 * L
                pe.wait_ge(in_small[L], 16 * N_SMALL[L])
                pe.wait_ge(consts, 3)
                base = [0, 5][L]
                if L == 1:
                    pe.wait_ge(s_dve, base)
                mm(ps_p[:, 0, 0:D], wsm[0], wsm[1], start=True, stop=True)
                tr(ps_p[:, 1, 0:D], wsm[2], ident[:, :])
                if L == 0:
                    tr(ps_p[:, 1, D:2 * D], wsm[3], ident[:, :])
                    tr(ps_p[:, 1, 3 * D:3 * D + E * HC], b1row[0], ident[0:E * HC, 0:E * HC])
                    pe.wait_ge(s_dve, 1)
                    tr(ps_p[:, 1, 2 * D:2 * D + E], erow[:, 0, :], ident[0:E, 0:E])
                    tr(ps_p[:, 1, 2 * D + E:2 * D + 2 * E], erow[:, 1, :], ident[0:E, 0:E]).then_inc(s_pe, 1)
                else:
                    tr(ps_p[:, 1, 3 * D:3 * D + E * HC], b1row[1], ident[0:E * HC, 0:E * HC]).then_inc(s_pe, 1)
                pe.wait_ge(s_dve, base + 2 - L)
                tr(ps_a[:, 0:NB], crow[:, 2, :], ident[0:NB, 0:NB]).then_inc(s_pe, 1)
                pe.wait_ge(s_dve, base + 3 - L)
                mm(ps_s[0:NB, 0, 0:3 * D], scT[:, :], wmod[L][:, 0:3 * D], start=True, stop=True)
                mm(ps_s[0:NB, 1, 0:3 * D], scT[:, :], wmod[L][:, 3 * D:6 * D], start=True, stop=True).then_inc(s_pe, 1)
                pe.wait_ge(s_dve, base + 4 - L)
                tr(ps_a[:, 0:NB], csrow[:, 0, :], ident[0:NB, 0:NB])
                tr(ps_a[:, NB:2 * NB], csrow[:, 1, :], ident[0:NB, 0:NB]).then_inc(s_pe, 1)

            def constant_rows():
                pe.wait_ge(in_moe[1], 16)
                for e in range(E):
                    for c in range(HC):
                        last = mm(ps_o[0:1, e // 4, (e % 4) * D:(e % 4 + 1) * D], relu_b1[:, e * HC + c:e * HC + c + 1],
                                  W2[1][:, e, c, :], start=(c == 0), stop=(c == HC - 1))
                last.then_inc(s_pe, 1)

            def head(L, b, u):
                pe.wait_ge(xn_ready[L], BIAS + b + 1)
                pe.wait_ge(hT2_ready[L], BIAS + b - 2)
                for j in range(J):
                    last = tr(ps_a[:, j * P:(j + 1) * P], xn[:, u, j, :], ident[:, :])
                last.then_inc(h_tr[L], 1)
                pe.wait_ge(hT_ready[L], BIAS + b + 1)
                pe.wait_ge(r_ready[L], BIAS + b - 2)
                if L == 0:
                    pe.wait_ge(y_add, BIAS + b - 1)
                mm(ps_b[:, :], A[L][:, :], hT[:, u, :], start=True, stop=True).then_inc(g_mm[L], 1)
                for j in range(J):
                    last = mm(ps_a[:, j * P:(j + 1) * P], hT[:, u, j * P:(j + 1) * P], WvT[L][:, :], start=True, stop=True)
                last.then_inc(v_mm[L], 1)

            def scores(L, n, b, u, j):
                if j == 0:
                    pe.wait_ge(gT_ready[L], BIAS + b + 1)
                pe.wait_ge(exp_done[L], BIAS + n - 1)
                mm(ps_s[:, j % 2, :], gT[:, u, j * P:(j + 1) * P], hT[:, u, :], start=True, stop=True).then_inc(s_mm[L], 1)

            def prob_tr(L, n, j):
                pe.wait_ge(exp_done[L], BIAS + n + 1)
                pe.wait_ge(pt_ready[L], BIAS + n - 1)
                for c in range(J):
                    last = tr(ps_p[:, j % 2, c * P:(c + 1) * P], prob[:, j % 2, c * P:(c + 1) * P], ident[:, :])
                last.then_inc(pt_mm[L], 1)

            def prob_v(L, n, u, j):
                pe.wait_ge(pt_ready[L], BIAS + n + 1)
                pe.wait_ge(o_done[L], BIAS + n - 1)
                for c in range(J):
                    last = mm(ps_o[:, j % 2, 0:D], probT[:, j % 2, c, :], V[:, u, c, :], start=(c == 0), stop=(c == J - 1))
                last.then_inc(pv_mm[L], 1)

            def out_proj(b, u):
                pe.wait_ge(o_done[0], BIAS + 4 * b + 4)
                pe.wait_ge(wog_ready, BIAS + b + 1)
                pe.wait_ge(r_ready[0], BIAS + b)
                pe.wait_ge(gT_ready[0], BIAS + upto(b + 2))
                for j in range(J):
                    last = mm(ps_b[:, j * P:(j + 1) * P], On[:, j, :], woG[:, u, :], start=True, stop=True)
                last.then_inc(y_mm, 1)

            def post_tr(L, q, u, last_v):
                pe.wait_ge(hc_ready[L], BIAS + q + 1)
                pe.wait_ge(v_ready[L], BIAS + last_v)
                for j in range(J):
                    last = tr(ps_a[:, j * P:(j + 1) * P], Hc[:, u, j, :], ident[:, :])
                last.then_inc(p_tr[L], 1)

            def router(L, q):
                pe.wait_ge(hT2_ready[L], BIAS + q + 1)
                pe.wait_ge(gT_ready[L], BIAS + upto(q + 3))
                if L == 0:
                    pe.wait_ge(y_add, BIAS + q + 1)
                w = NR[L]
                for j in range(J):
                    last = mm(ps_b[:, j * w:(j + 1) * w], hT2[:, j * P:(j + 1) * P], RW[L][:, :], start=True, stop=True)
                last.then_inc(r_mm[L], 1)

            def ranks(L, g):
                c = TOPK[L] * GT
                pe.wait_ge(m_ready, 2 * L + g + 1)
                pe.wait_ge(gT_ready[L], BIAS + (NB - 1 if g == 0 else NB))
                mm(ps_b[:, 0:E * c], upper[:, :], Mb[:, 0:E * c], start=True, stop=True)
                last = mm(ps_b[:, E * c:2 * E * c], ones[:, :], Mb[:, 0:E * c], start=True, stop=True)
                last.then_inc(rank_mm, 1)

            def body(L, b, u, prev2, prev, nxt, rank=0):
                for j in range(J):
                    n = 4 * b + j
                    if j < 3:
                        scores(L, n + 1, b, u, j + 1)
                    elif nxt:
                        scores(L, n + 1, b + 1, 1 - u, 0)
                    prob_tr(L, n, j)
                    if j == 1 and prev and L == 0:
                        out_proj(b - 1, 1 - u)
                    if j > 0:
                        prob_v(L, n - 1, u, j - 1)
                    elif prev:
                        prob_v(L, n - 1, 1 - u, 3)
                    if j == 0 and rank:
                        pe.wait_ge(rank_read, rank)
                    if j == 0 and prev2:
                        router(L, b - 2)
                    if j == 2 and nxt:
                        head(L, b + 1, 1 - u)
                    if j == 3 and prev:
                        post_tr(L, b - 1, 1 - u, b + 2 if nxt else NB)

            def x_tr(L, q, r):
                if r % 2 == 0:
                    pe.wait_ge(ld[L][r // 2], (q + 1) * 16)
                pe.wait_ge(xT_ready[L], BIAS + q * 4 + r)
                tr(ps_a[:, 0:P], xt[:, r, :], ident[:, :]).then_inc(xt_mm[L], 1)

            def up(L, q, r):
                pe.wait_ge(w1_in[L][r], (q + 1) * 16)
                pe.wait_ge(xT_ready[L], BIAS + q * 4 + (r + 1))
                pe.wait_ge(hTm_ready[L], BIAS + q * 4 + (r - 1))
                for c in range(HC):
                    last = mm(ps_s[:, r % 2, c * P:(c + 1) * P], W1[:, r, c * P:(c + 1) * P], xT[:, r % 2, :], start=True, stop=True)
                last.then_inc(up_mm[L], 1)

            def down(L, q, r, e):
                pe.wait_ge(hTm_ready[L], BIAS + q * 4 + (r + 1))
                pe.wait_ge(y_ready[L], BIAS + q * 4 + (r - 1))
                for c in range(HC):
                    last = mm(ps_o[:, r % 2, 0:D], hTm[:, r % 2, c, :],
                              W2[L][:, bass.ds(e, 1), c, :].rearrange("p a d -> p (a d)"), start=(c == 0), stop=(c == HC - 1))
                last.then_inc(dn_mm[L], 1)

            def quad(L, q, last=False):
                e = experts(PE, q)
                for r in range(4):
                    if not (last and r >= 2):
                        x_tr(L, q + (r + 2) // 4, (r + 2) % 4)
                    if not (last and r == 3):
                        up(L, q + (r + 1) // 4, (r + 1) % 4)
                    down(L, q, r, e[r])

            for L in (0, 1):
                setup(L)
            pe.wait_ge(s_dve, 10)
            for L in (0, 1):
                NG = TILES[L] // 4
                if L == 1:
                    pe.wait_ge(y_ready[0], BIAS + 2 * TILES[0])
                    constant_rows()
                head(L, 0, 0)
                scores(L, 0, 0, 0, 0)
                if L == 1:
                    pe.wait_ge(rows_ready, 3)
                body(L, 0, 0, False, False, True)
                body(L, 1, 1, False, True, True)
                with pe.Fori(1, 3, 1) as i:
                    body(L, 2 * i, 0, True, True, True)
                    body(L, 2 * i + 1, 1, True, True, True)
                ranks(L, 0)
                body(L, 6, 0, True, True, True, rank=2 * L + 1)
                body(L, 7, 1, True, True, False)
                prob_v(L, 4 * 7 + 3, 1, 3)
                router(L, 6)
                pe.wait_ge(in_moe[L], 16 * in_moe_all[L])
                pe.wait_ge(hT2_ready[L], BIAS + NB - 1)
                pe.wait_ge(exp_done[L], BIAS + NB * J)
                pe.wait_ge(route_done, 2 * L + 1)
                x_tr(L, 0, 0)
                x_tr(L, 0, 1)
                up(L, 0, 0)
                if L == 0:
                    out_proj(7, 1)
                pe.wait_ge(o_done[L], BIAS + NB * J)
                quad(L, 0)
                pe.wait_ge(xT_ready[L], BIAS + 6)
                post_tr(L, 7, 1, NB)
                pe.wait_ge(hT2_ready[L], BIAS + NB)
                quad(L, 1)
                router(L, 7)
                quad(L, 2)
                ranks(L, 1)
                with pe.Fori(3, NG, 1) as q:
                    quad(L, q)
                pe.wait_ge(route_done, 2 * L + 2)
                with pe.Fori(NG, 2 * NG - 1, 1) as q:
                    quad(L, q)
                quad(L, 2 * NG - 1, last=True)

        @block.gpsimd
        def _(pool):
            bias(pool, "pool")
            g = nc.gpsimd
            steps = [0]

            def link(ins):
                steps[0] += 1
                ins.then_inc(pool_chain, 1)
                pool.wait_ge(pool_chain, steps[0])

            g.memset(H[:, 0:J, :], 0.0).then_inc(consts, 1)
            link(g.memset(ident[:, :], 0.0))
            link(g.affine_select(out=ident[:, :], in_=ident[:, :], compare_op=ALU.not_equal, fill=1.0, base=0,
                                 pattern=[[-1, P]], channel_multiplier=1))
            link(g.memset(ones[:, :], 1.0))
            link(g.affine_select(out=upper[:, :], in_=ones[:, :], compare_op=ALU.is_gt, fill=0.0, base=0,
                                 pattern=[[1, P]], channel_multiplier=-1))
            kw = dict(channel_multiplier=0, allow_small_or_imprecise_dtypes=True)
            link(g.iota(rev8[:, :], pattern=[[-1, E]], base=E, **kw))
            link(g.iota(up8[:, :], pattern=[[1, E]], base=1, **kw))
            link(g.iota(thr16[:, :], pattern=[[P, GT]], base=0, **kw))
            link(g.iota(iotaT[:, :], pattern=[[1, TILES[0]]], base=0, **kw))
            link(g.memset(onesf[:, :], 1.0))
            for L in (0, 1):
                link(g.memset(keep[L][:, :], 1.0))
                last = g.memset(keep[L][:, :].rearrange("p (e c) -> p e c", e=E)[:, :, 0:1], 0.0)
                last.then_inc(consts, 1)

            def normalise(L, b, u):
                pool.wait_ge(ln1_ready[L], BIAS + b + 1)
                pool.wait_ge(h_tr[L], BIAS + b - 1)
                def wide(stat):
                    return stat[:, u, :].unsqueeze(2).to_broadcast([P, J, D])

                g.tensor_tensor(xn[:, u, :, :], X[:, bass.ds(b * J, J), :], wide(rs1), ALU.mult).then_inc(xn_chain[L], 1)
                pool.wait_ge(xn_chain[L], b + 1)
                g.tensor_tensor(xn[:, u, :, :], xn[:, u, :, :], wide(nb1), ALU.add).then_inc(xn_ready[L], 1)

            def scale_wo(b, u):
                pool.wait_ge(y_mm, BIAS + b - 1)
                g.tensor_tensor(woG[:, u, :], woT[:, :], MB[:, bass.ds(b, 1), 0, :].rearrange("p a d -> p (a d)"),
                                ALU.mult).then_inc(wog_ready, 1)

            def squares(q, u):
                pool.wait_ge(hc_ready[0], BIAS + q + 1)
                pool.wait_ge(sq_used, BIAS + q - 1)
                g.tensor_tensor(sq[:, u, :, :], Hc[:, u, :, :], Hc[:, u, :, :], ALU.mult).then_inc(sq_ready, 1)

            def body(L, b, u, prev, nxt):
                if nxt:
                    normalise(L, b + 1, 1 - u)
                if L == 0:
                    scale_wo(b, u)
                    if prev:
                        squares(b - 1, 1 - u)

            def scatter(L, grp):
                pool.wait_ge(route_done, 2 * L + grp + 1)
                for u in (0, 1):
                    pool.wait_ge(hkeep[L][u], 16 + 16 * (GB // 2) * (grp + 1))
                if L == 0 and grp == 0:
                    pool.wait_ge(xs_zero, 32)
                for c in range(TOPK[L] * GT):
                    g.indirect_dma_start(out=xs_d[grp], out_offset=bass.IndirectOffsetOnAxis(ap=slot[:, grp, c:c + 1], axis=0),
                                         in_=H[:, grp * GT + c % GT, :], in_offset=None).then_inc(scat[L][grp], 16)

            def gather(L, grp, i, r, count):
                pool.wait_ge(comb_done[L], BIAS + count - 3)
                for k in range(TOPK[L]):
                    last = g.tensor_copy(cur[:, r, k:k + 1], slot[:, grp, bass.ds(i + k * GT, 1)])
                    last.then_inc(cur_ready[L], 1)
                wait_apart(pool, cur_ready[L], TOPK[L] * (count + 1))
                for k in range(TOPK[L]):
                    g.indirect_dma_start(out=yg[:, r, k, :], out_offset=None, in_=ys_d[L][grp],
                                         in_offset=bass.IndirectOffsetOnAxis(ap=cur[:, r, k:k + 1], axis=0)).then_inc(gat[L][r], 16)

            def stored_rows(L, grp):
                for h in (0, 1):
                    pool.wait_ge(st[L][h], 16 + 16 * (TILES[L] // 4) * (grp + 1))

            def gathers(L, grp):
                stored_rows(L, grp)
                with pool.Fori(0, GT // 4, 1) as q:
                    for r in range(4):
                        gather(L, grp, q * 4 + r, r, q * 4 + (r + grp * GT))

            pool.wait_ge(in_x0, 16)
            normalise(0, 0, 0)
            pool.wait_ge(mod_in[0], 32)
            pool.wait_ge(s_dve, 5)
            for L in (0, 1):
                if L == 1:
                    stored_rows(0, 1)
                    for r in range(4):
                        gather(0, 1, r, r, GT + r)
                    normalise(1, 0, 0)
                body(L, 0, 0, False, True)
                if L == 1:
                    for r in range(4):
                        gather(0, 1, 4 + r, r, GT + 4 + r)
                body(L, 1, 1, True, True)
                with pool.Fori(1, 3, 1) as i:
                    for k in (0, 1):
                        body(L, 2 * i + k, k, True, True)
                        if L == 1:
                            for r in (2 * k, 2 * k + 1):
                                gather(0, 1, i * 4 + (4 + r), r, i * 4 + (GT + 4 + r))
                body(L, 6, 0, True, True)
                if L == 0:
                    scale_wo(7, 1)
                scatter(L, 0)
                if L == 0:
                    squares(6, 0)
                    squares(7, 1)
                scatter(L, 1)
                gathers(L, 0)
                if L == 1:
                    gathers(1, 1)

        @block.scalar
        def _(act):
            bias(act, "act")
            fn = nc.scalar.activation

            def evac(out_, in_):
                return fn(out_, in_, ACT.Copy)

            def setup(L):
                act.wait_ge(in_small[L], 16 * N_SMALL[L])
                fn(crow[:, 1, :], crow[:, 0, :], ACT.Exp, scale=-1.0).then_inc(s_act, 1)

            def head(L, b, u):
                act.wait_ge(h_tr[L], BIAS + b + 1)
                src = ps_a[:, :].rearrange("p (j t) -> p j t", j=J)
                dst = hT[:, u, :].rearrange("p (t j) -> p j t", j=J) if L == 0 else hT[:, u, :].rearrange("p (j t) -> p j t", j=J)
                fn(dst, src, ACT.Identity, bias=saT[L][:, bass.ds(b, 1)], scale=caT[L][:, bass.ds(b, 1)]).then_inc(hT_ready[L], 1)
                act.wait_ge(g_mm[L], BIAS + b + 1)
                evac(gT[:, u, :], ps_b[:, :]).then_inc(gT_ready[L], 1)
                if L == 0:
                    act.wait_ge(v_mm[0], BIAS + b + 1)
                    evac(V[:, u, :, :], ps_a[:, :].rearrange("p (j d) -> p j d", j=J)).then_inc(v_ready[0], 1)

            def exps(L, n, j, u):
                act.wait_ge(negm_ready[L], BIAS + n + 1)
                act.wait_ge(pt_mm[L], BIAS + n - 1)
                k = 4 * u + j
                fn(prob[:, j % 2, :], ps_s[:, j % 2, :], ACT.Exp, bias=negm[:, k:k + 1],
                   accum_out=rowsum[:, k:k + 1]).then_inc(exp_done[L], 1)

            def prob_out(L, n, j):
                act.wait_ge(pt_mm[L], BIAS + n + 1)
                act.wait_ge(pv_mm[L], BIAS + n - 1)
                evac(probT[:, j % 2, :, :], ps_p[:, j % 2, :].rearrange("p (c q) -> p c q", c=J)).then_inc(pt_ready[L], 1)

            def attn_out(n, j, u, b):
                act.wait_ge(pv_mm[0], BIAS + n + 1)
                act.wait_ge(rinv_ready[0], BIAS + n + 1)
                if j == 0:
                    act.wait_ge(y_mm, BIAS + b)
                fn(On[:, j, :], ps_o[:, j % 2, 0:D], ACT.Copy, scale=rinv[:, 4 * u + j:4 * u + j + 1]).then_inc(o_done[0], 1)

            def post(L, q):
                act.wait_ge(p_tr[L], BIAS + q + 1)
                act.wait_ge(r_mm[L], BIAS + q)
                evac(hT2[:, :], ps_a[:, :]).then_inc(hT2_ready[L], 1)

            def body(L, b, u, prev, nxt):
                for j in range(J):
                    n = 4 * b + j
                    if j < 3:
                        exps(L, n + 1, j + 1, u)
                    elif nxt:
                        exps(L, n + 1, 0, 1 - u)
                    prob_out(L, n, j)
                    if L == 0:
                        if j > 0:
                            attn_out(n - 1, j - 1, u, b)
                        elif prev:
                            attn_out(n - 1, 3, 1 - u, b - 1)
                    if j == 2 and nxt:
                        head(L, b + 1, 1 - u)
                    if j == 3 and prev:
                        post(L, b - 1)

            def x_out(L, q, r):
                act.wait_ge(xt_mm[L], BIAS + q * 4 + (r + 1))
                act.wait_ge(up_mm[L], BIAS + q * 4 + (r - 1))
                evac(xT[:, r % 2, :], ps_a[:, 0:P]).then_inc(xT_ready[L], 1)

            def hidden(L, q, r, e):
                act.wait_ge(up_mm[L], BIAS + q * 4 + (r + 1))
                act.wait_ge(dn_mm[L], BIAS + q * 4 + (r - 1))
                for c in range(HC):
                    last = fn(hTm[:, r % 2, c, :], ps_s[:, r % 2, c * P:(c + 1) * P], ACT.Gelu if L == 0 else ACT.Relu,
                              bias=b1T[L][:, bass.ds(e * HC + c, 1)])
                last.then_inc(hTm_ready[L], 1)

            def quad(L, q, last=False):
                e = experts(Activation, q)
                for r in range(4):
                    hidden(L, q, r, e[r])
                    if not (last and r >= 2):
                        x_out(L, q + (r + 2) // 4, (r + 2) % 4)

            def top2_exp(g):
                act.wait_ge(gap_ready, g + 1)
                fn(row[:, 5, :], row[:, 4, :], ACT.Exp).then_inc(gap_exp, 1)

            for L in (0, 1):
                setup(L)
            for L in (0, 1):
                act.wait_ge(s_dve, [5, 10][L])
                head(L, 0, 0)
                exps(L, 0, 0, 0)
                body(L, 0, 0, False, True)
                body(L, 1, 1, True, True)
                with act.Fori(1, 3, 1) as i:
                    body(L, 2 * i, 0, True, True)
                    body(L, 2 * i + 1, 1, True, True)
                if L == 0:
                    top2_exp(0)
                body(L, 6, 0, True, True)
                body(L, 7, 1, True, False)
                if L == 0:
                    attn_out(4 * 7 + 3, 3, 1, 7)
                act.wait_ge(route_done, 2 * L + 1)
                x_out(L, 0, 0)
                x_out(L, 0, 1)
                quad(L, 0)
                post(L, 7)
                quad(L, 1)
                quad(L, 2)
                if L == 0:
                    top2_exp(1)
                NG = TILES[L] // 4
                with act.Fori(3, NG, 1) as q:
                    quad(L, q)
                act.wait_ge(route_done, 2 * L + 2)
                with act.Fori(NG, 2 * NG - 1, 1) as q:
                    quad(L, q)
                quad(L, 2 * NG - 1, last=True)

        @block.vector
        def _(dve):
            bias(dve, "dve")
            v = nc.vector
            steps = [0]

            def link(ins):
                steps[0] += 1
                ins.then_inc(chain, 1)
                dve.wait_ge(chain, steps[0])

            def rsqrt(x, y, t, out_, step):
                step(v.tensor_scalar(y.bitcast(I32), x.bitcast(I32), -0.5, float(MAGIC), ALU.mult, ALU.add))
                for k in range(3):
                    step(v.tensor_tensor(t, y, y, ALU.mult))
                    step(v.scalar_tensor_tensor(t, t, -0.5, x, ALU.mult, ALU.mult))
                    step(v.scalar_tensor_tensor(out_ if k == 2 else y, t, 1.5, y, ALU.add, ALU.mult))

            def setup(L):
                pe0, d0 = [0, 4][L], [0, 5][L]
                dve.wait_ge(in_small[L], 16 * N_SMALL[L])
                if L == 0:
                    link(v.tensor_tensor(erow[:, 1, :], erow[:, 0, :], erow[:, 0, :], ALU.mult))
                    link(v.tensor_reduce(nte[:, 0:1], erow[:, 1, :], AX.X, ALU.add))
                    rsqrt(nte[:, 0:1], nte[:, 1:2], nte[:, 2:3], nte[:, 3:4], link)
                    link(v.tensor_tensor(nte[:, 4:5], nte[:, 3:4], nte[:, 0:1], ALU.mult))
                    link(v.tensor_scalar(nte[:, 5:6], nte[:, 4:5], NORM_EPS, None, ALU.add))
                    link(v.reciprocal(nte[:, 6:7], nte[:, 5:6]))
                    v.tensor_scalar(erow[:, 1, :], erow[:, 0, :], nte[:, 6:7], None, ALU.mult).then_inc(s_dve, 1)
                dve.wait_ge(s_act, L + 1)
                link(v.tensor_scalar(crow[:, 1, :], crow[:, 1, :], 1.0, None, ALU.add))
                link(v.reciprocal(crow[:, 3, :], crow[:, 1, :]))
                v.tensor_tensor(crow[:, 2, :], crow[:, 0, :], crow[:, 3, :], ALU.mult).then_inc(s_dve, 1)
                dve.wait_ge(s_pe, pe0 + 1)
                v.tensor_scalar(A[L][:, :], ps_p[:, 0, 0:D], SCALE[L], None, ALU.mult)
                v.tensor_copy(WvT[L][:, :], ps_p[:, 1, 0:D])
                if L == 0:
                    v.tensor_copy(woT[:, :], ps_p[:, 1, D:2 * D])
                    v.tensor_copy(RW[0][:, :], ps_p[:, 1, 2 * D:2 * D + 2 * E])
                else:
                    v.tensor_scalar(relu_b1[:, :], ps_p[:, 1, 3 * D:3 * D + E * HC], 0.0, None, ALU.max)
                v.tensor_copy(b1T[L][:, :], ps_p[:, 1, 3 * D:3 * D + E * HC])
                dve.wait_ge(s_pe, pe0 + 2)
                v.tensor_copy(scT[:, :], ps_a[:, 0:NB]).then_inc(s_dve, 1)
                dve.wait_ge(s_pe, pe0 + 3)
                if L == 1:
                    dve.wait_ge(mod_out[0], 16)
                link(v.tensor_scalar(csrow[:, 0, :], ps_s[0:NB, 0, D:2 * D], 1.0, None, ALU.add))
                v.tensor_copy(csrow[:, 1, :], ps_s[0:NB, 0, 0:D]).then_inc(s_dve, 1)
                v.tensor_scalar(crow[:, 1, :], ps_s[0:NB, 1, D:2 * D], 1.0, None, ALU.add)
                v.tensor_copy(crow[:, 2, :], ps_s[0:NB, 1, 0:D])
                for m, src in ((0, ps_s[0:NB, 0, 2 * D:3 * D]), (3, ps_s[0:NB, 1, 2 * D:3 * D])):
                    link(v.tensor_copy(crow[:, m, :], src))
                    link(v.scalar_tensor_tensor(erow[:, 0, :], crow[:, m, :], -1.0, crow[:, m, :], ALU.mult, ALU.max))
                    link(v.tensor_scalar(erow[:, 0, :], erow[:, 0, :], 0.25, None, ALU.max))
                    link(v.tensor_scalar(erow[:, 1, :], crow[:, m, :], 0.0, 2.0, ALU.is_ge, ALU.mult))
                    last = v.scalar_tensor_tensor(crow[:, m, :], erow[:, 1, :], -1.0, erow[:, 0, :], ALU.add, ALU.mult)
                    if m == 0:
                        link(last)
                last.then_inc(rows_ready, 1)
                dve.wait_ge(s_pe, pe0 + 4)
                link(v.tensor_copy(caT[L][:, :], ps_a[:, 0:NB]))
                if L == 1:
                    dve.wait_ge(rows_ready, 2)
                v.tensor_copy(saT[L][:, :], ps_a[:, NB:2 * NB]).then_inc(s_dve, 1 if L == 0 else 2)

            def constant_rows():
                dve.wait_ge(s_pe, 9)
                dve.wait_ge(in_small[1], 16 * N_SMALL[1])
                b2, r = B2[1][0:1, :, :], ps_o[0:1, :, :].rearrange("p a (e d) -> p (a e) d", d=D)
                total, rows = rrow[:, 0:D], B2[1][0:1, :, :]
                link(v.tensor_reduce(rrow[:, 0:D], b2.rearrange("p e d -> p d e"), AX.X, ALU.add))
                link(v.tensor_reduce(rrow[:, D:2 * D], r.rearrange("p e d -> p d e"), AX.X, ALU.add))
                link(v.tensor_tensor(rrow[:, 0:D], rrow[:, 0:D], rrow[:, D:2 * D], ALU.add))
                v.tensor_tensor(rows, rrow[:, 0:D].unsqueeze(1).to_broadcast([1, E, D]), r, ALU.subtract).then_inc(rows_ready, 1)

            def tile(ap, n):
                return ap[:, bass.ds(n, 1), :].rearrange("p a d -> p (a d)")

            def ln_stats(b, sem_, st_, mv_, nt_, rstd):
                base = LN_STEPS * b
                for j in range(J):
                    v.bn_stats(st_[:, j, :], tile(X, b * J + j)).then_inc(sem_, 1)
                wait_apart(dve, sem_, base + J)
                for j in range(J):
                    v.bn_aggr(mv_[:, j, :], st_[:, j, :]).then_inc(sem_, 1)
                dve.wait_ge(sem_, base + 2 * J)
                k = [2 * J]

                def step(ins):
                    k[0] += 1
                    ins.then_inc(sem_, 1)
                    dve.wait_ge(sem_, base + k[0])

                step(v.tensor_scalar(nt_[:, 0, :], mv_[:, :, 1], LN_EPS, None, ALU.add))
                rsqrt(nt_[:, 0, :], nt_[:, 1, :], nt_[:, 2, :], rstd, step)
                assert k[0] == LN_STEPS

            def ln1(L, b, u):
                if L == 1:
                    dve.wait_ge(comb_done[0], BIAS + b * J + J)
                wait_apart(dve, xn_ready[L], BIAS + b - 1)
                ln_stats(b, ln1_chain[L], st1, mv1, nt1, rs1[:, u, :])
                v.scalar_tensor_tensor(nb1[:, u, :], mv1[:, :, 0], -1.0, rs1[:, u, :], ALU.mult, ALU.mult).then_inc(ln1_ready[L], 1)

            def post(L, q, u, half):
                wait_apart(dve, *((y_add, BIAS + q + 1) if L == 0 else (o_done[1], BIAS + 4 * q + 4)))
                ln_stats(q, ln2_chain[L], st2, mv2, nt2, rs2[:, u, :])
                dve.wait_ge(p_tr[L], BIAS + q - 1)
                if L == 0:
                    dve.wait_ge(sq_ready, BIAS + q - 1)
                dve.wait_ge(hkeep[L][u], 16 + 16 * half)
                for j in range(J):
                    v.scalar_tensor_tensor(Hc[:, u, j, :], tile(X, q * J + j), mv2[:, j, 0:1],
                                           MB[:, bass.ds(q, 1), 1, :].rearrange("p a d -> p (a d)"),
                                           ALU.subtract, ALU.mult).then_inc(hc_chain[L], 1)
                dve.wait_ge(hc_chain[L], J * q + J)
                for j in range(J):
                    last = v.scalar_tensor_tensor(Hc[:, u, j, :], Hc[:, u, j, :], rs2[:, u, j:j + 1],
                                                  MB[:, bass.ds(q, 1), 2, :].rearrange("p a d -> p (a d)"), ALU.mult, ALU.add)
                last.then_inc(hc_ready[L], 1)

            def row_max(L, n, j, u):
                dve.wait_ge(s_mm[L], BIAS + n + 1)
                v.tensor_reduce(negm[:, 4 * u + j:4 * u + j + 1], ps_s[:, j % 2, :], AX.X, ALU.max, negate=True)\
                 .then_inc(negm_ready[L], 1)

            def row_scale(L, n, j, u):
                dve.wait_ge(exp_done[L], BIAS + n + 1)
                v.reciprocal(rinv[:, 4 * u + j:4 * u + j + 1], rowsum[:, 4 * u + j:4 * u + j + 1]).then_inc(rinv_ready[L], 1)

            def attn_out(n, j, u):
                dve.wait_ge(pv_mm[1], BIAS + n + 1)
                dve.wait_ge(rinv_ready[1], BIAS + n + 1)
                v.scalar_tensor_tensor(tile(X, n), ps_o[:, j % 2, 0:D], rinv[:, 4 * u + j:4 * u + j + 1], tile(X, n),
                                       ALU.mult, ALU.add).then_inc(o_done[1], 1)

            def y_out(b):
                dve.wait_ge(y_mm, BIAS + b + 1)
                xb = X[:, bass.ds(b * J, J), :]
                v.tensor_tensor(xb, ps_b[:, :].rearrange("p (j d) -> p j d", j=J), xb, ALU.add).then_inc(y_add, 1)

            def router_out(L, q):
                dve.wait_ge(r_mm[L], BIAS + q + 1)
                v.tensor_copy(sims[:, bass.ds(q * J, J), 0:NR[L]],
                              ps_b[:, 0:J * NR[L]].rearrange("p (j e) -> p j e", j=J)).then_inc(r_ready[L], 1)

            def sum_squares(q, u):
                dve.wait_ge(sq_ready, BIAS + q + 1)
                v.tensor_reduce(sumsq[:, bass.ds(q * J, J)], sq[:, u, :, :], AX.X, ALU.add).then_inc(sq_used, 1)

            def values_out(b, u):
                dve.wait_ge(v_mm[1], BIAS + b + 1)
                v.tensor_tensor(V[:, u, :, :], ps_a[:, :].rearrange("p (j d) -> p j d", j=J),
                                MB[:, bass.ds(b, 1), 0, :].to_broadcast([P, J, D]), ALU.mult).then_inc(v_ready[1], 1)

            def combine(L, b, at, r, count, uses):
                dve.wait_ge(gat[L][r], 16 * TOPK[L] * uses)
                a = acc[:, r % 2, :]
                c0 = count * (2 * TOPK[L] - 1)
                gb = tile(GBB[L], b)
                if L == 0:
                    v.tensor_scalar(a, yg[:, r, 0, :], weight[:, 0, bass.ds(at, 1)], None, ALU.mult).then_inc(comb_chain[0], 1)
                    dve.wait_ge(comb_chain[0], c0 + 1)
                    v.scalar_tensor_tensor(a, yg[:, r, 1, :], weight[:, 1, bass.ds(at, 1)], a, ALU.mult, ALU.add).then_inc(comb_chain[0], 1)
                    dve.wait_ge(comb_chain[0], c0 + 2)
                    v.tensor_tensor(a, a, gb, ALU.mult).then_inc(comb_chain[0], 1)
                    dve.wait_ge(comb_chain[0], c0 + 3)
                else:
                    v.tensor_tensor(a, yg[:, r, 0, :], gb, ALU.mult).then_inc(comb_chain[1], 1)
                    dve.wait_ge(comb_chain[1], c0 + 1)
                v.tensor_tensor(tile(X, at), tile(X, at), a, ALU.add).then_inc(comb_done[L], 1)

            def route(L, g):
                C, T = NC[L], slice(g * GT, (g + 1) * GT)
                dve.wait_ge(r_ready[L], BIAS + GB * (g + 1))
                three = [P, GT, E]
                Mv = M[:, 0:E * C].rearrange("p (e c) -> p c e", e=E)

                def over_e(x):
                    return x.unsqueeze(2).to_broadcast(three)

                def over_t(x):
                    return x.unsqueeze(1).to_broadcast(three)

                def first_of(mask, k):
                    link(v.tensor_tensor(rtmp[:, :, :], mask, over_t(rev8[:, :]), ALU.mult))
                    link(v.tensor_reduce(row[:, 1, :], rtmp[:, :, :], AX.X, ALU.max))
                    link(v.tensor_tensor(Mv[:, k * GT:(k + 1) * GT, :], over_t(rev8[:, :]), over_e(row[:, 1, :]), ALU.is_equal))

                def best(k, to):
                    link(v.tensor_reduce(row[:, to, :], score[:, :, :], AX.X, ALU.max))
                    link(v.tensor_tensor(rtmp[:, :, :], score[:, :, :], over_e(row[:, to, :]), ALU.is_equal))
                    first_of(rtmp[:, :, :], k)

                if L == 0:
                    dve.wait_ge(sq_used, BIAS + GB * (g + 1))
                    raw, cosn, ss = sims[:, T, 0:E], sims[:, T, E:2 * E], sumsq[:, T]
                    rsqrt(ss, row[:, 0, :], row[:, 1, :], row[:, 2, :], link)
                    link(v.tensor_tensor(row[:, 3, :], ss, row[:, 2, :], ALU.mult))
                    link(v.tensor_scalar(row[:, 3, :], row[:, 3, :], NORM_EPS, None, ALU.add))
                    link(v.reciprocal(row[:, 2, :], row[:, 3, :]))
                    link(v.tensor_tensor(score[:, :, :], cosn, over_e(row[:, 2, :]), ALU.mult))
                    link(v.scalar_tensor_tensor(score[:, :, :], over_t(bonus[:, :]), CACHE_BONUS, score[:, :, :], ALU.mult, ALU.add))
                    link(v.tensor_reduce(row[:, 0, :], raw, AX.X, ALU.min))
                    link(v.tensor_tensor(rtmp[:, :, :], raw, over_e(row[:, 0, :]), ALU.is_equal))
                    link(v.tensor_tensor(rtmp[:, :, :], rtmp[:, :, :], over_t(up8[:, :]), ALU.mult))
                    link(v.tensor_reduce(row[:, 1, :], rtmp[:, :, :], AX.X, ALU.max))
                    link(v.tensor_tensor(rtmp[:, :, :], over_t(up8[:, :]), over_e(row[:, 1, :]), ALU.is_equal))
                    link(v.scalar_tensor_tensor(score[:, :, :], rtmp[:, :, :], -BIG, score[:, :, :], ALU.mult, ALU.add))
                    best(0, 2)
                    link(v.scalar_tensor_tensor(score[:, :, :], Mv[:, 0:GT, :], -BIG, score[:, :, :], ALU.mult, ALU.add))
                    best(1, 3)
                    v.tensor_tensor(row[:, 4, :], row[:, 3, :], row[:, 2, :], ALU.subtract).then_inc(gap_ready, 1)
                else:
                    link(v.tensor_tensor(score[:, :, :], sims[:, T, 0:E], over_t(brB[:, :]), ALU.add))
                    best(0, 2)
                v.tensor_copy(Mb[:, 0:E * C], M[:, 0:E * C]).then_inc(m_ready, 1)
                if L == 0:
                    dve.wait_ge(gap_exp, g + 1)
                    link(v.tensor_scalar(row[:, 6, :], row[:, 5, :], 1.0, None, ALU.add))
                    link(v.reciprocal(weight[:, 0, T], row[:, 6, :]))
                    link(v.tensor_tensor(weight[:, 1, T], weight[:, 0, T], row[:, 5, :], ALU.mult))
                dve.wait_ge(rank_mm, 2 * L + g + 1)
                N = E * C
                link(v.tensor_copy(tot[:, 0:N], ps_b[:, N:2 * N]))
                link(v.tensor_tensor_scan(cum[:, 0:N], keep[L][:, :], tot[:, 0:N], 0.0, ALU.mult, ALU.add))
                link(v.tensor_tensor(tot[:, 0:N], cum[:, 0:N], tot[:, 0:N], ALU.subtract))
                v.tensor_tensor(tot[:, 0:N], tot[:, 0:N], ps_b[:, 0:N], ALU.add).then_inc(rank_read, 1)
                dve.wait_ge(rank_read, 2 * L + g + 1)
                n_e = cum[:, 0:N].rearrange("p (e c) -> p e c", e=E)[:, :, C - 1:C]
                cnt = cmpt[:, 0:GT, :].rearrange("p t e -> p (t e)").rearrange("p (e t) -> p e t", e=E)
                link(v.tensor_tensor(cnt, n_e.to_broadcast([P, E, GT]),
                                     thr16[:, :].unsqueeze(1).to_broadcast([P, E, GT]), ALU.is_gt))
                link(v.tensor_reduce(exs[:, 0, :], cnt, AX.X, ALU.add))
                link(v.tensor_tensor_scan(exs[:, 1, :], onesf[:, :], exs[:, 0, :], 0.0, ALU.mult, ALU.add))
                link(v.tensor_tensor(exs[:, 2, :], exs[:, 1, :], exs[:, 0, :], ALU.subtract))
                link(v.tensor_scalar(exs[:, 2, :], exs[:, 2, :], float(P), None, ALU.mult))
                tv = tot[:, 0:N].rearrange("p (e c) -> p e c", e=E)
                link(v.tensor_tensor(tv, tv, exs[:, 2, :].unsqueeze(2).to_broadcast([P, E, C]), ALU.add))
                link(v.tensor_tensor(tot[:, 0:N], tot[:, 0:N], M[:, 0:N], ALU.mult))
                link(v.tensor_reduce(slotf[:, 0:C], tot[:, 0:N].rearrange("p (e c) -> p c e", e=E), AX.X, ALU.add))
                link(v.tensor_copy(slot[:, g, 0:C], slotf[:, 0:C]))
                NT = TILES[L]
                link(v.tensor_tensor(cmpt[:, 0:NT, :], exs[:, 1, :].unsqueeze(1).to_broadcast([P, NT, E]),
                                     iotaT[:, 0:NT].unsqueeze(2).to_broadcast([P, NT, E]), ALU.is_le))
                link(v.tensor_reduce(eidf[:, 0:NT], cmpt[:, 0:NT, :], AX.X, ALU.add))
                v.tensor_scalar(eid[:, g * NT:(g + 1) * NT], eidf[:, 0:NT], float(E - 1), None, ALU.min).then_inc(route_done, 1)
                dve.wait_ge(route_done, 2 * L + g + 1)

            def body(L, b, u, half, prev2, prev, nxt, combos=(), squares=True):
                for j in range(J):
                    n = 4 * b + j
                    if j < 3:
                        row_max(L, n + 1, j + 1, u)
                    elif nxt:
                        row_max(L, n + 1, 0, 1 - u)
                    row_scale(L, n, j, u)
                    if L == 1:
                        if j > 0:
                            attn_out(n - 1, j - 1, u)
                        elif prev:
                            attn_out(n - 1, 3, 1 - u)
                    if j == 0:
                        if prev2:
                            router_out(L, b - 2)
                        if nxt:
                            ln1(L, b + 1, 1 - u)
                    if j == 1 and prev:
                        if L == 0:
                            y_out(b - 1)
                        post(L, b - 1, 1 - u, half)
                    if j == 2 and nxt and L == 1:
                        values_out(b + 1, 1 - u)
                    if j == 3 and prev and L == 0 and squares:
                        sum_squares(b - 1, 1 - u)
                    for c in combos[j:j + 1]:
                        for args in c:
                            combine(0, *args)

            def expert_out(L, q, r, e):
                dve.wait_ge(dn_mm[L], BIAS + q * 4 + (r + 1))
                if r % 2 == 0:
                    dve.wait_ge(st[L][r // 2], 16 + q * 16)
                v.tensor_tensor(yt[:, r, :], ps_o[:, r % 2, 0:D], tile(B2[L], e), ALU.add).then_inc(y_ready[L], 1)

            def quad(L, q, tiles=None):
                e = experts(DVE, q)
                for r in range(4):
                    expert_out(L, q, r, e[r])
                    if tiles is not None:
                        combine(L, tiles, tiles * 4 + r, r, tiles * 4 + r, tiles + 1)

            dve.wait_ge(in_x0, 16)
            ln1(0, 0, 0)
            for L in (0, 1):
                setup(L)
            dve.wait_ge(in_x, 16 * (NB - 1))
            dve.wait_ge(mod_in[0], 32)
            for L in (0, 1):
                NQ, CQ = 2 * TILES[L] // 4, TILES[L] // 4 + 1
                if L == 1:
                    ln1(1, 0, 0)
                    constant_rows()
                    dve.wait_ge(mod_in[1], 32)
                    values_out(0, 0)
                row_max(L, 0, 0, 0)

                def combos(b):
                    if L == 0:
                        return ()
                    if isinstance(b, int):
                        return [[(GB + b, GT + 4 * b + r, r, GT + 4 * b + r, GB + b + 1)] for r in range(4)]
                    i, k = b[1:]
                    return [[], []] + [[(i + (GB + 1), i * 4 + (GT + 4 + r), r, i * 4 + (GT + 4 + r), i + (GB + 2))] for r in (2 * k, 2 * k + 1)]

                body(L, 0, 0, 0, False, False, True, combos(0))
                body(L, 1, 1, 0, False, True, True, combos(1))
                with dve.Fori(1, 3, 1) as i:
                    body(L, 2 * i, 0, i - 1, True, True, True, combos((None, i, 0)))
                    body(L, 2 * i + 1, 1, i, True, True, True, combos((None, i, 1)))
                route(L, 0)
                body(L, 6, 0, 2, True, True, True)
                body(L, 7, 1, 3, True, True, False, squares=False)
                if L == 1:
                    attn_out(4 * 7 + 3, 3, 1)
                router_out(L, 6)
                dve.wait_ge(in_moe[L], 16 * in_moe_all[L])
                if L == 1:
                    dve.wait_ge(b2_in, 16)
                if L == 0:
                    y_out(7)
                post(L, 7, 1, 3)
                quad(L, 0)
                quad(L, 1)
                router_out(L, 7)
                if L == 0:
                    sum_squares(6, 0)
                    sum_squares(7, 1)
                quad(L, 2)
                route(L, 1)
                with dve.Fori(3, CQ, 1) as q:
                    quad(L, q)
                with dve.Fori(CQ, min(CQ + 4, NQ - 1), 1) as q:
                    quad(L, q, tiles=q - CQ)
                if CQ + 4 < NQ - 1:
                    with dve.Fori(CQ + 4, NQ - 1, 1) as q:
                        quad(L, q)
                quad(L, NQ - 1)
            with dve.Fori(0, 4, 1) as i:
                for r in range(4):
                    combine(1, i + GB, i * 4 + (GT + r), r, i * 4 + (GT + r), i + (GB + 1))


_INS = ['L0_attn_q', 'L0_attn_wq', 'L0_attn_wk', 'L0_attn_wv', 'L0_attn_wo', 'L0_ffn_uzman_embeddings', 'L0_ffn_W1',
        'L0_ffn_b1', 'L0_ffn_W2', 'L0_ffn_b2', 'L0_ffn_onbellek_durumu', 'L0_c', 'L0_wmod', 'L1_attn_W_qkv', 'L1_ffn_W1',
        'L1_ffn_b1', 'L1_ffn_W2', 'L1_ffn_b2', 'L1_ffn_Wr', 'L1_ffn_br', 'L1_c', 'L1_wmod']
_OUTS = [((8, 512, 128), 'float32')]


def kernel(**inputs):
    import numpy as _np
    import concourse.bacc as _bacc
    from concourse import mybir as _mybir
    from concourse.bass_utils import run_bass_kernel_spmd as _run

    nc = _bacc.Bacc("TRN2", target_bir_lowering=False, num_devices=1)
    arrays, args = {}, []
    for name in _INS:
        a = _np.ascontiguousarray(inputs[name])
        arrays[f"in_{name}_dram"] = a
        args.append(nc.dram_tensor(f"in_{name}_dram", a.shape, _mybir.dt.from_np(a.dtype), kind="ExternalInput").ap())
    for i, (shape, dtype) in enumerate(_OUTS):
        dt = _mybir.dt.from_np(_np.dtype(dtype))
        args.append(nc.dram_tensor(f"out_{i}_dram", shape, dt, kind="ExternalOutput").ap())
    adaln_kernel(nc, *args)
    r = _run(nc, [arrays], core_ids=[0])
    return r.results[0]["out_0_dram"]
```

```python
from contextlib import ExitStack

import concourse.bass as bass
from concourse import mybir

P = 128
F32 = mybir.dt.float32
BF16 = mybir.dt.bfloat16
I32 = mybir.dt.int32
ALU = mybir.AluOpType
ACT = mybir.ActivationFunctionType
AX = mybir.AxisListType

NB = 8
S = 512
D = 128
J = S // P
E = 8
HID = 512
HC = HID // P
TOPK = [2, 1]
NR = [2 * E, E]
GROUPS = [(3, 5), (4, 4)]
FIRST = [(0, n) for n, _ in GROUPS]
GT = [[J * n for n in group] for group in GROUPS]
NC = [[TOPK[L] * n for n in GT[L]] for L in (0, 1)]
NT = [[c + E for c in NC[L]] for L in (0, 1)]
ALL = [sum(n) for n in NT]
MAX_GT, MAX_NC, MAX_NT = [max(max(a) for a in x) for x in (GT, NC, NT)]
RING = 8
LEAD = [3, 2]
BIAS = 4
ROUTE_AT = [[(1, 2), (1, 3), (2, 0), (2, 1), (2, 3), (3, 0), (3, 0), (3, 1)],
            [(1, 0), (1, 0), (1, 1), (1, 1), (1, 3), (2, 0), (2, 0), (2, 0)]]
RANKS_AT = [(2, 2), (1, 2)]
SP, PE, Activation, DVE = (mybir.EngineType.SP, mybir.EngineType.PE, mybir.EngineType.Activation, mybir.EngineType.DVE)
LN_EPS = 1e-5
NORM_EPS = 1e-8
CACHE_BONUS = 0.1
BIG = 3.0e38
MAGIC = 0x5F3759DF


def adaln_kernel(nc, L0_attn_q, L0_attn_wq, L0_attn_wk, L0_attn_wv, L0_attn_wo,
                 L0_ffn_uzman_embeddings, L0_ffn_W1, L0_ffn_b1, L0_ffn_W2, L0_ffn_b2,
                 L0_ffn_onbellek_durumu, L0_c, L0_wmod, L1_attn_W_qkv, L1_ffn_W1, L1_ffn_b1,
                 L1_ffn_W2, L1_ffn_b2, L1_ffn_Wr, L1_ffn_br, L1_c, L1_wmod, out):
    W1_D, W2_D = [L0_ffn_W1, L1_ffn_W1], [L0_ffn_W2, L1_ffn_W2]
    B1_D, B2_D = [L0_ffn_b1, L1_ffn_b1], [L0_ffn_b2, L1_ffn_b2]
    C_D, WMOD_D = [L0_c, L1_c], [L0_wmod, L1_wmod]
    SCALE = [(D / 16) ** -0.5, D ** -0.5]

    xs_d = [nc.dram_tensor(f"xs_scratch{g}", (max(NT[0][g], NT[1][g]) * P, D), F32, kind="Internal").ap() for g in (0, 1)]
    ys_d = [[nc.dram_tensor(f"ys_scratch{L}{g}", (NT[L][g] * P, D), F32, kind="Internal").ap() for g in (0, 1)]
            for L in (0, 1)]
    mod_d = [nc.dram_tensor(f"mod_scratch{L}", (NB, 4 * D), F32, kind="Internal").ap() for L in (0, 1)]
    b2_d = nc.dram_tensor("b2_scratch", (1, E * D), F32, kind="Internal").ap()

    ctx = ExitStack()
    with ctx:
        def sb(name, shape, dt=F32):
            return ctx.enter_context(nc.sbuf_tensor(name, shape, dt))

        def sem(name):
            return ctx.enter_context(nc.semaphore(name))

        def sem2(name):
            return [sem(f"{name}_{L}") for L in (0, 1)]

        ps_a = ctx.enter_context(nc.psum_tensor("ps_a", [P, 512], F32))
        ps_b = ctx.enter_context(nc.psum_tensor("ps_b", [P, 512], F32))
        ps_s = ctx.enter_context(nc.psum_tensor("ps_s", [P, 2, 512], F32))
        ps_p = ctx.enter_context(nc.psum_tensor("ps_p", [P, 2, 512], F32))
        ps_o = ctx.enter_context(nc.psum_tensor("ps_o", [P, 2, 512], F32))

        X = sb("X", [P, NB * J, D])
        W1 = sb("W1", [P, 4, HID])
        W2 = [sb(f"W2_{L}", [P, E, HC, D]) for L in (0, 1)]
        B2 = [sb(f"B2_{L}", [P, E, D]) for L in (0, 1)]
        MB = sb("MB", [P, NB, 3, D])
        GBB = [sb(f"GBB_{L}", [P, NB, D]) for L in (0, 1)]
        H = sb("H", [P, NB * J, D])
        Hc = sb("Hc", [P, 2, J, D])
        xn = sb("xn", [P, 2, J, D])
        hT = sb("hT", [P, 2, S])
        gT = sb("gT", [P, 2, S])
        V = sb("V", [P, 2, J, D])
        prob = sb("prob", [P, 2, S])
        probT = sb("probT", [P, 2, J, P])
        hT2 = sb("hT2", [P, S])
        sq = sb("sq", [P, J, D])
        xt = sb("xt", [P, 4, D])
        xT = sb("xT", [P, 2, P])
        hTm = sb("hTm", [P, 2, HC, P])
        yt = sb("yt", [P, 4, D])
        yg = sb("yg", [P, RING, 2, D])
        On = yg[:, 0:J, 0, :]
        acc = sb("acc", [P, J, D])
        A = [sb(f"A_{L}", [P, D]) for L in (0, 1)]
        WvT = [sb(f"WvT_{L}", [P, D]) for L in (0, 1)]
        woT = sb("woT", [P, D])
        WG = sb("WG", [P, J, D])
        RW = [sb(f"RW_{L}", [P, NR[L]]) for L in (0, 1)]
        caT = [sb(f"caT_{L}", [P, NB]) for L in (0, 1)]
        saT = [sb(f"saT_{L}", [P, NB]) for L in (0, 1)]
        ident = sb("ident", [P, P])
        upper = sb("upper", [P, P], BF16)
        ones = sb("ones", [P, P], BF16)
        rev8 = sb("rev8", [P, E])
        up8 = sb("up8", [P, E])
        thr16 = sb("thr16", [P, MAX_GT])
        iotaT = sb("iotaT", [P, MAX_NT])
        run = [[sb(f"run_{L}{g}", [P, E * NC[L][g]]) for g in (0, 1)] for L in (0, 1)]
        onesf = sb("onesf", [P, E])
        bonus = sb("bonus", [P, E])
        brB = sb("brB", [P, E])
        stats = sb("stats", [P, 2, 2, J, 6])
        mv = sb("mv", [P, 2, NB + 5, J, 2])
        var = sb("var", [P, 3, NB + 5, J])
        rdev = sb("rdev", [P, 3, NB + 5, J])
        newton = sb("newton", [P, 2, 3, J])
        nb = sb("nb", [P, 2, NB + 5, J])
        negm = sb("negm", [P, 8])
        rowsum = sb("rowsum", [P, 8])
        rinv = sb("rinv", [P, 8])
        sims = sb("sims", [P, NB * J, NR[0]])
        score = sb("score", [P, MAX_GT, E])
        rtmp = sb("rtmp", [P, MAX_GT, E])
        cmpt = sb("cmpt", [P, MAX_NT, E])
        M = sb("M", [P, E * MAX_NC])
        Mb = sb("Mb", [P, E * MAX_NC], BF16)
        cum = sb("cum", [P, E * MAX_NC])
        tot = sb("tot", [P, E * MAX_NC])
        row = sb("row", [P, 8, MAX_GT])
        exs = sb("exs", [P, 3, E])
        slotf = sb("slotf", [P, MAX_NC])
        slot = sb("slot", [P, 2, MAX_NC], I32)
        weight = sb("weight", [P, 2, NB * J])
        eidf = sb("eidf", [P, MAX_NT])
        eid = sb("eid", [P, max(ALL)], I32)
        crow = sb("crow", [NB, 4, D])
        silu_c = sb("silu_c", [NB, 3, D])
        scT = sb("scT", [P, NB])
        gate = sb("gate", [NB, 2, D])
        wsm = [sb(f"wsm_{L}", [P, 4 - L, D]) for L in (0, 1)]
        erow = sb("erow", [E, 2, D])
        nte = sb("nte", [E, 8])
        wmod = [sb(f"wmod_{L}", [P, 6 * D]) for L in (0, 1)]
        b1row = sb("b1row", [E * HC, 2, D])
        b1T = [sb(f"b1T_{L}", [P, E * HC]) for L in (0, 1)]
        relu_b1 = sb("relu_b1", [P, E * HC])
        rrow = sb("rrow", [1, 2, D])

        in_small = sem2("in_small")
        in_c, in_w = sem2("in_c"), sem2("in_w")
        in_x = [sem(f"in_x_{b}") for b in range(NB)]
        in_moe = sem2("in_moe")
        consts = sem("consts")
        s_act, s_pe, s_dve = sem("setup_act"), sem("setup_pe"), sem("setup_dve")
        rows_ready = sem("rows_ready")
        mod_out, mod_in = sem2("mod_out"), sem2("mod_in")
        b2_out, b2_in = sem("b2_out"), sem("b2_in")
        r_prod = sem("r_prod")
        xs_zero = sem("xs_zero")
        chain = sem("dve_chain")
        pool_chain = sem("pool_chain")
        ln1_ready = sem2("ln1_ready")
        xn_ready = sem2("xn_ready")
        xn_chain = sem2("xn_chain")
        h_tr = sem2("h_tr")
        hT_ready = sem2("hT_ready")
        g_mm = sem2("g_mm")
        gT_ready = sem2("gT_ready")
        v_mm = sem2("v_mm")
        v_ready = sem2("v_ready")
        s_mm = sem2("s_mm")
        negm_ready = sem2("negm_ready")
        exp_done = sem2("exp_done")
        rinv_ready = sem2("rinv_ready")
        pt_mm = sem2("pt_mm")
        pt_ready = sem2("pt_ready")
        pv_mm = sem2("pv_mm")
        o_done = sem2("o_done")
        wg_ready = sem2("wg_ready")
        y_mm = sem("y_mm")
        y_add = sem("y_add")
        ln2_ready = sem("ln2_ready")
        hn_ready = sem("hn_ready")
        hc_ready = sem2("hc_ready")
        hkeep = [[sem(f"hkeep_{L}_{u}") for u in (0, 1)] for L in (0, 1)]
        p_tr = sem2("p_tr")
        hT2_ready = sem2("hT2_ready")
        r_mm = sem2("r_mm")
        r_ready = sem2("r_ready")
        sq_ready = sem("sq_ready")
        weights_ready = sem("weights_ready")
        m_ready, rank_mm, rank_read, route_done = sem("m_ready"), sem("rank_mm"), sem("rank_read"), sem("route_done")
        gap_ready, gap_exp = sem("gap_ready"), sem("gap_exp")
        scat = [[sem(f"scat_{L}_{g}") for g in (0, 1)] for L in (0, 1)]
        ld = [[sem(f"ld_{L}_{h}") for h in (0, 1)] for L in (0, 1)]
        w1_in = [[sem(f"w1_in_{L}_{r}") for r in range(4)] for L in (0, 1)]
        st = [[sem(f"st_{L}_{h}") for h in (0, 1)] for L in (0, 1)]
        xt_mm = sem2("xt_mm")
        xT_ready = sem2("xT_ready")
        up_mm = sem2("up_mm")
        hTm_ready = sem2("hTm_ready")
        dn_mm = sem2("dn_mm")
        y_ready = sem2("y_ready")
        gat_end = [sem(f"gat_end_{c}") for c in range(GT[1][1])]
        gat = [sem(f"gat_{r}") for r in range(RING)]
        scaled = sem("scaled")
        rows_used = sem2("rows_used")
        comb_done = sem2("comb_done")
        stored = sem("stored")

        paced = {
            "pe": h_tr + g_mm + v_mm + s_mm + pt_mm + pv_mm + [y_mm] + p_tr + r_mm + xt_mm + up_mm + dn_mm,
            "act": hT_ready + gT_ready + v_ready + [sq_ready] + exp_done + pt_ready + [o_done[0]] + hT2_ready + xT_ready + hTm_ready,
            "dve": ln1_ready + negm_ready + rinv_ready + [o_done[1], y_add] + hc_ready + r_ready
                   + y_ready + comb_done,
            "pool": xn_ready + wg_ready,
        }

        def gathered(L, t):
            uses = t // RING + 1
            return 32 * uses if L == 0 else 32 * (NB * J // RING) + 16 * uses

        def upto(n):
            return min(n, NB)

        def experts(engine, q):
            return nc.values_load_multi_w_load_instructions(
                eid[0:1, bass.ds(q * 4, 4)], engines=[engine], min_val=0, max_val=E - 1,
                skip_runtime_bounds_check_because="it counts experts up to E - 1")[1]

        def bias(eng, name):
            for s in paced[name]:
                eng.sem_inc(s, BIAS)

        block = ctx.enter_context(nc.Block())

        @block.sync
        def _(sp):
            for L in (0, 1):
                for u in (0, 1):
                    sp.sem_inc(hkeep[L][u], 16)
                for h in (0, 1):
                    sp.sem_inc(st[L][h], 16)

            def load_batch(b):
                sp.dma_start(X[:, b * J:(b + 1) * J, :], L0_attn_q[b].rearrange("(p j) d -> p j d", j=J)).then_inc(in_x[b], 16)

            def load_mods(L):
                sp.dma_start(MB[:, :, :, :].rearrange("p b m d -> p b (m d)"),
                             mod_d[L][:, 0:3 * D].partition_broadcast(P)).then_inc(mod_in[L], 16)
                sp.dma_start(GBB[L][:, :, :], mod_d[L][:, 3 * D:4 * D].partition_broadcast(P)).then_inc(mod_in[L], 16)

            sp.dma_start(crow[:, 0, :], C_D[0]).then_inc(in_c[0], 16)
            load_batch(0)
            sp.dma_start(wmod[0][:, :], WMOD_D[0]).then_inc(in_w[0], 16)
            for n, src in enumerate((L0_attn_wq, L0_attn_wk, L0_attn_wv)):
                sp.dma_start(wsm[0][:, n, :], src).then_inc(in_w[0], 16)
            load_batch(1)
            sp.dma_start(wsm[0][:, 3, :], L0_attn_wo).then_inc(in_small[0], 16)
            sp.dma_start(erow[:, 0, :], L0_ffn_uzman_embeddings).then_inc(in_small[0], 16)
            sp.dma_start(b1row[:, 0, :], B1_D[0].rearrange("e (c p) -> (e c) p", p=P)).then_inc(in_small[0], 16)
            sp.dma_start(bonus[:, :], L0_ffn_onbellek_durumu.partition_broadcast(P)).then_inc(in_small[0], 16)
            for b in range(2, NB):
                load_batch(b)
            sp.wait_ge(rows_ready, 1)
            sp.dma_start(mod_d[0], crow[:, :, :].rearrange("b m d -> b (m d)")).then_inc(mod_out[0], 16)
            sp.wait_ge(mod_out[0], 16)
            load_mods(0)
            sp.dma_start(crow[:, 0, :], C_D[1]).then_inc(in_c[1], 16)
            sp.dma_start(wmod[1][:, :], WMOD_D[1]).then_inc(in_w[1], 16)
            for n in range(3):
                sp.dma_start(wsm[1][:, n, :], L1_attn_W_qkv[n * D:(n + 1) * D, :]).then_inc(in_w[1], 16)
            sp.dma_start(RW[1][:, :], L1_ffn_Wr).then_inc(in_small[1], 16)
            sp.dma_start(brB[:, :], L1_ffn_br.partition_broadcast(P)).then_inc(in_small[1], 16)
            sp.dma_start(b1row[:, 1, :], B1_D[1].rearrange("e (c p) -> (e c) p", p=P)).then_inc(in_small[1], 16)
            sp.dma_start(B2[1][0:1, :, :].rearrange("a e d -> a (e d)"), L1_ffn_b2.rearrange("(a e) d -> a (e d)", a=1)).then_inc(in_small[1], 16)
            for L in (0, 1):
                sp.dma_start(W2[L][:, :, :, :], W2_D[L].rearrange("e (c p) d -> p e c d", p=P)).then_inc(in_moe[L], 16)
            sp.dma_start(B2[0][:, :, :].rearrange("p e d -> p (e d)"),
                         B2_D[0].rearrange("e d -> (e d)").partition_broadcast(P)).then_inc(in_moe[0], 16)
            sp.wait_ge(consts, 3)
            for g in (0, 1):
                sp.dma_start(xs_d[g].rearrange("(a p r) d -> p a (r d)", p=P, r=J),
                             H[:, 0:J, :].rearrange("p j d -> p (j d)").unsqueeze(1)
                             .to_broadcast([P, max(NT[0][g], NT[1][g]) // J, J * D]))\
                  .then_inc(xs_zero, 16)

            def load(L, g, q, h, first=False):
                if not first:
                    sp.wait_ge(xt_mm[L], BIAS + q * 4 + (2 * h - 2))
                sp.dma_start(xt[:, 2 * h:2 * h + 2, :], rows(xs_d[g], q * 4 + (2 * h - g * NT[L][0]))).then_inc(ld[L][h], 16)

            def weights(L, e, q, r, first=False):
                if not first:
                    sp.wait_ge(up_mm[L], BIAS + q * 4 + (r - 3))
                sp.dma_start(W1[:, r, :], W1_D[L][bass.ds(e, 1), :, :].rearrange("a d h -> d (a h)")).then_inc(w1_in[L][r], 16)

            def store(L, g, q, h):
                sp.wait_ge(y_ready[L], BIAS + q * 4 + (2 * h + 2))
                sp.dma_start(rows(ys_d[L][g], q * 4 + (2 * h - g * NT[L][0])), yt[:, 2 * h:2 * h + 2, :]).then_inc(st[L][h], 16)

            def rows(scratch, t):
                return scratch[bass.ds(t * P, 2 * P), :].rearrange("(k p) d -> p k d", p=P)

            def fetch(L, g, q, g_a=0, g_b=0, stores=2, first=False):
                e = experts(SP, q)
                load(L, g, q, 0, first)
                weights(L, e[0], q, 0, first)
                weights(L, e[1], q, 1, first)
                if stores == 2:
                    store(L, g_a, q - 2, 1)
                load(L, g, q, 1, first)
                weights(L, e[2], q, 2, first)
                weights(L, e[3], q, 3, first)
                if stores:
                    store(L, g_b, q - 1, 0)

            def keep(L, q):
                sp.wait_ge(hc_ready[L], BIAS + q + 1)
                sp.dma_start(H[:, q * J:(q + 1) * J, :], Hc[:, q % 2, :, :]).then_inc(hkeep[L][q % 2], 16)

            sp.wait_ge(xs_zero, 32)
            for L in (0, 1):
                for q in range(NB - 1):
                    keep(L, q)
                NG, NQ = NT[L][0] // 4, ALL[L] // 4
                sp.wait_ge(route_done, 2 * L + 1)
                sp.wait_ge(scat[L][0], 16 * NC[L][0])
                fetch(L, 0, 0, stores=0, first=True)
                keep(L, NB - 1)
                fetch(L, 0, 1, stores=1)
                with sp.Fori(2, NG, 1) as q:
                    fetch(L, 0, q)
                sp.wait_ge(route_done, 2 * L + 2)
                sp.wait_ge(scat[L][1], 16 * NC[L][1])
                fetch(L, 1, NG)
                fetch(L, 1, NG + 1, 0, 1)
                if L == 0:
                    sp.wait_ge(rows_ready, 2)
                    sp.dma_start(mod_d[1], crow[:, :, :].rearrange("b m d -> b (m d)")).then_inc(mod_out[1], 16)
                fetch(L, 1, NG + 2, 1, 1)
                if L == 0:
                    sp.wait_ge(mod_out[1], 16)
                    load_mods(1)
                with sp.Fori(NG + 3, NQ, 1) as q:
                    fetch(L, 1, q, 1, 1)
                store(L, 1, NQ - 2, 1)
                store(L, 1, NQ - 1, 0)
                store(L, 1, NQ - 1, 1)
                if L == 0:
                    sp.wait_ge(rows_ready, 3)
                    sp.dma_start(b2_d, B2[1][0:1, :, :].rearrange("p e d -> p (e d)")).then_inc(b2_out, 16)
                    sp.wait_ge(b2_out, 16)
                    sp.dma_start(B2[1][:, :, :].rearrange("p e d -> p (e d)"),
                                 b2_d.rearrange("a n -> (a n)").partition_broadcast(P)).then_inc(b2_in, 16)
            for b in range(NB):
                sp.wait_ge(comb_done[1], BIAS + b + 1)
                sp.dma_start(out[b].rearrange("(p j) d -> p j d", j=J), X[:, b * J:(b + 1) * J, :]).then_inc(stored, 16)
            sp.wait_ge(stored, 16 * NB)

        in_moe_all = [2, 1]

        @block.tensor
        def _(pe):
            bias(pe, "pe")
            mm, tr = nc.tensor.matmul, nc.tensor.transpose

            rows_bank = [ps_o[0:NB, 1, :], ps_p[0:NB, 0, :]]

            def setup_products(L):
                pe.wait_ge(consts, 3)
                pe.wait_ge(in_w[L], 16 * 4)
                mm(ps_p[:, 0, 0:D], wsm[L][:, 0, :], wsm[L][:, 1, :], start=True, stop=True)
                tr(ps_p[:, 1, 0:D], wsm[L][:, 2, :], ident[:, :])
                pe.wait_ge(s_dve, 5 * L + 1)
                tr(ps_p[:, 1, D:D + NB], silu_c[:, 2, :], ident[0:NB, 0:NB]).then_inc(s_pe, 1)

            def setup_mods(L):
                pe.wait_ge(s_dve, 5 * L + 2)
                mm(ps_p[:, 1, D + NB:D + 2 * NB], wmod[L][:, D:2 * D], scT[:, :], start=True, stop=True)
                mm(ps_p[:, 1, D + 2 * NB:D + 3 * NB], wmod[L][:, 0:D], scT[:, :], start=True, stop=True).then_inc(s_pe, 1)
                mm(rows_bank[L], scT[:, :], wmod[L][:, 2 * D:6 * D], start=True, stop=True).then_inc(s_pe, 1)

            def setup_rest(L):
                pe.wait_ge(in_small[L], 16 * 4)
                last = tr(ps_p[:, 1, 2 * D:2 * D + E * HC], b1row[:, L, :], ident[0:E * HC, 0:E * HC])
                if L == 0:
                    tr(ps_p[:, 1, 3 * D:4 * D], wsm[0][:, 3, :], ident[:, :])
                    pe.wait_ge(s_dve, 4)
                    k = 2 * D + E * HC
                    tr(ps_p[:, 1, k:k + E], erow[:, 0, :], ident[0:E, 0:E])
                    last = tr(ps_p[:, 1, k + E:k + 2 * E], erow[:, 1, :], ident[0:E, 0:E])
                last.then_inc(s_pe, 1)

            products = H[:, :, :].rearrange("p (e c) d -> p e c d", e=E)

            def constant_rows():
                pe.wait_ge(r_prod, E)
                for h in (0, 1):
                    for c in range(HC):
                        last = mm(ps_p[0:1, h, :].rearrange("p (e d) -> p e d", d=D), onesf[:, 0:1],
                                  products[:, 4 * h:4 * h + 4, c, :], start=(c == 0), stop=(c == HC - 1))
                last.then_inc(s_pe, 1)

            def head_tr(L, b):
                pe.wait_ge(xn_ready[L], BIAS + b + 1)
                pe.wait_ge(v_ready[L], BIAS + b)
                for j in range(J):
                    last = tr(ps_a[:, j * P:(j + 1) * P], xn[:, b % 2, j, :], ident[:, :])
                last.then_inc(h_tr[L], 1)

            def head_g(L, b):
                pe.wait_ge(hT_ready[L], BIAS + b + 1)
                pe.wait_ge(r_ready[L], BIAS + b - 3)
                if L == 0:
                    pe.wait_ge(y_add, BIAS + b - 2)
                mm(ps_b[:, :], A[L][:, :], hT[:, b % 2, :], start=True, stop=True).then_inc(g_mm[L], 1)

            def head_v(L, b):
                pe.wait_ge(hT_ready[L], BIAS + b + 1)
                pe.wait_ge(hT2_ready[L], BIAS + b - 2)
                if L == 1:
                    pe.wait_ge(wg_ready[1], BIAS + b + 1)
                w = WvT[0][:, :] if L == 0 else WG[:, b % 4, :]
                for j in range(J):
                    last = mm(ps_a[:, j * P:(j + 1) * P], hT[:, b % 2, j * P:(j + 1) * P], w, start=True, stop=True)
                last.then_inc(v_mm[L], 1)

            def scores(L, n):
                b, j = n // J, n % J
                if j == 0:
                    pe.wait_ge(gT_ready[L], BIAS + b + 1)
                pe.wait_ge(exp_done[L], BIAS + n - 1)
                mm(ps_s[:, j % 2, :], gT[:, b % 2, j * P:(j + 1) * P], hT[:, b % 2, :], start=True, stop=True).then_inc(s_mm[L], 1)

            def prob_tr(L, n):
                pe.wait_ge(exp_done[L], BIAS + n + 1)
                pe.wait_ge(pt_ready[L], BIAS + n - 1)
                for c in range(J):
                    last = tr(ps_p[:, n % 2, c * P:(c + 1) * P], prob[:, n % 2, c * P:(c + 1) * P], ident[:, :])
                last.then_inc(pt_mm[L], 1)

            def prob_v(L, n):
                b = n // J
                pe.wait_ge(pt_ready[L], BIAS + n + 1)
                if n % J == 0:
                    pe.wait_ge(v_ready[L], BIAS + b + 1)
                pe.wait_ge(o_done[L], BIAS + n - 1)
                for c in range(J):
                    last = mm(ps_o[:, n % 2, 0:D], probT[:, n % 2, c, :], V[:, b % 2, c, :], start=(c == 0), stop=(c == J - 1))
                last.then_inc(pv_mm[L], 1)

            def out_proj(b):
                pe.wait_ge(o_done[0], BIAS + 4 * b + 4)
                pe.wait_ge(wg_ready[0], BIAS + b + 1)
                pe.wait_ge(r_ready[0], BIAS + b)
                pe.wait_ge(gT_ready[0], BIAS + upto(b + 3))
                for j in range(J):
                    last = mm(ps_b[:, j * P:(j + 1) * P], On[:, j, :], WG[:, b % 4, :], start=True, stop=True)
                last.then_inc(y_mm, 1)

            def post_tr(L, q):
                pe.wait_ge(hc_ready[L], BIAS + q + 1)
                pe.wait_ge(v_ready[L], BIAS + upto(q + 3))
                pe.wait_ge(hT_ready[L], BIAS + upto(q + 4))
                for j in range(J):
                    last = tr(ps_a[:, j * P:(j + 1) * P], Hc[:, q % 2, j, :], ident[:, :])
                last.then_inc(p_tr[L], 1)

            def router(L, q):
                pe.wait_ge(hT2_ready[L], BIAS + q + 1)
                pe.wait_ge(gT_ready[L], BIAS + upto(q + 4))
                if L == 0:
                    pe.wait_ge(y_add, BIAS + q + 1)
                w = NR[L]
                for j in range(J):
                    last = mm(ps_b[:, j * w:(j + 1) * w], hT2[:, j * P:(j + 1) * P], RW[L][:, :], start=True, stop=True)
                last.then_inc(r_mm[L], 1)

            def ranks(L, g):
                n = E * NC[L][g]
                pe.wait_ge(m_ready, 2 * L + g + 1)
                if g == 0:
                    pe.wait_ge(r_ready[L], BIAS + FIRST[L][1] + 1 - L)
                    pe.wait_ge(gT_ready[L], BIAS + FIRST[L][1] + RANKS_AT[L][0] + 2)
                    if L == 0:
                        pe.wait_ge(y_add, BIAS + FIRST[0][1] + 2)
                    before, total = ps_b[:, 0:n], ps_b[:, n:2 * n]
                else:
                    before, total = ps_p[:, 0, 0:n], ps_p[:, 1, 0:n]
                mm(before, upper[:, :], Mb[:, 0:n], start=True, stop=True)
                mm(total, ones[:, :], Mb[:, 0:n], start=True, stop=True).then_inc(rank_mm, 1)

            def body(L, b):
                for j in range(J):
                    n = 4 * b + j
                    if j == 1 and b >= 1 and L == 0:
                        out_proj(b - 1)
                    prob_tr(L, n)
                    if n + 2 < NB * J:
                        scores(L, n + 2)
                    if j == 0 and b >= 2:
                        post_tr(L, b - 2)
                    if j == 0 and b == FIRST[L][1] + RANKS_AT[L][0] + 1:
                        pe.wait_ge(rank_read, 2 * L + 1)
                    if j == 0 and b + 1 < NB:
                        head_g(L, b + 1)
                    if n >= 1:
                        prob_v(L, n - 1)
                    if j == 0 and b >= 2:
                        router(L, b - 2)
                    if (b - FIRST[L][1], j) == RANKS_AT[L]:
                        ranks(L, 0)
                    if j == 1 and b + 1 < NB:
                        head_v(L, b + 1)
                    if j == 3 and b + 2 < NB:
                        head_tr(L, b + 2)

            def x_tr(L, q, r):
                if r % 2 == 0:
                    pe.wait_ge(ld[L][r // 2], (q + 1) * 16)
                pe.wait_ge(xT_ready[L], BIAS + q * 4 + r)
                tr(ps_a[:, 0:P], xt[:, r, :], ident[:, :]).then_inc(xt_mm[L], 1)

            def up(L, q, r):
                pe.wait_ge(w1_in[L][r], (q + 1) * 16)
                pe.wait_ge(xT_ready[L], BIAS + q * 4 + (r + 1))
                pe.wait_ge(hTm_ready[L], BIAS + q * 4 + (r - 1))
                for c in range(HC):
                    last = mm(ps_s[:, r % 2, c * P:(c + 1) * P], W1[:, r, c * P:(c + 1) * P], xT[:, r % 2, :], start=True, stop=True)
                last.then_inc(up_mm[L], 1)

            def down(L, q, r, e):
                pe.wait_ge(hTm_ready[L], BIAS + q * 4 + (r + 1))
                pe.wait_ge(y_ready[L], BIAS + q * 4 + (r - 1))
                for c in range(HC):
                    last = mm(ps_o[:, r % 2, 0:D], hTm[:, r % 2, c, :],
                              W2[L][:, bass.ds(e, 1), c, :].rearrange("p a d -> p (a d)"), start=(c == 0), stop=(c == HC - 1))
                last.then_inc(dn_mm[L], 1)

            def quad(L, q, between=(), last=False):
                e = experts(PE, q)
                for r in range(4):
                    if not (last and r >= 2):
                        x_tr(L, q + (r + 2) // 4, (r + 2) % 4)
                    if not (last and r == 3):
                        up(L, q + (r + 1) // 4, (r + 1) % 4)
                    down(L, q, r, e[r])
                    if r < len(between):
                        between[r]()
                    if last and L == 0 and r == 2:
                        pe.wait_ge(xT_ready[0], BIAS + ALL[0])
                        head_tr(1, 0)
                    if last and L == 0 and r == 3:
                        head_g(1, 0)

            setup_products(0)
            setup_mods(0)
            for L in (0, 1):
                NG, NQ = NT[L][0] // 4, ALL[L] // 4
                if L == 0:
                    head_tr(0, 0)
                    head_g(0, 0)
                    setup_rest(0)
                head_v(L, 0)
                scores(L, 0)
                scores(L, 1)
                head_tr(L, 1)
                if L == 0:
                    pe.wait_ge(s_dve, 5)
                for b in range(NB):
                    body(L, b)
                prob_v(L, NB * J - 1)
                post_tr(L, NB - 2)
                router(L, NB - 2)
                if L == 0:
                    out_proj(NB - 1)
                pe.wait_ge(exp_done[L], BIAS + NB * J)
                pe.wait_ge(o_done[L], BIAS + NB * J)
                pe.wait_ge(hT2_ready[L], BIAS + NB - 1)
                pe.wait_ge(in_moe[L], 16 * in_moe_all[L])
                pe.wait_ge(route_done, 2 * L + 1)
                x_tr(L, 0, 0)
                x_tr(L, 0, 1)
                up(L, 0, 0)

                def last_post():
                    pe.wait_ge(xT_ready[L], BIAS + 3)
                    post_tr(L, NB - 1)
                    pe.wait_ge(hT2_ready[L], BIAS + NB)

                quad(L, 0, [last_post, lambda: router(L, NB - 1)])
                quad(L, 1, [lambda: None, lambda: None, lambda: None, lambda: ranks(L, 1)])

                quad(L, 2)
                if L == 0:
                    pe.wait_ge(rank_read, 2)
                    for q, part in enumerate((lambda: setup_products(1), lambda: setup_mods(1), lambda: setup_rest(1))):
                        quad(0, 3 + q)
                        part()
                with pe.Fori(3 + 3 * (1 - L), NG, 1) as q:
                    quad(L, q)
                pe.wait_ge(route_done, 2 * L + 2)
                if L == 0:
                    Q = NQ - GROUPS[0][0] - 2
                    with pe.Fori(NG, Q, 1) as q:
                        quad(0, q)
                    quad(0, Q)
                    constant_rows()
                with pe.Fori(Q + 1 if L == 0 else NG, NQ - 1, 1) as q:
                    quad(L, q)
                quad(L, NQ - 1, last=True)
                if L == 0:
                    pe.wait_ge(y_ready[0], BIAS + ALL[0])

        @block.gpsimd
        def _(pool):
            bias(pool, "pool")
            g = nc.gpsimd
            steps = [0]

            def link(ins):
                steps[0] += 1
                ins.then_inc(pool_chain, 1)
                pool.wait_ge(pool_chain, steps[0])

            g.memset(H[:, 0:J, :], 0.0).then_inc(consts, 1)
            link(g.memset(ident[:, :], 0.0))
            link(g.affine_select(out=ident[:, :], in_=ident[:, :], compare_op=ALU.not_equal, fill=1.0, base=0,
                                 pattern=[[-1, P]], channel_multiplier=1))
            link(g.memset(ones[:, :], 1.0))
            link(g.affine_select(out=upper[:, :], in_=ones[:, :], compare_op=ALU.is_gt, fill=0.0, base=0,
                                 pattern=[[1, P]], channel_multiplier=-1))
            kw = dict(channel_multiplier=0, allow_small_or_imprecise_dtypes=True)
            link(g.iota(rev8[:, :], pattern=[[-1, E]], base=E, **kw))
            link(g.iota(up8[:, :], pattern=[[1, E]], base=1, **kw))
            link(g.iota(thr16[:, :], pattern=[[P, MAX_GT]], base=0, **kw))
            link(g.iota(iotaT[:, :], pattern=[[1, MAX_NT]], base=0, **kw))
            link(g.memset(onesf[:, :], 1.0))
            for L in (0, 1):
                for k in (0, 1):
                    link(g.memset(run[L][k][:, :], 1.0))
                    last = g.memset(run[L][k][:, :].rearrange("p (e c) -> p e c", e=E)[:, :, 0:1], 0.0)
                last.then_inc(consts, 1)

            def normalise(L, b):
                u = b % 2
                pool.wait_ge(ln1_ready[L], BIAS + b + 1)
                pool.wait_ge(h_tr[L], BIAS + b - 1)

                def wide(stat):
                    return stat.unsqueeze(2).to_broadcast([P, J, D])

                g.tensor_tensor(xn[:, u, :, :], X[:, b * J:(b + 1) * J, :], wide(rdev[:, 1, b + 3 - LEAD[L], :]), ALU.mult).then_inc(xn_chain[L], 1)
                pool.wait_ge(xn_chain[L], b + 1)
                g.tensor_tensor(xn[:, u, :, :], xn[:, u, :, :], wide(nb[:, 1, b + 3 - LEAD[L], :]), ALU.add).then_inc(xn_ready[L], 1)

            def scale_weights(L, b):
                pool.wait_ge([y_mm, v_mm[1]][L], BIAS + b - 3)
                g.tensor_tensor(WG[:, b % 4, :], [woT, WvT[1]][L][:, :], MB[:, b, 0, :], ALU.mult).then_inc(wg_ready[L], 1)

            def scatter(L, grp):
                pool.wait_ge(route_done, 2 * L + grp + 1)
                for u in (0, 1):
                    pool.wait_ge(hkeep[L][u], 16 + 16 * ((FIRST[L][grp] + GROUPS[L][grp] + 1 - u) // 2))
                if L == 0 and grp == 0:
                    pool.wait_ge(xs_zero, 32)
                for c in range(NC[L][grp]):
                    g.indirect_dma_start(out=xs_d[grp], out_offset=bass.IndirectOffsetOnAxis(ap=slot[:, grp, c:c + 1], axis=0),
                                         in_=H[:, FIRST[L][grp] * J + c % GT[L][grp], :], in_offset=None).then_inc(scat[L][grp], 16)

            def gather(L, t):
                grp = int(t >= GT[L][0])
                if t >= RING:
                    pool.wait_ge(rows_used[L], (t - RING) // J + 1)
                for k in range(TOPK[L]):
                    c = t - FIRST[L][grp] * J + k * GT[L][grp]
                    g.indirect_dma_start(out=yg[:, t % RING, k, :], out_offset=None, in_=ys_d[L][grp],
                                         in_offset=bass.IndirectOffsetOnAxis(ap=slot[:, grp, c:c + 1], axis=0)).then_inc(gat[t % RING], 16)

            def stored_rows(L, grp):
                for h in (0, 1):
                    pool.wait_ge(st[L][h], 16 + 16 * (sum(NT[L][0:grp + 1]) // 4))

            pool.wait_ge(in_x[0], 16)
            normalise(0, 0)
            normalise(0, 1)
            for L in (0, 1):
                if L == 1:
                    normalise(1, 0)
                    normalise(1, 1)
                    pool.wait_ge(mod_in[1], 32)
                    scale_weights(1, 0)
                    scale_weights(1, 1)
                    stored_rows(0, 1)
                    for t in range(GT[0][0], GT[0][0] + J):
                        gather(0, t)
                for b in range(NB):
                    left = range(NB * J)[GT[0][0] + b * J + J:][:J] if L == 1 else ()
                    for t in left[:2]:
                        gather(0, t)
                    if b + 2 < NB:
                        normalise(L, b + 2)
                    if L == 0 and b == 0:
                        pool.wait_ge(mod_in[0], 32)
                        pool.wait_ge(s_dve, 5)
                        for k in range(3):
                            scale_weights(0, k)
                    if L == 0 and b + 3 < NB:
                        scale_weights(0, b + 3)
                    if L == 1 and b + 2 < NB:
                        scale_weights(1, b + 2)
                    for t in left[2:]:
                        gather(0, t)
                    if b == FIRST[L][1] + 2 + (L == 0):
                        scatter(L, 0)
                scatter(L, 1)
                if L == 0:
                    for k in (0, 1):
                        pool.wait_ge(scat[0][k], 16 * NC[0][k])
                    pool.wait_ge(in_moe[1], 16)
                    pool.wait_ge(s_dve, 10)
                    for e in range(E):
                        g.tensor_tensor(H[:, e * HC:(e + 1) * HC, :], W2[1][:, e, :, :],
                                        relu_b1[:, e * HC:(e + 1) * HC].unsqueeze(2).to_broadcast([P, HC, D]), ALU.mult).then_inc(r_prod, 1)
                stored_rows(L, 0)
                for t in range(GT[L][0]):
                    gather(L, t)
                if L == 1:
                    stored_rows(1, 1)
                    for c in range(GT[1][1]):
                        g.indirect_dma_start(out=H[:, c, :], out_offset=None, in_=ys_d[1][1],
                                             in_offset=bass.IndirectOffsetOnAxis(ap=slot[:, 1, c:c + 1], axis=0)).then_inc(gat_end[c], 16)

        @block.scalar
        def _(act):
            bias(act, "act")
            fn = nc.scalar.activation

            def evac(out_, in_):
                return fn(out_, in_, ACT.Copy)

            def setup(L):
                act.wait_ge(in_c[L], 16)
                fn(silu_c[:, 0, :], crow[:, 0, :], ACT.Exp, scale=-1.0).then_inc(s_act, 1)

            def head_h(L, b):
                act.wait_ge(h_tr[L], BIAS + b + 1)
                src = ps_a[:, :].rearrange("p (j t) -> p j t", j=J)
                dst = hT[:, b % 2, :].rearrange("p (t j) -> p j t", j=J) if L == 0 else hT[:, b % 2, :].rearrange("p (j t) -> p j t", j=J)
                fn(dst, src, ACT.Identity, bias=saT[L][:, b:b + 1], scale=caT[L][:, b:b + 1]).then_inc(hT_ready[L], 1)

            def head_g(L, b):
                act.wait_ge(g_mm[L], BIAS + b + 1)
                evac(gT[:, b % 2, :], ps_b[:, :]).then_inc(gT_ready[L], 1)

            def head_v(L, b):
                act.wait_ge(v_mm[L], BIAS + b + 1)
                evac(V[:, b % 2, :, :], ps_a[:, :].rearrange("p (j d) -> p j d", j=J)).then_inc(v_ready[L], 1)

            def exps(L, n):
                act.wait_ge(negm_ready[L], BIAS + n + 1)
                act.wait_ge(pt_mm[L], BIAS + n - 1)
                k = n % 8
                fn(prob[:, n % 2, :], ps_s[:, n % 2, :], ACT.Exp, bias=negm[:, k:k + 1],
                   accum_out=rowsum[:, k:k + 1]).then_inc(exp_done[L], 1)

            def prob_out(L, n):
                act.wait_ge(pt_mm[L], BIAS + n + 1)
                act.wait_ge(pv_mm[L], BIAS + n - 1)
                evac(probT[:, n % 2, :, :], ps_p[:, n % 2, :].rearrange("p (c q) -> p c q", c=J)).then_inc(pt_ready[L], 1)

            def attn_out(n):
                act.wait_ge(pv_mm[0], BIAS + n + 1)
                act.wait_ge(rinv_ready[0], BIAS + n + 1)
                if n % J == 0:
                    act.wait_ge(y_mm, BIAS + n // J)
                k = n % 8
                fn(On[:, n % J, :], ps_o[:, n % 2, 0:D], ACT.Copy, scale=rinv[:, k:k + 1]).then_inc(o_done[0], 1)

            def post(L, q):
                act.wait_ge(p_tr[L], BIAS + q + 1)
                act.wait_ge(r_mm[L], BIAS + q)
                evac(hT2[:, :], ps_a[:, :]).then_inc(hT2_ready[L], 1)

            def normalise(q):
                act.wait_ge(ln2_ready, q + 1)
                act.wait_ge(p_tr[1], BIAS + q - 1)
                act.wait_ge(hkeep[1][q % 2], 16 + 16 * (q // 2))
                for j in range(J):
                    last = fn(Hc[:, q % 2, j, :], X[:, q * J + j, :], ACT.Identity,
                              bias=nb[:, 0, q + 4, j:j + 1], scale=rdev[:, 0, q + 4, j:j + 1])
                last.then_inc(hn_ready, 1)

            def scale_rows(b):
                if b >= 1:
                    act.wait_ge(rows_used[0], b)
                    act.wait_ge(comb_done[0], BIAS + b)
                else:
                    act.wait_ge(weights_ready, 1)
                if b == FIRST[0][1]:
                    act.wait_ge(weights_ready, 2)
                for j in range(J):
                    t = b * J + j
                    act.wait_ge(gat[t % RING], gathered(0, t))
                    last = fn(acc[:, j, :], yg[:, t % RING, 0, :], ACT.Copy, scale=weight[:, 0, t:t + 1])
                last.then_inc(scaled, 1)

            def squares(q):
                act.wait_ge(hc_ready[0], BIAS + q + 1)
                for j in range(J):
                    last = fn(sq[:, j, :], Hc[:, q % 2, j, :], ACT.Square, accum_out=var[:, 2, q + 5, j:j + 1])
                last.then_inc(sq_ready, 1)

            def body(L, b):
                for j in range(J):
                    n = 4 * b + j
                    prob_out(L, n)
                    if L == 0 and b == FIRST[0][1] + 2 and j == 3:
                        top2_exp(0)
                    if j == 0 and b >= 2:
                        post(L, b - 2)
                    if n + 2 < NB * J:
                        exps(L, n + 2)
                    if j == 0 and b + 1 < NB:
                        head_g(L, b + 1)
                    if L == 0 and j == 0 and b >= 2:
                        squares(b - 2)
                    if L == 0 and n >= 1:
                        attn_out(n - 1)
                    if j == 1 and b + 1 < NB:
                        head_v(L, b + 1)
                    if L == 1 and j == 1 and b + FIRST[0][1] < NB:
                        scale_rows(b + FIRST[0][1])
                    if L == 1 and j == 2 and b >= 1:
                        normalise(b - 1)
                    if j == 3 and b + 2 < NB:
                        head_h(L, b + 2)

            def x_out(L, q, r):
                act.wait_ge(xt_mm[L], BIAS + q * 4 + (r + 1))
                act.wait_ge(up_mm[L], BIAS + q * 4 + (r - 1))
                evac(xT[:, r % 2, :], ps_a[:, 0:P]).then_inc(xT_ready[L], 1)

            def hidden(L, q, r, e):
                act.wait_ge(up_mm[L], BIAS + q * 4 + (r + 1))
                act.wait_ge(dn_mm[L], BIAS + q * 4 + (r - 1))
                for c in range(HC):
                    last = fn(hTm[:, r % 2, c, :], ps_s[:, r % 2, c * P:(c + 1) * P], ACT.Gelu if L == 0 else ACT.Relu,
                              bias=b1T[L][:, bass.ds(e * HC + c, 1)])
                last.then_inc(hTm_ready[L], 1)

            def quad(L, q, between=(), last=False):
                e = experts(Activation, q)
                for r in range(4):
                    hidden(L, q, r, e[r])
                    if not (last and r >= 2):
                        x_out(L, q + (r + 2) // 4, (r + 2) % 4)
                    if r < len(between):
                        between[r]()
                    if last and L == 0 and r == 2:
                        act.wait_ge(s_dve, 8)
                        head_h(1, 0)
                    if last and L == 0 and r == 3:
                        head_g(1, 0)

            def top2_exp(g):
                act.wait_ge(gap_ready, g + 1)
                n = GT[0][g]
                fn(row[:, 5, 0:n], row[:, 4, 0:n], ACT.Exp).then_inc(gap_exp, 1)

            setup(0)
            for L in (0, 1):
                if L == 0:
                    act.wait_ge(s_dve, 3)
                    head_h(0, 0)
                    head_g(0, 0)
                head_v(L, 0)
                exps(L, 0)
                exps(L, 1)
                head_h(L, 1)
                for b in range(NB):
                    body(L, b)
                if L == 0:
                    attn_out(NB * J - 1)
                post(L, NB - 2)
                if L == 0:
                    squares(NB - 2)
                    setup(1)
                act.wait_ge(route_done, 2 * L + 1)
                x_out(L, 0, 0)
                x_out(L, 0, 1)
                quad(L, 0, [lambda: post(L, NB - 1), lambda: squares(NB - 1) if L == 0 else None])
                quad(L, 1)
                quad(L, 2, [lambda: top2_exp(1)] if L == 0 else ())
                NG, NQ = NT[L][0] // 4, ALL[L] // 4
                with act.Fori(3, NG, 1) as q:
                    quad(L, q)
                act.wait_ge(route_done, 2 * L + 2)
                if L == 0:
                    CQ = NQ - 2 * GROUPS[0][0] - 1
                    with act.Fori(NG, CQ, 1) as q:
                        quad(0, q)
                    for b in range(GROUPS[0][0]):
                        quad(0, CQ + b, [lambda: scale_rows(b)])
                with act.Fori(CQ + GROUPS[0][0] if L == 0 else NG, NQ - 1, 1) as q:
                    quad(L, q)
                quad(L, NQ - 1, last=True)

        @block.vector
        def _(dve):
            bias(dve, "dve")
            v = nc.vector
            steps = [0]

            def link(ins):
                steps[0] += 1
                ins.then_inc(chain, 1)
                dve.wait_ge(chain, steps[0])

            def rsqrt(x, y, t, out_, step):
                step(v.tensor_scalar(y.bitcast(I32), x.bitcast(I32), -0.5, float(MAGIC), ALU.mult, ALU.add))
                for k in range(3):
                    step(v.tensor_tensor(t, y, y, ALU.mult))
                    step(v.scalar_tensor_tensor(t, t, -0.5, x, ALU.mult, ALU.mult))
                    step(v.scalar_tensor_tensor(out_ if k == 2 else y, t, 1.5, y, ALU.add, ALU.mult))

            def silu(L):
                dve.wait_ge(s_act, L + 1)
                link(v.tensor_scalar(silu_c[:, 0, :], silu_c[:, 0, :], 1.0, None, ALU.add))
                link(v.reciprocal(silu_c[:, 1, :], silu_c[:, 0, :]))
                v.tensor_tensor(silu_c[:, 2, :], crow[:, 0, :], silu_c[:, 1, :], ALU.mult).then_inc(s_dve, 1)

            def products_out(L):
                dve.wait_ge(s_pe, 4 * L + 1)
                v.tensor_copy(scT[:, :], ps_p[:, 1, D:D + NB])
                v.tensor_scalar(A[L][:, :], ps_p[:, 0, 0:D], SCALE[L], None, ALU.mult)
                v.tensor_copy(WvT[L][:, :], ps_p[:, 1, 0:D]).then_inc(s_dve, 1)

            def mod_columns(L):
                dve.wait_ge(s_pe, 4 * L + 2)
                v.tensor_scalar(caT[L][:, :], ps_p[:, 1, D + NB:D + 2 * NB], 1.0, None, ALU.add)
                v.tensor_copy(saT[L][:, :], ps_p[:, 1, D + 2 * NB:D + 3 * NB]).then_inc(s_dve, 1)

            def mod_rows(L, half):
                rows = [ps_o[0:NB, 1, :], ps_p[0:NB, 0, :]][L]
                if half == 0:
                    dve.wait_ge(s_pe, 4 * L + 3)
                    if L == 1:
                        dve.wait_ge(mod_out[0], 16)
                    v.tensor_scalar(crow[:, 1, :], rows[:, 2 * D:3 * D], 1.0, None, ALU.add)
                    v.tensor_copy(crow[:, 2, :], rows[:, D:2 * D])
                m, src = ((0, rows[:, 0:D]), (3, rows[:, 3 * D:4 * D]))[half]
                link(v.tensor_copy(crow[:, m, :], src))
                link(v.scalar_tensor_tensor(gate[:, 0, :], crow[:, m, :], -1.0, crow[:, m, :], ALU.mult, ALU.max))
                link(v.tensor_scalar(gate[:, 0, :], gate[:, 0, :], 0.25, None, ALU.max))
                link(v.tensor_scalar(gate[:, 1, :], crow[:, m, :], 0.0, 2.0, ALU.is_ge, ALU.mult))
                last = v.scalar_tensor_tensor(crow[:, m, :], gate[:, 1, :], -1.0, gate[:, 0, :], ALU.add, ALU.mult)
                if half == 0:
                    link(last)
                else:
                    last.then_inc(rows_ready, 1)
                    dve.wait_ge(rows_ready, L + 1)

            def expert_norms():
                dve.wait_ge(in_small[0], 16 * 4)
                link(v.tensor_tensor(erow[:, 1, :], erow[:, 0, :], erow[:, 0, :], ALU.mult))
                link(v.tensor_reduce(nte[:, 0:1], erow[:, 1, :], AX.X, ALU.add))
                rsqrt(nte[:, 0:1], nte[:, 1:2], nte[:, 2:3], nte[:, 3:4], link)
                link(v.tensor_tensor(nte[:, 4:5], nte[:, 3:4], nte[:, 0:1], ALU.mult))
                link(v.tensor_scalar(nte[:, 5:6], nte[:, 4:5], NORM_EPS, None, ALU.add))
                link(v.reciprocal(nte[:, 6:7], nte[:, 5:6]))
                v.tensor_scalar(erow[:, 1, :], erow[:, 0, :], nte[:, 6:7], None, ALU.mult).then_inc(s_dve, 1)

            def rest_out(L):
                dve.wait_ge(s_pe, 4 * L + 4)
                k = 2 * D + E * HC
                if L == 0:
                    v.tensor_copy(woT[:, :], ps_p[:, 1, 3 * D:4 * D])
                    v.tensor_copy(RW[0][:, :], ps_p[:, 1, k:k + 2 * E])
                else:
                    v.tensor_scalar(relu_b1[:, :], ps_p[:, 1, 2 * D:k], 0.0, None, ALU.max)
                v.tensor_copy(b1T[L][:, :], ps_p[:, 1, 2 * D:k]).then_inc(s_dve, 1 + L)

            def constant_rows(part):
                b2, r = B2[1][0:1, :, :], ps_p[0:1, :, :].rearrange("p a (e d) -> p (a e) d", d=D)
                if part == 0:
                    dve.wait_ge(s_pe, 9)
                    link(v.tensor_reduce(rrow[:, 0, :], r.rearrange("p e d -> p d e"), AX.X, ALU.add))
                elif part == 1:
                    dve.wait_ge(in_small[1], 16 * 4)
                    link(v.tensor_reduce(rrow[:, 1, :], b2.rearrange("p e d -> p d e"), AX.X, ALU.add))
                    link(v.tensor_tensor(rrow[:, 0, :], rrow[:, 0, :], rrow[:, 1, :], ALU.add))
                else:
                    v.tensor_tensor(b2, rrow[:, 0:1, :].to_broadcast([1, E, D]), r, ALU.subtract).then_inc(rows_ready, 1)

            def tile(ap, n):
                return ap[:, bass.ds(n, 1), :].rearrange("p a d -> p (a d)")

            def mean_var(kind, b, body):
                for j in range(J):
                    last = v.bn_stats(stats[:, kind, body % 2, j, :], X[:, b * J + j, :])
                link(last)
                for j in range(J):
                    last = v.bn_aggr(mv[:, kind, body + 3, j, :], stats[:, kind, body % 2, j, :])
                link(last)

            def ln1_stats(L, b):
                if L == 0:
                    dve.wait_ge(in_x[b], 16)
                else:
                    dve.wait_ge(comb_done[0], BIAS + b + 1)
                mean_var(1, b, b - LEAD[L])

            def ln2_stats(L, q):
                dve.wait_ge(*((y_add, BIAS + q + 1) if L == 0 else (o_done[1], BIAS + 4 * q + 4)))
                mean_var(0, q, q + 1)

            def deviations(L, body, ln2, ln1, norm):
                c = body + 3
                for kind, there in ((0, ln2), (1, ln1)):
                    if there:
                        link(v.tensor_scalar(var[:, kind, c, :], mv[:, kind, c, :, 1], LN_EPS, None, ALU.add))
                if norm:
                    dve.wait_ge(sq_ready, BIAS + body - 1)
                kinds = slice([k for k in (0, 1, 2) if (ln2, ln1, norm)[k]][0], 3 if norm else 2 if ln1 else 1)
                rsqrt(var[:, kinds, c, :], newton[:, 0, kinds, :], newton[:, 1, kinds, :], rdev[:, kinds, c, :], link)
                for kind, there, ready in ((0, ln2 and L == 1, ln2_ready), (1, ln1, ln1_ready[L])):
                    if there:
                        v.scalar_tensor_tensor(nb[:, kind, c, :], mv[:, kind, c, :, 0], -1.0, rdev[:, kind, c, :],
                                               ALU.mult, ALU.mult).then_inc(ready, 1)

            def ln1(L, b):
                ln1_stats(L, b)
                deviations(L, b - LEAD[L], False, True, False)

            def moe_input(L, q):
                if L == 0 and q == 0:
                    dve.wait_ge(mod_in[0], 32)
                u = q % 2
                if L == 0 or q == NB - 1:
                    dve.wait_ge(p_tr[L], BIAS + q - 1)
                    if L == 0:
                        dve.wait_ge(sq_ready, BIAS + q - 1)
                    dve.wait_ge(hkeep[L][u], 16 + 16 * (q // 2))
                    for j in range(J):
                        last = v.scalar_tensor_tensor(Hc[:, u, j, :], X[:, q * J + j, :], mv[:, 0, q + 4, j, 0:1], MB[:, q, 1, :],
                                                      ALU.subtract, ALU.mult)
                    link(last)
                    for j in range(J):
                        last = v.scalar_tensor_tensor(Hc[:, u, j, :], Hc[:, u, j, :], rdev[:, 0, q + 4, j:j + 1], MB[:, q, 2, :],
                                                      ALU.mult, ALU.add)
                    last.then_inc(hc_ready[L], 1)
                    return
                dve.wait_ge(hn_ready, q + 1)
                h = Hc[:, u, :, :]
                link(v.tensor_tensor(h, h, MB[:, q, 1, :].unsqueeze(1).to_broadcast([P, J, D]), ALU.mult))
                v.tensor_tensor(h, h, MB[:, q, 2, :].unsqueeze(1).to_broadcast([P, J, D]), ALU.add).then_inc(hc_ready[L], 1)

            def row_max(L, n):
                dve.wait_ge(s_mm[L], BIAS + n + 1)
                k = n % 8
                v.tensor_reduce(negm[:, k:k + 1], ps_s[:, n % 2, :], AX.X, ALU.max, negate=True).then_inc(negm_ready[L], 1)

            def row_scale(L, n):
                dve.wait_ge(exp_done[L], BIAS + n + 1)
                k = n % 8
                v.reciprocal(rinv[:, k:k + 1], rowsum[:, k:k + 1]).then_inc(rinv_ready[L], 1)

            def attn_out(n):
                dve.wait_ge(pv_mm[1], BIAS + n + 1)
                dve.wait_ge(rinv_ready[1], BIAS + n + 1)
                k = n % 8
                v.scalar_tensor_tensor(X[:, n, :], ps_o[:, n % 2, 0:D], rinv[:, k:k + 1], X[:, n, :],
                                       ALU.mult, ALU.add).then_inc(o_done[1], 1)

            def y_out(b):
                dve.wait_ge(y_mm, BIAS + b + 1)
                xb = X[:, b * J:(b + 1) * J, :]
                v.tensor_tensor(xb, ps_b[:, :].rearrange("p (j d) -> p j d", j=J), xb, ALU.add).then_inc(y_add, 1)

            def router_out(L, q):
                dve.wait_ge(r_mm[L], BIAS + q + 1)
                v.tensor_copy(sims[:, q * J:(q + 1) * J, 0:NR[L]],
                              ps_b[:, 0:J * NR[L]].rearrange("p (j e) -> p j e", j=J)).then_inc(r_ready[L], 1)

            def combine(L, b, part):
                T = slice(b * J, (b + 1) * J)
                ring = slice(b * J % RING, b * J % RING + J)
                gb = GBB[L][:, b, :].unsqueeze(1).to_broadcast([P, J, D])
                if part == 0 and L == 0:
                    dve.wait_ge(scaled, b + 1)
                    for j in range(J):
                        last = v.scalar_tensor_tensor(acc[:, j, :], yg[:, b * J % RING + j, 1, :],
                                                      weight[:, 1, b * J + j:b * J + j + 1], acc[:, j, :], ALU.mult, ALU.add)
                    last.then_inc(rows_used[0], 1)
                elif part == 0:
                    for j in range(J):
                        dve.wait_ge(gat[(b * J + j) % RING], gathered(1, b * J + j))
                    v.tensor_tensor(acc[:, :, :], yg[:, ring, 0, :], gb, ALU.mult).then_inc(rows_used[1], 1)
                else:
                    dve.wait_ge(rows_used[L], b + 1)
                    if L == 0:
                        link(v.tensor_tensor(acc[:, :, :], acc[:, :, :], gb, ALU.mult))
                    v.tensor_tensor(X[:, T, :], X[:, T, :], acc[:, :, :], ALU.add).then_inc(comb_done[L], 1)

            def route(L, g, part):
                n, C = GT[L][g], NC[L][g]
                N = E * C
                T = slice(FIRST[L][g] * J, FIRST[L][g] * J + n)
                done = FIRST[L][g] + GROUPS[L][g]
                three = [P, n, E]
                Mv = M[:, 0:N].rearrange("p (e c) -> p c e", e=E)
                sc, tmp = score[:, 0:n, :], rtmp[:, 0:n, :]

                def r_(k):
                    return row[:, k, 0:n]

                def over_e(x):
                    return x.unsqueeze(2).to_broadcast(three)

                def over_t(x):
                    return x.unsqueeze(1).to_broadcast(three)

                def best(k, to):
                    link(v.tensor_reduce(r_(to), sc, AX.X, ALU.max))
                    link(v.tensor_tensor(tmp, sc, over_e(r_(to)), ALU.is_equal))
                    link(v.tensor_tensor(tmp, tmp, over_t(rev8[:, :]), ALU.mult))
                    link(v.tensor_reduce(r_(1), tmp, AX.X, ALU.max))
                    link(v.tensor_tensor(Mv[:, k * n:(k + 1) * n, :], over_t(rev8[:, :]), over_e(r_(1)), ALU.is_equal))

                if part == 0 and L == 0:
                    if g == 1:
                        deviations(0, NB + 1, False, False, True)
                    cols = slice(FIRST[0][g] + 5, done + 5)
                    ss, rs = [x[:, 2, cols, :].rearrange("p b j -> p (b j)") for x in (var, rdev)]
                    link(v.tensor_tensor(r_(3), ss, rs, ALU.mult))
                    link(v.tensor_scalar(r_(3), r_(3), NORM_EPS, None, ALU.add))
                    link(v.reciprocal(r_(2), r_(3)))
                elif part == 1 and L == 0:
                    dve.wait_ge(r_ready[0], BIAS + done)
                    raw, cosn = sims[:, T, 0:E], sims[:, T, E:2 * E]
                    link(v.tensor_tensor(sc, cosn, over_e(r_(2)), ALU.mult))
                    link(v.scalar_tensor_tensor(sc, over_t(bonus[:, :]), CACHE_BONUS, sc, ALU.mult, ALU.add))
                    link(v.tensor_reduce(r_(0), raw, AX.X, ALU.min))
                    link(v.tensor_tensor(tmp, raw, over_e(r_(0)), ALU.is_equal))
                    link(v.tensor_tensor(tmp, tmp, over_t(up8[:, :]), ALU.mult))
                    link(v.tensor_reduce(r_(1), tmp, AX.X, ALU.max))
                    link(v.tensor_tensor(tmp, over_t(up8[:, :]), over_e(r_(1)), ALU.is_equal))
                    link(v.scalar_tensor_tensor(sc, tmp, -BIG, sc, ALU.mult, ALU.add))
                elif part == 1:
                    dve.wait_ge(r_ready[1], BIAS + done)
                    link(v.tensor_tensor(sc, sims[:, T, 0:E], over_t(brB[:, :]), ALU.add))
                elif part == 2:
                    best(0, 2)
                elif part == 3:
                    if L == 0:
                        link(v.scalar_tensor_tensor(sc, Mv[:, 0:n, :], -BIG, sc, ALU.mult, ALU.add))
                        best(1, 3)
                        v.tensor_tensor(r_(4), r_(3), r_(2), ALU.subtract).then_inc(gap_ready, 1)
                    v.tensor_copy(Mb[:, 0:N], M[:, 0:N]).then_inc(m_ready, 1)
                elif part == 4:
                    dve.wait_ge(rank_mm, 2 * L + g + 1)
                    before, total = (ps_b[:, 0:N], ps_b[:, N:2 * N]) if g == 0 else (ps_p[:, 0, 0:N], ps_p[:, 1, 0:N])
                    link(v.tensor_copy(tot[:, 0:N], total))
                    link(v.tensor_tensor_scan(cum[:, 0:N], run[L][g][:, :], tot[:, 0:N], 0.0, ALU.mult, ALU.add))
                    link(v.tensor_tensor(tot[:, 0:N], cum[:, 0:N], tot[:, 0:N], ALU.subtract))
                    v.tensor_tensor(tot[:, 0:N], tot[:, 0:N], before, ALU.add).then_inc(rank_read, 1)
                    dve.wait_ge(rank_read, 2 * L + g + 1)
                elif part == 5:
                    n_e = cum[:, 0:N].rearrange("p (e c) -> p e c", e=E)[:, :, C - 1:C]
                    cnt = cmpt[:, 0:n, :].rearrange("p t e -> p (t e)").rearrange("p (e t) -> p e t", e=E)
                    link(v.tensor_tensor(cnt, n_e.to_broadcast([P, E, n]),
                                         thr16[:, 0:n].unsqueeze(1).to_broadcast([P, E, n]), ALU.is_gt))
                    link(v.tensor_reduce(exs[:, 0, :], cnt, AX.X, ALU.add))
                    link(v.tensor_tensor_scan(exs[:, 1, :], onesf[:, :], exs[:, 0, :], 0.0, ALU.mult, ALU.add))
                    link(v.tensor_tensor(exs[:, 2, :], exs[:, 1, :], exs[:, 0, :], ALU.subtract))
                    link(v.tensor_scalar(exs[:, 2, :], exs[:, 2, :], float(P), None, ALU.mult))
                    tv = tot[:, 0:N].rearrange("p (e c) -> p e c", e=E)
                    link(v.tensor_tensor(tv, tv, exs[:, 2, :].unsqueeze(2).to_broadcast([P, E, C]), ALU.add))
                    link(v.tensor_tensor(tot[:, 0:N], tot[:, 0:N], M[:, 0:N], ALU.mult))
                    link(v.tensor_reduce(slotf[:, 0:C], tot[:, 0:N].rearrange("p (e c) -> p c e", e=E), AX.X, ALU.add))
                    link(v.tensor_copy(slot[:, g, 0:C], slotf[:, 0:C]))
                elif part == 6:
                    w, first = NT[L][g], sum(NT[L][0:g])
                    link(v.tensor_tensor(cmpt[:, 0:w, :], exs[:, 1, :].unsqueeze(1).to_broadcast([P, w, E]),
                                         iotaT[:, 0:w].unsqueeze(2).to_broadcast([P, w, E]), ALU.is_le))
                    link(v.tensor_reduce(eidf[:, 0:w], cmpt[:, 0:w, :], AX.X, ALU.add))
                    v.tensor_scalar(eid[:, first:first + w], eidf[:, 0:w], float(E - 1), None, ALU.min).then_inc(route_done, 1)
                    dve.wait_ge(route_done, 2 * L + g + 1)
                elif part == 7 and L == 0:
                    dve.wait_ge(gap_exp, g + 1)
                    link(v.tensor_scalar(r_(6), r_(5), 1.0, None, ALU.add))
                    link(v.reciprocal(weight[:, 0, T], r_(6)))
                    v.tensor_tensor(weight[:, 1, T], weight[:, 0, T], r_(5), ALU.mult).then_inc(weights_ready, 1)

            def body(L, b):
                after = 1 - L
                for j in range(J):
                    n = 4 * b + j
                    row_scale(L, n)
                    if n + 2 < NB * J:
                        row_max(L, n + 2)
                    if L == 1 and n >= 1:
                        attn_out(n - 1)
                    if j == 0 and b >= 2:
                        router_out(L, b - 2)
                    with_ln1 = b + LEAD[L] < NB and (L == 0 or b + LEAD[1] >= FIRST[0][1])
                    if j == 0 and with_ln1:
                        ln1_stats(L, b + LEAD[L])
                    if j == after and b >= 1:
                        if L == 0:
                            y_out(b - 1)
                        ln2_stats(L, b - 1)
                    if j == after + 1 and (b >= 1 or with_ln1):
                        deviations(L, b, b >= 1, with_ln1, L == 0 and b >= 2)
                    if L == 1 and j >= 2 and b + FIRST[0][1] < NB:
                        combine(0, b + FIRST[0][1], j - 2)
                    if L == 1 and j == 3 and b >= 1:
                        moe_input(1, b - 1)
                    if L == 0 and j == 3 and b >= 1:
                        moe_input(0, b - 1)
                    for part, at in enumerate(ROUTE_AT[L]):
                        if (b - FIRST[L][1], j) == at:
                            route(L, 0, part)

            def expert_out(L, q, r, e):
                dve.wait_ge(dn_mm[L], BIAS + q * 4 + (r + 1))
                if r % 2 == 0:
                    dve.wait_ge(st[L][r // 2], 16 + q * 16)
                v.tensor_tensor(yt[:, r, :], ps_o[:, r % 2, 0:D], tile(B2[L], e), ALU.add).then_inc(y_ready[L], 1)

            def quad(L, q, between=()):
                e = experts(DVE, q)
                for r in range(4):
                    expert_out(L, q, r, e[r])
                    if r < len(between):
                        between[r]()

            link(v.memset(var[:, :, :, :], 1.0))
            silu(0)
            ln1(0, 0)
            products_out(0)
            mod_columns(0)
            ln1(0, 1)
            expert_norms()
            rest_out(0)
            for L in (0, 1):
                NQ = ALL[L] // 4
                CQ = NQ - GROUPS[L][0] - 1 if L == 1 else NQ - 2 * GROUPS[0][0] - 1
                row_max(L, 0)
                row_max(L, 1)
                if L == 0:
                    mod_rows(0, 0)
                    mod_rows(0, 1)
                    ln1(0, 2)
                for b in range(NB):
                    body(L, b)
                if L == 1:
                    attn_out(NB * J - 1)
                router_out(L, NB - 2)
                if L == 0:
                    y_out(NB - 1)
                ln2_stats(L, NB - 1)
                deviations(L, NB, True, False, L == 0)
                moe_input(L, NB - 1)
                dve.wait_ge(in_moe[L], 16 * in_moe_all[L])
                if L == 1:
                    dve.wait_ge(b2_in, 16)
                quad(L, 0, [lambda: None, lambda: None, lambda: (router_out(L, NB - 1), route(L, 1, 0)), lambda: route(L, 1, 1)])
                quad(L, 1, [lambda: route(L, 1, 2), lambda: route(L, 1, 3)])
                quad(L, 2, [lambda: route(L, 1, 4), lambda: (route(L, 1, 5), route(L, 1, 6)), lambda: None, lambda: route(L, 1, 7)])
                if L == 0:
                    quad(0, 3, [lambda: silu(1)])
                    quad(0, 4, [lambda: products_out(1)])
                    quad(0, 5, [lambda: mod_columns(1), lambda: mod_rows(1, 0), lambda: mod_rows(1, 1)])
                    quad(0, 6, [lambda: rest_out(1)])
                with dve.Fori(3 + 4 * (1 - L), CQ, 1) as q:
                    quad(L, q)
                for b in range(GROUPS[L][0]):
                    quad(L, CQ + b, [lambda: None, lambda: combine(L, b, 0), lambda: combine(L, b, 1)])
                if L == 0:
                    quad(0, CQ + GROUPS[0][0], [lambda k=k: constant_rows(k) for k in (0, 1, 2)])
                    for b in range(GROUPS[0][0]):
                        quad(0, NQ - GROUPS[0][0] + b, [lambda: ln1_stats(1, b),
                                                        lambda: deviations(1, b - LEAD[1], False, True, False)])
                    dve.wait_ge(mod_in[1], 32)
                else:
                    quad(1, NQ - 1)
            for c in range(GT[1][1]):
                b, t = FIRST[1][1] + c // J, FIRST[1][1] * J + c
                dve.wait_ge(gat_end[c], 16)
                link(v.tensor_tensor(H[:, c, :], H[:, c, :], GBB[1][:, b, :], ALU.mult))
                last = v.tensor_tensor(X[:, t, :], X[:, t, :], H[:, c, :], ALU.add)
                if c % J == J - 1:
                    last.then_inc(comb_done[1], 1)


_INS = ['L0_attn_q', 'L0_attn_wq', 'L0_attn_wk', 'L0_attn_wv', 'L0_attn_wo', 'L0_ffn_uzman_embeddings', 'L0_ffn_W1',
        'L0_ffn_b1', 'L0_ffn_W2', 'L0_ffn_b2', 'L0_ffn_onbellek_durumu', 'L0_c', 'L0_wmod', 'L1_attn_W_qkv', 'L1_ffn_W1',
        'L1_ffn_b1', 'L1_ffn_W2', 'L1_ffn_b2', 'L1_ffn_Wr', 'L1_ffn_br', 'L1_c', 'L1_wmod']
_OUTS = [((8, 512, 128), 'float32')]


def kernel(**inputs):
    import numpy as _np
    import concourse.bacc as _bacc
    from concourse import mybir as _mybir
    from concourse.bass_utils import run_bass_kernel_spmd as _run

    nc = _bacc.Bacc("TRN2", target_bir_lowering=False, num_devices=1)
    arrays, args = {}, []
    for name in _INS:
        a = _np.ascontiguousarray(inputs[name])
        arrays[f"in_{name}_dram"] = a
        args.append(nc.dram_tensor(f"in_{name}_dram", a.shape, _mybir.dt.from_np(a.dtype), kind="ExternalInput").ap())
    for i, (shape, dtype) in enumerate(_OUTS):
        dt = _mybir.dt.from_np(_np.dtype(dtype))
        args.append(nc.dram_tensor(f"out_{i}_dram", shape, dt, kind="ExternalOutput").ap())
    adaln_kernel(nc, *args)
    r = _run(nc, [arrays], core_ids=[0])
    return r.results[0]["out_0_dram"]
```
